# Optimizing a Trainium2 kernel written in Bass

```python
import numpy as np
import jax
import jax.numpy as jnp

def _softmax(x, axis=-1):
    return jax.nn.softmax(x, axis=axis)

def _gelu(x):
    return jax.nn.gelu(x, approximate=True)

def _silu(x):
    return jax.nn.silu(x)

def _sigmoid(x):
    return jax.nn.sigmoid(x)

def _layernorm(x, axis=-1, eps=1e-05):
    m = jnp.mean(x, axis=axis, keepdims=True)
    v = jnp.var(x, axis=axis, keepdims=True)
    return (x - m) / jnp.sqrt(v + eps)

def _scatter_add(tgt, idx, src, axis=0):
    return tgt.at[idx].add(src)

def _segment_sum(src, seg, n):
    return jax.ops.segment_sum(src, seg, n)
kernel_name = 'mk_vit_tower_d2_tok_img768_r4_b35e6d'

def setup_inputs(seed: int=0):
    np.random.seed(seed)
    _w = jnp.asarray

    def _rec_inputs():
        import jax
        import jax.numpy as jnp
        _rk = jax.random.key(seed)
        x = -0.00016672 + 0.999947 * jax.random.normal(jax.random.fold_in(_rk, 1), (16, 96, 96, 3), jnp.float32)
        return x
    x = _rec_inputs()

    def _L0_tok_setup():
        import jax, jax.numpy as jnp
        import numpy as np
        PATCH = 16
        HIDDEN = 192

        def extract_patches(x, p):
            B, H, W, C = x.shape
            Hp, Wp = (H // p, W // p)
            x = x.reshape(B, Hp, p, Wp, p, C)
            x = x.transpose(0, 1, 3, 2, 4, 5)
            return x.reshape(B, Hp * Wp, p * p * C)
        key = jax.random.key(seed)
        k1, k2, k3, k4, k5 = jax.random.split(key, 5)
        B, H, W, C = (64, 96, 96, 3)
        num_patches = (H // PATCH) ** 2
        patch_dim = PATCH * PATCH * C
        contactMap = jax.random.normal(k1, (B, H, W, C), dtype=jnp.float32)
        W_proj = jax.random.normal(k2, (patch_dim, HIDDEN), dtype=jnp.float32) * (1.0 / np.sqrt(patch_dim))
        b_proj = jnp.zeros((HIDDEN,), dtype=jnp.float32)
        cls_token = jax.random.normal(k3, (1, 1, HIDDEN), dtype=jnp.float32) * 0.05
        pos_embedding = jax.random.normal(k4, (num_patches + 1, HIDDEN), dtype=jnp.float32) * 0.05
        return {'contactMap': contactMap, 'W_proj': W_proj, 'b_proj': b_proj, 'cls_token': cls_token, 'pos_embedding': pos_embedding}
    _L0_tok_all = _L0_tok_setup()
    _L0_tok_in = {k: v for k, v in _L0_tok_all.items() if k in ('W_proj', 'b_proj', 'cls_token', 'pos_embedding')}
    del _L0_tok_all

    def _L0_attn_setup():
        import jax, jax.numpy as jnp
        import numpy as np
        B, S, D, H, E = (8, 196, 192, 12, 8)
        HD = D // H
        FF = 4 * D
        EPS = 1e-05

        def _layernorm(x, g, b):
            mu = jnp.mean(x, axis=-1, keepdims=True)
            var = jnp.var(x, axis=-1, keepdims=True)
            return (x - mu) * jax.lax.rsqrt(var + EPS) * g + b

        def _rotate_half(x):
            x1, x2 = jnp.split(x, 2, axis=-1)
            return jnp.concatenate((-x2, x1), axis=-1)

        def _rope(seq_len):
            inv_freq = 1.0 / 10000.0 ** (jnp.arange(0, HD, 2, dtype=jnp.float32) / HD)
            freqs = jnp.arange(seq_len, dtype=jnp.float32)[:, None] * inv_freq[None, :]
            emb = jnp.concatenate((freqs, freqs), axis=-1)
            return emb[None, :, None, :]

        def _attention(x, Wq, bq, Wk, bk, Wv, bv):
            b, s, _ = x.shape
            q = (x @ Wq + bq).reshape(b, s, H, HD)
            k = (x @ Wk + bk).reshape(b, s, 1, HD)
            v = (x @ Wv + bv).reshape(b, s, 1, HD)
            k = jnp.broadcast_to(k, (b, s, H, HD))
            v = jnp.broadcast_to(v, (b, s, H, HD))
            pe = _rope(s)
            cos, sin = (jnp.cos(pe), jnp.sin(pe))
            q = q * cos + _rotate_half(q) * sin
            k = k * cos + _rotate_half(k) * sin
            scale = HD ** (-0.5)
            attn = jnp.einsum('bshd,bsgd->bshg', q, k) * scale
            attn = jax.nn.softmax(attn, axis=-1)
            out = jnp.einsum('bshg,bsgd->bshd', attn, v)
            return out.reshape(b, s, H * HD)

        def _moe(x, Wg, bg, W1, b1, W2, b2):
            b, s, d = x.shape
            xt = x.reshape(-1, d)
            gates = jax.nn.softmax(xt @ Wg + bg, axis=-1)
            top1 = jnp.argmax(gates, axis=-1)
            out = jnp.zeros_like(xt)
            for e in range(E):
                h = jax.nn.gelu(xt @ W1[e] + b1[e], approximate=False)
                y = h @ W2[e] + b2[e]
                out = jnp.where((top1 == e)[:, None], y, out)
            return out.reshape(b, s, d)
        key = jax.random.key(seed)
        ks = jax.random.split(key, 12)
        s = 0.02
        inp = {'x': jax.random.normal(ks[0], (B, S, D), jnp.float32), 'ln1_g': jnp.ones((D,), jnp.float32), 'ln1_b': jnp.zeros((D,), jnp.float32), 'Wq': jax.random.normal(ks[1], (D, D), jnp.float32) * s, 'bq': jnp.zeros((D,), jnp.float32), 'Wk': jax.random.normal(ks[2], (D, HD), jnp.float32) * s, 'bk': jnp.zeros((HD,), jnp.float32), 'Wv': jax.random.normal(ks[3], (D, HD), jnp.float32) * s, 'bv': jnp.zeros((HD,), jnp.float32), 'ln2_g': jnp.ones((D,), jnp.float32), 'ln2_b': jnp.zeros((D,), jnp.float32), 'Wg': jax.random.normal(ks[4], (D, E), jnp.float32) * s, 'bg': jnp.zeros((E,), jnp.float32), 'W1': jax.random.normal(ks[5], (E, D, FF), jnp.float32) * s, 'b1': jnp.zeros((E, FF), jnp.float32), 'W2': jax.random.normal(ks[6], (E, FF, D), jnp.float32) * s, 'b2': jnp.zeros((E, D), jnp.float32)}
        return inp
    _L0_attn_all = _L0_attn_setup()
    _L0_attn_in = {k: v for k, v in _L0_attn_all.items() if k in ('ln1_g', 'ln1_b', 'Wq', 'bq', 'Wk', 'bk', 'Wv', 'bv', 'ln2_g', 'ln2_b', 'Wg', 'bg', 'W1', 'b1', 'W2', 'b2')}
    del _L0_attn_all

    def _L0_ffn_setup():
        import jax, jax.numpy as jnp
        import numpy as np
        B, S, H, D, E = (4, 512, 192, 256, 8)
        TOP_K = 2
        EPS = 1e-08
        LN_EPS = 1e-05

        def _gelu(t):
            return jax.nn.gelu(t, approximate=False)

        def _layer_norm(t, gamma, beta):
            mu = jnp.mean(t, axis=-1, keepdims=True)
            var = jnp.mean(jnp.square(t - mu), axis=-1, keepdims=True)
            return (t - mu) * jax.lax.rsqrt(var + LN_EPS) * gamma + beta
        key = jax.random.key(seed)
        ks = jax.random.split(key, 8)
        x = jax.random.normal(ks[0], (B, S, H), dtype=jnp.float32)
        w1 = jax.random.normal(ks[1], (H, H // 2), dtype=jnp.float32) * 0.02
        b1 = jnp.zeros((H // 2,), dtype=jnp.float32)
        w2 = jax.random.normal(ks[2], (H // 2, E), dtype=jnp.float32) * 0.02
        b2 = jnp.zeros((E,), dtype=jnp.float32)
        a_dn = float(np.sqrt(6.0 / (H + D)))
        a_up = float(np.sqrt(6.0 / (D + H)))
        down_w = jax.random.uniform(ks[3], (E, H, D), dtype=jnp.float32, minval=-a_dn, maxval=a_dn)
        down_b = jnp.zeros((E, D), dtype=jnp.float32)
        up_w = jax.random.uniform(ks[4], (E, D, H), dtype=jnp.float32, minval=-a_up, maxval=a_up)
        gamma = jnp.ones((H,), dtype=jnp.float32)
        beta = jnp.zeros((H,), dtype=jnp.float32)
        return {'x': x, 'w1': w1, 'b1': b1, 'w2': w2, 'b2': b2, 'down_w': down_w, 'down_b': down_b, 'up_w': up_w, 'gamma': gamma, 'beta': beta}
    _L0_ffn_all = _L0_ffn_setup()
    _L0_ffn_in = {k: v for k, v in _L0_ffn_all.items() if k in ('w1', 'b1', 'w2', 'b2', 'down_w', 'down_b', 'up_w', 'gamma', 'beta')}
    del _L0_ffn_all

    def _L1_attn_setup():
        import jax, jax.numpy as jnp
        import numpy as np
        B, N, C, H = (4, 512, 192, 12)
        D = C // H
        SCALE = D ** (-0.5)
        key = jax.random.key(seed)
        k1, k2, k3 = jax.random.split(key, 3)
        x = jax.random.normal(k1, (B, N, C), dtype=jnp.float32)
        w_qkv = jax.random.normal(k2, (C, 3 * C), dtype=jnp.float32) * 0.02
        w_proj = jax.random.normal(k3, (C, C), dtype=jnp.float32) * 0.02
        b_proj = jnp.zeros((C,), dtype=jnp.float32)
        temperature = jnp.ones((H, 1, 1), dtype=jnp.float32) * 0.5
        return {'x': x, 'w_qkv': w_qkv, 'w_proj': w_proj, 'b_proj': b_proj, 'temperature': temperature}
    _L1_attn_all = _L1_attn_setup()
    _L1_attn_in = {k: v for k, v in _L1_attn_all.items() if k in ('w_qkv', 'w_proj', 'b_proj', 'temperature')}
    del _L1_attn_all

    def _L1_ffn_setup():
        import jax, jax.numpy as jnp
        import numpy as np
        EPS_NORM = 1e-05
        RMS_EPS = 1e-05

        def _l2_normalize(v):
            n = jnp.sqrt(jnp.sum(v * v, axis=-1, keepdims=True))
            return v / jnp.maximum(n, EPS_NORM)

        def _rms_norm(x, weight, eps):
            ms = jnp.mean(x * x, axis=-1, keepdims=True)
            return x * jax.lax.rsqrt(ms + eps) * weight
        key = jax.random.key(seed)
        ks = jax.random.split(key, 6)
        B, T, D = (8, 1024, 192)
        S, F = (64, 768)
        x = jax.random.normal(ks[0], (B, T, D), dtype=jnp.float32)
        slots = 0.02 * jax.random.normal(ks[1], (S, D), dtype=jnp.float32)
        scale = jnp.ones((S,), dtype=jnp.float32)
        fc1_weight = 0.02 * jax.random.normal(ks[2], (S, D, F), dtype=jnp.float32)
        fc1_bias = jnp.zeros((S, F), dtype=jnp.float32)
        fc2_weight = 0.02 * jax.random.normal(ks[3], (S, F, D), dtype=jnp.float32)
        fc2_bias = jnp.zeros((S, D), dtype=jnp.float32)
        norm_weight = jnp.ones((D,), dtype=jnp.float32)
        return {'x': x, 'slots': slots, 'scale': scale, 'fc1_weight': fc1_weight, 'fc1_bias': fc1_bias, 'fc2_weight': fc2_weight, 'fc2_bias': fc2_bias, 'norm_weight': norm_weight}
    _L1_ffn_all = _L1_ffn_setup()
    _L1_ffn_in = {k: v for k, v in _L1_ffn_all.items() if k in ('slots', 'scale', 'fc1_weight', 'fc1_bias', 'fc2_weight', 'fc2_bias', 'norm_weight')}
    del _L1_ffn_all
    return {'x': x, 'L0_tok_W_proj': _L0_tok_in['W_proj'], 'L0_tok_b_proj': _L0_tok_in['b_proj'], 'L0_tok_cls_token': _L0_tok_in['cls_token'], 'L0_tok_pos_embedding': _L0_tok_in['pos_embedding'], 'L0_attn_ln1_g': _L0_attn_in['ln1_g'], 'L0_attn_ln1_b': _L0_attn_in['ln1_b'], 'L0_attn_Wq': _L0_attn_in['Wq'], 'L0_attn_bq': _L0_attn_in['bq'], 'L0_attn_Wk': _L0_attn_in['Wk'], 'L0_attn_bk': _L0_attn_in['bk'], 'L0_attn_Wv': _L0_attn_in['Wv'], 'L0_attn_bv': _L0_attn_in['bv'], 'L0_attn_ln2_g': _L0_attn_in['ln2_g'], 'L0_attn_ln2_b': _L0_attn_in['ln2_b'], 'L0_attn_Wg': _L0_attn_in['Wg'], 'L0_attn_bg': _L0_attn_in['bg'], 'L0_attn_W1': _L0_attn_in['W1'], 'L0_attn_b1': _L0_attn_in['b1'], 'L0_attn_W2': _L0_attn_in['W2'], 'L0_attn_b2': _L0_attn_in['b2'], 'L0_ffn_w1': _L0_ffn_in['w1'], 'L0_ffn_b1': _L0_ffn_in['b1'], 'L0_ffn_w2': _L0_ffn_in['w2'], 'L0_ffn_b2': _L0_ffn_in['b2'], 'L0_ffn_down_w': _L0_ffn_in['down_w'], 'L0_ffn_down_b': _L0_ffn_in['down_b'], 'L0_ffn_up_w': _L0_ffn_in['up_w'], 'L0_ffn_gamma': _L0_ffn_in['gamma'], 'L0_ffn_beta': _L0_ffn_in['beta'], 'L1_attn_w_qkv': _L1_attn_in['w_qkv'], 'L1_attn_w_proj': _L1_attn_in['w_proj'], 'L1_attn_b_proj': _L1_attn_in['b_proj'], 'L1_attn_temperature': _L1_attn_in['temperature'], 'L1_ffn_slots': _L1_ffn_in['slots'], 'L1_ffn_scale': _L1_ffn_in['scale'], 'L1_ffn_fc1_weight': _L1_ffn_in['fc1_weight'], 'L1_ffn_fc1_bias': _L1_ffn_in['fc1_bias'], 'L1_ffn_fc2_weight': _L1_ffn_in['fc2_weight'], 'L1_ffn_fc2_bias': _L1_ffn_in['fc2_bias'], 'L1_ffn_norm_weight': _L1_ffn_in['norm_weight']}

def reference(x, L0_tok_W_proj, L0_tok_b_proj, L0_tok_cls_token, L0_tok_pos_embedding, L0_attn_ln1_g, L0_attn_ln1_b, L0_attn_Wq, L0_attn_bq, L0_attn_Wk, L0_attn_bk, L0_attn_Wv, L0_attn_bv, L0_attn_ln2_g, L0_attn_ln2_b, L0_attn_Wg, L0_attn_bg, L0_attn_W1, L0_attn_b1, L0_attn_W2, L0_attn_b2, L0_ffn_w1, L0_ffn_b1, L0_ffn_w2, L0_ffn_b2, L0_ffn_down_w, L0_ffn_down_b, L0_ffn_up_w, L0_ffn_gamma, L0_ffn_beta, L1_attn_w_qkv, L1_attn_w_proj, L1_attn_b_proj, L1_attn_temperature, L1_ffn_slots, L1_ffn_scale, L1_ffn_fc1_weight, L1_ffn_fc1_bias, L1_ffn_fc2_weight, L1_ffn_fc2_bias, L1_ffn_norm_weight):
    import jax
    import jax.numpy as jnp

    def _L0_tok_ref(contactMap, W_proj, b_proj, cls_token, pos_embedding):
        import jax, jax.numpy as jnp
        import numpy as np
        PATCH = 16
        HIDDEN = 192

        def extract_patches(x, p):
            B, H, W, C = x.shape
            Hp, Wp = (H // p, W // p)
            x = x.reshape(B, Hp, p, Wp, p, C)
            x = x.transpose(0, 1, 3, 2, 4, 5)
            return x.reshape(B, Hp * Wp, p * p * C)
        B = contactMap.shape[0]
        patches = extract_patches(contactMap, PATCH)
        enc = jnp.einsum('bnd,dh->bnh', patches, W_proj) + b_proj
        cls = jnp.broadcast_to(cls_token.astype(contactMap.dtype), (B, 1, enc.shape[-1]))
        enc = jnp.concatenate([cls, enc], axis=1)
        return enc + pos_embedding

    def _L0_attn_ref(x, ln1_g, ln1_b, Wq, bq, Wk, bk, Wv, bv, ln2_g, ln2_b, Wg, bg, W1, b1, W2, b2):
        import jax, jax.numpy as jnp
        import numpy as np
        B, S, D, H, E = (8, 196, 192, 12, 8)
        HD = D // H
        FF = 4 * D
        EPS = 1e-05

        def _layernorm(x, g, b):
            mu = jnp.mean(x, axis=-1, keepdims=True)
            var = jnp.var(x, axis=-1, keepdims=True)
            return (x - mu) * jax.lax.rsqrt(var + EPS) * g + b

        def _rotate_half(x):
            x1, x2 = jnp.split(x, 2, axis=-1)
            return jnp.concatenate((-x2, x1), axis=-1)

        def _rope(seq_len):
            inv_freq = 1.0 / 10000.0 ** (jnp.arange(0, HD, 2, dtype=jnp.float32) / HD)
            freqs = jnp.arange(seq_len, dtype=jnp.float32)[:, None] * inv_freq[None, :]
            emb = jnp.concatenate((freqs, freqs), axis=-1)
            return emb[None, :, None, :]

        def _attention(x, Wq, bq, Wk, bk, Wv, bv):
            b, s, _ = x.shape
            q = (x @ Wq + bq).reshape(b, s, H, HD)
            k = (x @ Wk + bk).reshape(b, s, 1, HD)
            v = (x @ Wv + bv).reshape(b, s, 1, HD)
            k = jnp.broadcast_to(k, (b, s, H, HD))
            v = jnp.broadcast_to(v, (b, s, H, HD))
            pe = _rope(s)
            cos, sin = (jnp.cos(pe), jnp.sin(pe))
            q = q * cos + _rotate_half(q) * sin
            k = k * cos + _rotate_half(k) * sin
            scale = HD ** (-0.5)
            attn = jnp.einsum('bshd,bsgd->bshg', q, k) * scale
            attn = jax.nn.softmax(attn, axis=-1)
            out = jnp.einsum('bshg,bsgd->bshd', attn, v)
            return out.reshape(b, s, H * HD)

        def _moe(x, Wg, bg, W1, b1, W2, b2):
            b, s, d = x.shape
            xt = x.reshape(-1, d)
            gates = jax.nn.softmax(xt @ Wg + bg, axis=-1)
            top1 = jnp.argmax(gates, axis=-1)
            out = jnp.zeros_like(xt)
            for e in range(E):
                h = jax.nn.gelu(xt @ W1[e] + b1[e], approximate=False)
                y = h @ W2[e] + b2[e]
                out = jnp.where((top1 == e)[:, None], y, out)
            return out.reshape(b, s, d)
        res = x
        h = _layernorm(x, ln1_g, ln1_b)
        h = _attention(h, Wq, bq, Wk, bk, Wv, bv)
        x = res + h
        res = x
        h = _layernorm(x, ln2_g, ln2_b)
        h = _moe(h, Wg, bg, W1, b1, W2, b2)
        return res + h

    def _L0_ffn_ref(x, w1, b1, w2, b2, down_w, down_b, up_w, gamma, beta):
        import jax, jax.numpy as jnp
        import numpy as np
        B, S, H, D, E = (4, 512, 192, 256, 8)
        TOP_K = 2
        EPS = 1e-08
        LN_EPS = 1e-05

        def _gelu(t):
            return jax.nn.gelu(t, approximate=False)

        def _layer_norm(t, gamma, beta):
            mu = jnp.mean(t, axis=-1, keepdims=True)
            var = jnp.mean(jnp.square(t - mu), axis=-1, keepdims=True)
            return (t - mu) * jax.lax.rsqrt(var + LN_EPS) * gamma + beta
        logits = _gelu(x @ w1 + b1) @ w2 + b2
        routing = jax.nn.softmax(logits, axis=-1)
        topv, topi = jax.lax.top_k(routing, TOP_K)
        sparse = jnp.sum(jax.nn.one_hot(topi, E, dtype=routing.dtype) * topv[..., None], axis=-2)
        sparse = sparse / (jnp.sum(sparse, axis=-1, keepdims=True) + EPS)
        z = _gelu(jnp.einsum('bsh,ehd->bsed', x, down_w) + down_b)
        expert_out = jnp.einsum('bsed,edh->bseh', z, up_w)
        moe_out = jnp.einsum('bseh,bse->bsh', expert_out, sparse)
        return _layer_norm(x + moe_out, gamma, beta)

    def _L1_attn_ref(x, w_qkv, w_proj, b_proj, temperature):
        import jax, jax.numpy as jnp
        import numpy as np
        B, N, C, H = (4, 512, 192, 12)
        D = C // H
        SCALE = D ** (-0.5)
        b, n, c = x.shape
        h, d = (H, c // H)
        qkv = (x @ w_qkv).reshape(b, n, 3, h, d)
        q, k, v = jnp.moveaxis(qkv, 2, 0)
        q = q.transpose(0, 2, 1, 3)
        k = k.transpose(0, 2, 1, 3)
        v = v.transpose(0, 2, 1, 3)
        attn = jnp.einsum('bhnd,bhmd->bhnm', q, k) * SCALE
        eye = jnp.eye(n, dtype=attn.dtype)
        attn = attn * (1.0 - temperature[None] * eye)
        attn = jax.nn.softmax(attn, axis=-1)
        out = jnp.einsum('bhnm,bhmd->bhnd', attn, v)
        out = out.transpose(0, 2, 1, 3).reshape(b, n, c)
        return out @ w_proj + b_proj

    def _L1_ffn_ref(x, slots, scale, fc1_weight, fc1_bias, fc2_weight, fc2_bias, norm_weight):
        import jax, jax.numpy as jnp
        import numpy as np
        EPS_NORM = 1e-05
        RMS_EPS = 1e-05

        def _l2_normalize(v):
            n = jnp.sqrt(jnp.sum(v * v, axis=-1, keepdims=True))
            return v / jnp.maximum(n, EPS_NORM)

        def _rms_norm(x, weight, eps):
            ms = jnp.mean(x * x, axis=-1, keepdims=True)
            return x * jax.lax.rsqrt(ms + eps) * weight
        xn = _rms_norm(x, norm_weight, RMS_EPS)
        tok = _l2_normalize(xn)
        sl = _l2_normalize(slots) * scale[:, None]
        logits = jnp.einsum('sd,btd->bst', sl, tok)
        dispatch_w = jax.nn.softmax(logits, axis=-1)
        combine_w = jax.nn.softmax(logits, axis=-2)
        y = jnp.einsum('btd,bst->bsd', xn, dispatch_w)
        y = jnp.einsum('sio,bsi->bso', fc1_weight, y) + fc1_bias
        y = jax.nn.gelu(y, approximate=False)
        y = jnp.einsum('sio,bsi->bso', fc2_weight, y) + fc2_bias
        out = jnp.einsum('bsd,bst->btd', y, combine_w)
        return out
    h = _L0_tok_ref(x, L0_tok_W_proj, L0_tok_b_proj, L0_tok_cls_token, L0_tok_pos_embedding)
    h = h + _L0_attn_ref(_layernorm(h, axis=-1), L0_attn_ln1_g, L0_attn_ln1_b, L0_attn_Wq, L0_attn_bq, L0_attn_Wk, L0_attn_bk, L0_attn_Wv, L0_attn_bv, L0_attn_ln2_g, L0_attn_ln2_b, L0_attn_Wg, L0_attn_bg, L0_attn_W1, L0_attn_b1, L0_attn_W2, L0_attn_b2)
    h = h + _L0_ffn_ref(_layernorm(h, axis=-1), L0_ffn_w1, L0_ffn_b1, L0_ffn_w2, L0_ffn_b2, L0_ffn_down_w, L0_ffn_down_b, L0_ffn_up_w, L0_ffn_gamma, L0_ffn_beta)
    h = h + _L1_attn_ref(_layernorm(h, axis=-1), L1_attn_w_qkv, L1_attn_w_proj, L1_attn_b_proj, L1_attn_temperature)
    h = h + _L1_ffn_ref(_layernorm(h, axis=-1), L1_ffn_slots, L1_ffn_scale, L1_ffn_fc1_weight, L1_ffn_fc1_bias, L1_ffn_fc2_weight, L1_ffn_fc2_bias, L1_ffn_norm_weight)
    return h

_drawn_inputs = setup_inputs


def setup_inputs(seed=0):
    import zlib

    import numpy as np

    out = dict(_drawn_inputs(seed))
    spreads = {'L0_tok_b_proj': (0.0, 0.1),
     'L0_attn_ln1_g': (1.0, 0.2),
     'L0_attn_ln1_b': (0.0, 0.363),
     'L0_attn_bq': (0.0, 0.1),
     'L0_attn_bk': (0.0, 0.1),
     'L0_attn_bv': (0.0, 0.1),
     'L0_attn_ln2_g': (1.0, 0.2),
     'L0_attn_ln2_b': (0.0, 0.329),
     'L0_attn_bg': (0.0, 0.1),
     'L0_attn_b1': (0.0, 0.45),
     'L0_attn_b2': (0.0, 0.1),
     'L0_ffn_b1': (0.0, 0.1),
     'L0_ffn_b2': (0.0, 0.1),
     'L0_ffn_down_b': (0.0, 0.521),
     'L0_ffn_gamma': (1.0, 0.2),
     'L0_ffn_beta': (0.0, 0.1),
     'L1_attn_b_proj': (0.0, 0.362),
     'L1_attn_temperature': (0.5, 0.6),
     'L1_ffn_scale': (1.0, 0.6),
     'L1_ffn_fc1_bias': (0.0, 0.8),
     'L1_ffn_fc2_bias': (0.0, 2.0),
     'L1_ffn_norm_weight': (1.0, 0.6)}
    factors = {'L1_attn_w_qkv': 8.0,
     'L1_attn_w_proj': 8.0,
     'L1_ffn_slots': 27.388,
     'L1_ffn_fc1_weight': 8.0,
     'L1_ffn_fc2_weight': 8.0}
    for name, (base, spread) in spreads.items():
        noise = np.random.default_rng([zlib.crc32(name.encode()), seed]).standard_normal(out[name].shape)
        drawn = base * np.exp(spread * noise) if base else spread * noise
        out[name] = jnp.asarray(drawn.astype(out[name].dtype))
    for name, factor in factors.items():
        out[name] = (out[name] * factor).astype(out[name].dtype)
    return out
```

```python
from contextlib import ExitStack

import numpy as np

import concourse.bass as bass
from concourse import mybir

F32 = mybir.dt.float32
ALU = mybir.AluOpType
ACT = mybir.ActivationFunctionType
X = mybir.AxisListType.X

B, IMG, PATCH, CH = 16, 96, 16, 3
D = 192
KH = D // 2
S = (IMG // PATCH) ** 2 + 1
NTOK = B * S
IPT = 3
TR = IPT * S
TT = -(-B // IPT)
NPAD = TR * TT
LAST = NTOK - (TT - 1) * TR
NH = NTOK // 2
HEADS, HD = 12, 16
HH = HEADS // 2
HW = HH * S
NE = 8
FF = 768
FT = FF // 128
DZ = 256
ZT = DZ // 128
SLOTS = 64
GS = 8
NG = SLOTS // GS
QP = GS // 2
WP = IMG // PATCH
ROW = PATCH * CH
PDIM = PATCH * ROW
KT = PDIM // KH
LN_EPS = 1e-5

CONSTS = {}
_at = 0
for _name, _n in (("ident", 128), ("sel", 128), ("kmask", HH), ("vmask", IPT), ("eye", S), ("cos", HD),
                  ("sin", HD), ("bmask", TT * B), ("rev", NE), ("pmask", 2), ("mhalf", 8)):
    CONSTS[_name] = (_at, _at + _n)
    _at += _n
NCONST = _at


def constant_table():
    c = np.zeros((128, NCONST), np.float32)

    def put(name, a):
        lo, hi = CONSTS[name]
        c[: a.shape[0], lo:hi] = a

    row = np.arange(128)
    put("ident", np.eye(128, dtype=np.float32))
    put("sel", (row[:GS, None] == row[None, :] // B).astype(np.float32))
    put("kmask", (row[:KH, None] // HD == np.arange(HH)[None, :]).astype(np.float32))
    put("vmask", (row[:TR, None] // S == np.arange(IPT)[None, :]).astype(np.float32))
    put("eye", (row[:, None] % 64 == np.arange(S)[None, :]).astype(np.float32))
    inv = (np.float32(1.0) / np.float32(10000.0) ** (np.arange(0, HD, 2, dtype=np.float32) / HD)).astype(np.float32)
    ang = ((row[:TR] % S).astype(np.float32)[:, None] * inv[None, :]).astype(np.float32)
    cos, sin = np.cos(ang), np.sin(ang)
    put("cos", np.concatenate([cos, cos], 1))
    put("sin", np.concatenate([-sin, sin], 1))
    image = IPT * np.arange(TT)[None, :] + row[:TR, None] // S
    put("bmask", (image[:, :, None] == np.arange(B)).astype(np.float32).reshape(TR, TT * B))
    put("rev", np.broadcast_to(np.arange(NE, 0, -1, dtype=np.float32), (128, NE)))
    put("pmask", (row[:, None] // 64 == np.arange(2)[None, :]).astype(np.float32))
    put("mhalf", np.full((128, 8), -0.5, np.float32))
    return c


def bcast(ap, axis, n):
    ap = ap.unsqueeze(axis)
    shape = list(ap.shape)
    shape[axis] = n
    return ap.broadcast_to(shape)


def vit_tower(nc, w, consts, out):
    with ExitStack() as ctx:
        def sb(name, shape):
            return ctx.enter_context(nc.sbuf_tensor(name, shape, F32))

        sems = {}

        def sem(name):
            if name not in sems:
                sems[name] = ctx.enter_context(nc.semaphore(name))
            return sems[name]

        ps = ctx.enter_context(nc.psum_tensor("ps", [128, 8, 512], F32))

        fc1 = sb("fc1", [128, 2, QP * 3 * FF])
        fc2 = sb("fc2", [128, 2, GS * FT * D])
        fc1v = fc1[:, :, :].rearrange("p u (q c f) -> p u q c f", q=QP, c=3)
        fc2v = fc2[:, :, :].rearrange("p u (s m d) -> p u s m d", s=GS, m=FT)
        wa, wb = fc1[:, 1, :], fc2[:, 1, :]

        at = [0, 0]

        def carve(which, parts, n):
            lo = at[which]
            at[which] = lo + n
            assert at[which] <= QP * 3 * FF
            return (wa, wb)[which][0:parts, lo:lo + n]

        w1r = carve(0, KH, 2 * 2 * FF).rearrange("p (u k f) -> p u k f", u=2, k=2)
        w2r = carve(0, 128, 2 * FT * D).rearrange("p (u m d) -> p u m d", u=2, m=FT)
        wproj = carve(0, KH, KT * D).rearrange("p (k d) -> p k d", k=KT)
        downr = carve(0, KH, 2 * 2 * DZ).rearrange("p (u k f) -> p u k f", u=2, k=2)
        upr = carve(0, 128, 2 * ZT * D).rearrange("p (u j d) -> p u j d", u=2, j=ZT)
        xin = carve(1, B * WP, PATCH * IMG * CH).rearrange("p (r v c) -> p r v c", r=PATCH, v=WP)
        patT = carve(1, KH, KT * B * 36).rearrange("p (k n) -> p k n", k=KT)
        at[1] = 0
        vrep = carve(1, TR, B * D).rearrange("p (b d) -> p b d", b=B)
        kblk = carve(1, KH, 2 * 2 * 2 * HW).rearrange("p (u c i n) -> p u c i n", u=2, c=2, i=2)
        vblk = carve(1, TR, 2 * 2 * 4 * 48).rearrange("p (u i g n) -> p u i g n", u=2, i=2, g=4)
        qT = carve(1, KH, 2 * NPAD).rearrange("p (c n) -> p c n", c=2)
        kT = carve(1, KH, 2 * NPAD).rearrange("p (c n) -> p c n", c=2)
        at[1] = 0
        hT = carve(1, 128, FT * NPAD).rearrange("p (m n) -> p m n", m=FT)
        ohT = carve(1, 128, NPAD)
        zT = hT[:, 0:ZT, :]
        rT = hT[0:KH, ZT, :]

        cst = sb("cst", [128, NCONST])

        def const(name, parts=128):
            lo, hi = CONSTS[name]
            return cst[0:parts, lo:hi]

        ident = const("ident")
        h = sb("h", [TR, TT, D])
        a = sb("a", [TR, TT, D])
        t = sb("t", [TR, TT, D])
        xT = sb("xT", [KH, 2, NPAD])
        slT = sb("slT", [KH, 2, SLOTS])
        slots = sb("slots", [SLOTS, D])
        slsc = sb("slsc", [SLOTS, 1])
        lnv = sb("lnv", [KH, 4, 2])
        nw = sb("nw", [TR, D])
        st = sb("st", [TR, TT, 6])
        mv = sb("mv", [TR, TT, 2])
        rs = sb("rs", [TR, 8])
        ve = sb("ve", [TR, 8])
        m6 = sb("m6", [TR, 4, TT])
        sst = sb("sst", [SLOTS, 12])
        fb1 = sb("fb1", [128, 2, FF])
        fb2 = sb("fb2", [128, 2, D])

        shared = sb("shared", [128, 8540])
        used = [0]

        def share(parts, *dims):
            n = int(np.prod(dims))
            lo = used[0]
            used[0] += n
            assert used[0] <= 8540, used[0]
            v = shared[0:parts, lo:lo + n]
            names = "abcd"[:len(dims)]
            if len(dims) > 1:
                v = v.rearrange(f"p ({' '.join(names)}) -> p {' '.join(names)}", **dict(zip(names, dims)))
            return v

        posr = share(TR, D)
        addr = share(TR, D)
        wqkv0 = share(KH, 2, D + 2 * HD)
        bqkv0 = share(TR, D + 2 * HD)
        qkv = share(TR, TT, D + 2 * HD)
        krot = share(TR, TT, HD)
        ktmp = share(TR, TT, HD)
        s0 = share(TR, 2, TT, HEADS)
        wg0 = share(KH, 2, NE)
        bg0 = share(TR, NE)
        b1r = share(128, 2, FT)
        b2pad = share(128, D)
        w1s = share(KH, 2, KH)
        b1s = share(KH, 1)
        w2s = share(KH, NE)
        b2s = share(TR, NE)
        downb = share(128, 2, ZT)
        gamma = share(TR, D)
        beta = share(TR, D)
        wqkv1 = share(KH, 2, 3 * D)
        wpr1 = share(KH, 2, D)
        bpr1 = share(TR, D)
        temp = share(128, HEADS)
        dmask = share(128, HEADS, S)
        rtmp = share(TR, TT, D)
        used[0] -= TT * D
        sc = share(128, 2, HEADS * S)
        pT = share(TR, 2, 512)
        ob = share(128, 2, D)
        mx = share(128, 2, HEADS)
        den = share(128, 2, HEADS)
        lg = share(TR, TT, NE)
        key = share(TR, TT, NE)
        oh = share(TR, TT, NE)
        gate = share(TR, TT, NE)
        gcol = share(TR, 2, TT)
        used[0] = 0
        ycmp = share(128, 3, SLOTS // 2, B)
        dmt = share(TR, TT, IPT, SLOTS)
        comb = share(TR, TT, SLOTS)
        yg = share(128, 2, 3, QP, 32)
        hid = share(128, FF)
        hidT = share(128, FT, 2, 128)
        yslot = share(128, D)
        xe = share(TR, TT, GS, B)
        cmT = share(128, NPAD)
        mxd = share(SLOTS, 2, B)
        mxc = share(TR, 2, TT)
        disp = cmT[0:SLOTS, :]

        def load(eng, dst, src, name):
            eng.dma_start(dst, src).then_inc(sem(name), 16)

        def rowb(v, n):
            return v.unsqueeze(0).broadcast_to([n, v.shape[0]])

        w1d = w["L0_attn_W1"].rearrange("e (k p) f -> e p k f", k=2)
        w2d = w["L0_attn_W2"].rearrange("e (p m) d -> e p m d", m=FT)
        b1d = w["L0_attn_b1"].rearrange("e (p m) -> e p m", m=FT)
        downd = w["L0_ffn_down_w"].rearrange("e (k p) f -> e p k f", k=2)
        upd = w["L0_ffn_up_w"].rearrange("e (p j) d -> e p j d", j=ZT)
        downbd = w["L0_ffn_down_b"].rearrange("e (p j) -> e p j", j=ZT)
        fc1d = w["L1_ffn_fc1_weight"].rearrange("(g q two) (p c) f -> g q (two p) (c f)", q=QP, two=2, c=3)
        fc2d = w["L1_ffn_fc2_weight"].rearrange("(g s) (p m) d -> g s p (m d)", s=GS, m=FT)
        fb1d = w["L1_ffn_fc1_bias"].rearrange("(g s) f -> g s f", s=GS)
        fb2d = w["L1_ffn_fc2_bias"].rearrange("(g s) f -> g s f", s=GS)

        N_TOK, N_ATT0, N_SMALL = 10, 6, 23

        def moe_load(sp, u, e):
            load(sp, w1r[:, u], w1d[e], f"ld_w1_{u}")
            load(sp, b1r[:, u], b1d[e], f"ld_w1_{u}")
            load(sp, w2r[:, u], w2d[e], f"ld_w2_{u}")

        def ffn_load(sp, u, e):
            load(sp, downr[:, u], downd[e], f"ld_down_{u}")
            load(sp, downb[:, u], downbd[e], f"ld_down_{u}")
            load(sp, upr[:, u], upd[e], f"ld_up_{u}")

        def fc1_load(sp, u, q, g):
            load(sp, fc1[:, u, q * 3 * FF:(q + 1) * 3 * FF], fc1d[g, q], f"ld_fc1_{u}_{q}")

        def fc2_load(sp, u, q, g):
            for s in (2 * q, 2 * q + 1):
                load(sp, fc2[:, u, s * FT * D:(s + 1) * FT * D], fc2d[g, s], f"ld_fc2_{u}_{q}")

        def bias_load(sp, u, g):
            load(sp, fb1[0:GS, u], fb1d[g], f"ld_fb_{u}")
            load(sp, fb2[0:GS, u], fb2d[g], f"ld_fb_{u}")

        def replicate_v(sp):
            sp.wait_ge(sem("v_ready"), TT)
            for r in range(IPT):
                n = TT if r == 0 else TT - 1
                for g in range(IPT):
                    sp.dma_start(vrep[S * g:S * g + S, r:r + IPT * (n - 1) + 1:IPT, :],
                                 a[S * r:S * r + S, 0:n, :]).then_inc(sem("vrep"), 16)

        def gather_heads(sp):
            for j in range(B // 2):
                sp.wait_ge(sem("o_ready"), j + 1)
                for i in range(2):
                    b = 2 * j + i
                    sp.dma_start(t[S * (b % IPT):S * (b % IPT) + S, b // IPT, :],
                                 ob[64 * i:64 * i + S, j % 2, :]).then_inc(sem(f"gather{j % 2}"), 16)

        def rows_of(k):
            buf = (a, t)[k // 2 % 2][0:KH].rearrange("p x y -> p (x y)")
            return buf[:, (k % 2) * 576:(k % 2) * 576 + 576].rearrange("p (v r c) -> p v r c", v=WP, r=2)

        def emb_out(m, n):
            return xT[:, m, 0:NTOK].rearrange("p (b s) -> p b s", s=S)[:, :, 1:S]\
                .rearrange("p b (y x) -> p b y x", y=WP)[:, :, :, 3 * n:3 * n + 3]

        def emb_in(m, n):
            return ps[0:KH, 4 + 2 * m + n, 0:288].rearrange("p (x b y) -> p b y x", x=3, b=B)

        def hid_out(k, par):
            return hidT[:, 3 * k:3 * k + 3, par, :].rearrange("p m (q two b) -> p m q two b", q=QP, two=2)[:, :, :, par, :]

        def hid_in(k, par):
            return ps[:, 3 + k, 0:384].rearrange("p (m q two b) -> p m q two b", m=3, q=QP, two=2)[:, :, :, par, :]

        NORM = {n: i for i, n in enumerate(("in0", "ln1", "ln2", "ffn", "u", "ln3", "tok0", "tok"))}
        ROOT = {n: i for i, n in enumerate(("slots", "in0", "ln1", "ln2", "ffn", "u", "ln3", "tok0", "ms_a", "ms_x"))}
        TURN = {n: i for i, n in enumerate(("ln1", "ln2", "ffn", "ln3", "proj", "tok"))}
        PAIRS = B // 2

        block = ctx.enter_context(nc.Block())

        @block.sync
        def _(sp):
            load(sp, cst[:, :], consts, "ld_cst")
            xd = w["x"].rearrange("b (v r) x c -> (b v) r (x c)", v=WP)
            for k in range(4):
                load(sp, xin[:, 4 * k:4 * k + 4].rearrange("p r v c -> p r (v c)"), xd[:, 4 * k:4 * k + 4], f"ld_x{k}")
                if k == 0:
                    load(sp, wproj[:], w["L0_tok_W_proj"].rearrange("(k p) d -> p k d", p=KH), "ld_wproj")
            for r in range(IPT):
                load(sp, posr[S * r:S * r + S], w["L0_tok_pos_embedding"], "ld_tok")
                load(sp, addr[S * r + 1:S * r + S], rowb(w["L0_tok_b_proj"], S - 1), "ld_tok")
                load(sp, addr[S * r:S * r + 1], w["L0_tok_cls_token"].rearrange("a b d -> (a b) d"), "ld_tok")
            for n, (lo, hi) in zip("qkv", ((0, D), (D, D + HD), (D + HD, D + 2 * HD))):
                load(sp, wqkv0[:, :, lo:hi], w[f"L0_attn_W{n}"].rearrange("(k p) n -> p k n", k=2), "ld_att0")
                load(sp, bqkv0[:, lo:hi], rowb(w[f"L0_attn_b{n}"], TR), "ld_att0")
            for i, n in enumerate(("ln1_g", "ln1_b", "ln2_g", "ln2_b")):
                for k in range(2):
                    load(sp, lnv[:, i, k:k + 1], w[f"L0_attn_{n}"][KH * k:KH * k + KH].unsqueeze(1), "ld_small")
            for dst, src in (
                (wg0[:], w["L0_attn_Wg"].rearrange("(k p) n -> p k n", k=2)),
                (bg0[:], rowb(w["L0_attn_bg"], TR)),
                (w1s[:], w["L0_ffn_w1"].rearrange("(k p) n -> p k n", k=2)),
                (b1s[:], w["L0_ffn_b1"].unsqueeze(1)),
                (w2s[:], w["L0_ffn_w2"]),
                (b2s[:], rowb(w["L0_ffn_b2"], TR)),
                (gamma[:], rowb(w["L0_ffn_gamma"], TR)),
                (beta[:], rowb(w["L0_ffn_beta"], TR)),
                (wqkv1[:], w["L1_attn_w_qkv"].rearrange("(k p) n -> p k n", k=2)),
                (wpr1[:], w["L1_attn_w_proj"].rearrange("(k p) n -> p k n", k=2)),
                (bpr1[:], rowb(w["L1_attn_b_proj"], TR)),
                (temp[:], rowb(w["L1_attn_temperature"].rearrange("h a b -> (h a b)"), 128)),
                (nw[:], rowb(w["L1_ffn_norm_weight"], TR)),
                (slots[:], w["L1_ffn_slots"]),
                (slsc[:], w["L1_ffn_scale"].unsqueeze(1)),
            ):
                load(sp, dst, src, "ld_small")
            sp.wait_ge(sem("pads_zero"), 1)
            load(sp, b2pad[0:NE], w["L0_attn_b2"], "ld_b2")
            for u in range(2):
                moe_load(sp, u, u)
            for u in range(2):
                ffn_load(sp, u, u)
            for u in range(2):
                bias_load(sp, u, u)
            for q in range(QP):
                fc1_load(sp, 0, q, 0)
            for q in range(QP):
                fc2_load(sp, 0, q, 0)

            with sp.Fori(0, NE // 2 - 1) as e2:
                for u in range(2):
                    e = e2 * 2 + u
                    sp.wait_ge(sem("moe_y_mm"), TT * e + TT)
                    moe_load(sp, u, e + 2)
            with sp.Fori(0, NE // 2 - 1) as e2:
                for u in range(2):
                    e = e2 * 2 + u
                    sp.wait_ge(sem("ffn_y_mm"), TT * e + TT)
                    ffn_load(sp, u, e + 2)

            sp.wait_ge(sem("ffn_y_mm"), TT * NE)
            for q in range(QP):
                fc1_load(sp, 1, q, 1)
            replicate_v(sp)
            gather_heads(sp)
            sp.wait_ge(sem("o_mm"), PAIRS)
            for q in range(QP):
                fc2_load(sp, 1, q, 1)

            with sp.Fori(0, NG // 2 - 1) as g2:
                for u in range(2):
                    g = g2 * 2 + u
                    sp.wait_ge(sem("fc1_used"), g + 2)
                    bias_wait = sem("fc2_used")
                    for q in range(QP):
                        fc1_load(sp, u, q, g + 2)
                    sp.wait_ge(bias_wait, g + 1)
                    bias_load(sp, u, g + 2)
                    for q in range(QP):
                        fc2_load(sp, u, q, g + 2)

            sp.wait_ge(sem("out_ready"), 1)
            full = (TT - 1) * TR
            rows = out.rearrange("b s d -> (b s) d")
            load(sp, rows[0:full].rearrange("(t p) d -> p t d", p=TR), h[:, 0:TT - 1, :], "stored")
            load(sp, rows[full:NTOK], h[0:LAST, TT - 1, :], "stored")
            sp.wait_ge(sem("stored"), 32)

        def embed(pe, mm, k):
            for v in range(2):
                pe.wait_ge(sem(f"patches_copied{v}"), k + 1)
            for m in range(2):
                for n in range(2):
                    ins = mm(ps[0:KH, 4 + 2 * m + n, 0:288], wproj[:, k, KH * m:KH * m + KH],
                             patT[:, k, 288 * n:288 * n + 288], k == 0, k == KT - 1)
                    if k == KT - 1:
                        ins.then_inc(sem("emb_mm"), 1)

        @block.tensor
        def _(pe):
            idn = ident

            def mm(o, l, r, start=True, stop=True, **k):
                return pe.matmul(o, l, r, start=start, stop=stop, **k)

            def to_features(name, src):
                for j in range(TT // 2):
                    for i in range(2):
                        tt = 2 * j + i
                        pe.wait_ge(sem("rows"), TT * NORM[name] + tt + 1)
                        for c in range(2):
                            ins = pe.transpose(ps[0:KH, j, 256 * c + TR * i:256 * c + TR * i + TR],
                                               src[:, tt, KH * c:KH * c + KH], idn[0:TR, 0:TR])
                    ins.then_inc(sem("tp"), 1)

            def attention():
                def scores(j):
                    pe.wait_ge(sem("kblk"), j + 1)
                    if j >= 2:
                        pe.wait_ge(sem("s_read"), j - 1)
                    for c in range(2):
                        for i in range(2):
                            b = 2 * j + i
                            ins = mm(ps[64 * i:64 * i + 64, j % 2, HW * c:HW * c + HW],
                                     qT[:, c, S * b:S * b + 64], kblk[:, j % 2, c, i, :])
                    ins.then_inc(sem("s_mm"), 1)

                scores(0)
                for j in range(B // 2):
                    if j + 1 < B // 2:
                        scores(j + 1)
                    pe.wait_ge(sem("exp"), j + 1)
                    if j >= 2:
                        pe.wait_ge(sem("pT"), j - 1)
                    for g in range(4):
                        ins = pe.transpose(ps[0:TR, 2 + j % 2, 128 * g:128 * g + 128],
                                           sc[:, j % 2, TR * g:TR * g + TR], idn)
                    ins.then_inc(sem("pT_mm"), 1)
                    pe.wait_ge(sem("pT"), j + 1)
                    pe.wait_ge(sem("vblk"), j + 1)
                    if j >= 2:
                        pe.wait_ge(sem("o_ready"), j - 1)
                    for g in range(4):
                        for i in range(2):
                            ins = mm(ps[64 * i:64 * i + 64, 4 + j % 2, 48 * g:48 * g + 48],
                                     pT[:, j % 2, 128 * g + 64 * i:128 * g + 64 * i + 64],
                                     vblk[:, j % 2, i, g, :])
                    ins.then_inc(sem("o_mm"), 1)

            pe.wait_ge(sem("ld_cst"), 16)
            pe.wait_ge(sem("ld_wproj"), 16)
            for k in range(KT):
                for v in range(2):
                    n = 2 * k + v
                    pe.wait_ge(sem(f"patches_rows{k % 2}"), k // 2 + 1)
                    if n >= 4:
                        pe.wait_ge(sem(f"patches_copied{v}"), k - 1)
                    for i in range(3):
                        wp = 3 * v + i
                        ins = pe.transpose(ps[0:KH, n % 4, KH * i:KH * i + KH],
                                           (a, t)[k // 2 % 2][0:KH].rearrange("p x y -> p (x y)")[
                                               :, (k % 2) * 576 + KH * wp:(k % 2) * 576 + KH * wp + KH],
                                           idn[0:KH, 0:KH])
                    ins.then_inc(sem("patches_tp"), 1)
                if k >= 1:
                    embed(pe, mm, k - 1)
            embed(pe, mm, KT - 1)
            pe.wait_ge(sem("emb_cols"), 4)
            for j in range(TT // 2):
                for i in range(2):
                    for c in range(2):
                        ins = pe.transpose(ps[0:TR, j, D * i + KH * c:D * i + KH * c + KH],
                                           xT[:, c, TR * (2 * j + i):TR * (2 * j + i) + TR], idn[0:KH, 0:KH])
                ins.then_inc(sem("emb_tp"), 1)

            pe.wait_ge(sem("slots_rows"), 1)
            for c in range(2):
                ins = pe.transpose(ps[0:KH, 7, SLOTS * c:SLOTS * c + SLOTS], slots[:, KH * c:KH * c + KH],
                                   idn[0:SLOTS, 0:SLOTS])
            ins.then_inc(sem("slots_tp"), 1)

            to_features("ln1", t)
            pe.wait_ge(sem("cols"), 3 * TURN["ln1"] + 3)
            pe.wait_ge(sem("ld_att0"), 16 * N_ATT0)
            W3 = D + 2 * HD
            for tt in range(TT):
                for k in range(2):
                    ins = mm(ps[0:TR, 3 + tt // 2, W3 * (tt % 2):W3 * (tt % 2) + W3],
                             xT[:, k, TR * tt:TR * tt + TR], wqkv0[:, k, :], k == 0, k == 1)
                if tt % 2:
                    ins.then_inc(sem("qkv0_mm"), 1)

            to_features("ln2", t)
            pe.wait_ge(sem("cols"), 3 * TURN["ln2"] + 3)
            for tt in range(TT):
                for k in range(2):
                    ins = mm(ps[0:TR, 6, NE * tt:NE * tt + NE], xT[:, k, TR * tt:TR * tt + TR], wg0[:, k, :],
                             k == 0, k == 1)
            ins.then_inc(sem("gate_mm"), 1)
            pe.wait_ge(sem("onehot"), 1)
            for tt in range(TT):
                ins = pe.transpose(ps[0:NE, 7 if tt < 4 else 3, TR * (tt % 4):TR * (tt % 4) + TR], oh[:, tt, :],
                                   idn[0:TR, 0:TR])
            ins.then_inc(sem("ohT_tp"), 1)
            pe.wait_ge(sem("ohT"), 2)
            pe.wait_ge(sem("ld_b2"), 16)
            for tt in range(TT):
                ins = mm(ps[0:TR, tt // 2, D * (tt % 2):D * (tt % 2) + D], ohT[:, TR * tt:TR * tt + TR], b2pad[:])
            ins.then_inc(sem("b2_mm"), 1)
            pe.wait_ge(sem("moe_y"), 1)
            with pe.Fori(0, NE // 2) as e2:
                for u in range(2):
                    e = e2 * 2 + u
                    pe.wait_ge(sem(f"ld_w1_{u}"), e2 * 32 + 32)
                    for m in range(FT):
                        for n in range(2):
                            q = 2 * m + n
                            if q >= 4:
                                pe.wait_ge(sem("moe_h"), e * 12 + (q - 3))
                            for k in range(2):
                                ins = mm(ps[:, q % 4, 0:NH], w1r[:, u, k, m:FF:FT], xT[:, k, NH * n:NH * n + NH],
                                         k == 0, k == 1)
                            ins.then_inc(sem("moe_h_mm"), 1)
                    pe.wait_ge(sem("moe_h"), e * 12 + 12)
                    pe.wait_ge(sem(f"ld_w2_{u}"), e2 * 16 + 16)
                    for tt in range(TT):
                        if tt >= 2:
                            pe.wait_ge(sem("moe_y"), e * TT + tt)
                        else:
                            pe.wait_ge(sem("moe_y"), e * TT + 1)
                        for m in range(FT):
                            ins = mm(ps[0:TR, 4 + tt % 2, 0:D], hT[:, m, TR * tt:TR * tt + TR], w2r[:, u, m, :],
                                     m == 0, m == FT - 1)
                        ins.then_inc(sem("moe_y_mm"), 1)

            to_features("ffn", a)
            pe.wait_ge(sem("cols"), 3 * TURN["ffn"] + 3)
            for n in range(2):
                for k in range(2):
                    ins = mm(ps[0:KH, 6 + n, 0:NH], w1s[:, k, :], xT[:, k, NH * n:NH * n + NH], k == 0, k == 1)
            ins.then_inc(sem("router_mm"), 1)
            pe.wait_ge(sem("router_h"), 2)
            for tt in range(TT):
                ins = mm(ps[0:TR, 6, NE * tt:NE * tt + NE], rT[:, TR * tt:TR * tt + TR], w2s[:])
            ins.then_inc(sem("logits_mm"), 1)
            pe.wait_ge(sem("ffn_y"), 1)
            with pe.Fori(0, NE // 2) as e2:
                for u in range(2):
                    e = e2 * 2 + u
                    pe.wait_ge(sem(f"ld_down_{u}"), e2 * 32 + 32)
                    for j in range(ZT):
                        for n in range(2):
                            q = 2 * j + n
                            for k in range(2):
                                ins = mm(ps[:, q, 0:NH], downr[:, u, k, j:DZ:ZT], xT[:, k, NH * n:NH * n + NH],
                                         k == 0, k == 1)
                            ins.then_inc(sem("ffn_z_mm"), 1)
                    pe.wait_ge(sem("ffn_z"), e * 4 + 4)
                    pe.wait_ge(sem(f"ld_up_{u}"), e2 * 16 + 16)
                    for tt in range(TT):
                        if tt >= 2:
                            pe.wait_ge(sem("ffn_y"), e * TT + tt)
                        else:
                            pe.wait_ge(sem("ffn_y"), e * TT + 1)
                        for j in range(ZT):
                            ins = mm(ps[0:TR, 4 + tt % 2, 0:D], zT[:, j, TR * tt:TR * tt + TR], upr[:, u, j, :],
                                     j == 0, j == ZT - 1)
                        ins.then_inc(sem("ffn_y_mm"), 1)

            to_features("ln3", t)
            pe.wait_ge(sem("cols"), 3 * TURN["ln3"] + 3)
            for tt in range(TT):
                for k in range(2):
                    ins = mm(ps[0:TR, 4 + tt // 2, D * (tt % 2):D * (tt % 2) + D], xT[:, k, TR * tt:TR * tt + TR],
                             wqkv1[:, k, 2 * D:3 * D], k == 0, k == 1)
                if tt % 2:
                    ins.then_inc(sem("v1_mm"), 1)
            for m in range(4):
                for n in range(2):
                    q = 2 * m + n
                    if q >= 4:
                        pe.wait_ge(sem("qk1"), q - 3)
                    for k in range(2):
                        ins = mm(ps[0:KH, q % 4, 0:NH], wqkv1[:, k, KH * m:KH * m + KH],
                                 xT[:, k, NH * n:NH * n + NH], k == 0, k == 1)
                    ins.then_inc(sem("qk1_mm"), 1)
            pe.wait_ge(sem("qk1"), 8)
            pe.wait_ge(sem("v_ready"), TT)
            attention()
            for u in range(2):
                pe.wait_ge(sem(f"gather{u}"), 16 * PAIRS)
            for j in range(TT // 2):
                for i in range(2):
                    for c in range(2):
                        ins = pe.transpose(ps[0:KH, j, 256 * c + TR * i:256 * c + TR * i + TR],
                                           t[:, 2 * j + i, KH * c:KH * c + KH], idn[0:TR, 0:TR])
                ins.then_inc(sem("tp"), 1)
            pe.wait_ge(sem("cols"), 3 * TURN["proj"] + 3)
            for tt in range(TT):
                for k in range(2):
                    ins = mm(ps[0:TR, 5 + tt // 2, D * (tt % 2):D * (tt % 2) + D], xT[:, k, TR * tt:TR * tt + TR],
                             wpr1[:, k, :], k == 0, k == 1)
                if tt % 2:
                    ins.then_inc(sem("proj_mm"), 1)

            to_features("tok", t)
            pe.wait_ge(sem("cols"), 3 * TURN["tok"] + 3)
            pe.wait_ge(sem("slT"), 1)
            for n in range(2):
                for k in range(2):
                    ins = mm(ps[0:SLOTS, 4 + n, 0:NH], slT[:, k, :], xT[:, k, NH * n:NH * n + NH], k == 0, k == 1)
            ins.then_inc(sem("disp_mm"), 1)
            for tt in range(TT):
                for k in range(2):
                    ins = mm(ps[0:TR, 3, SLOTS * tt:SLOTS * tt + SLOTS], xT[:, k, TR * tt:TR * tt + TR],
                             slT[:, k, :], k == 0, k == 1)
            ins.then_inc(sem("comb_mm"), 1)
            pe.wait_ge(sem("disp"), 1)
            for tt in range(TT):
                ins = pe.transpose(ps[0:TR, 6, SLOTS * tt:SLOTS * tt + SLOTS], disp[:, TR * tt:TR * tt + TR],
                                   idn[0:SLOTS, 0:SLOTS])
            ins.then_inc(sem("disp_tp"), 1)
            pe.wait_ge(sem("dm"), 1)
            for c in range(3):
                for tt in range(TT):
                    n = IPT if tt < TT - 1 else 1
                    for par in range(2):
                        ins = mm(ps[64 * par:64 * par + 64, c, 96 * tt:96 * tt + 32 * n],
                                 a[:, tt, c:D:3], dmt[:, tt, 0:n, par:SLOTS:2])
                ins.then_inc(sem("y_mm"), 1)
            pe.wait_ge(sem("y_copied"), 6)
            for j in range(3):
                ins = mm(ps[0:TR, 5 + j, 0:2 * D], idn[0:TR, 0:TR],
                         h[:, 2 * j:2 * j + 2, :].rearrange("p a b -> p (a b)"), True, False, skip_group_check=True)
                if j < 2:
                    ins.then_inc(sem(("cm_tp", "fc1_used")[j]), 1)
            sel = const("sel")
            with pe.Fori(0, NG // 2) as g2:
                for u in range(2):
                    g = g2 * 2 + u
                    pe.wait_ge(sem(f"ld_fb_{u}"), g2 * 32 + 32)
                    for n in range(2):
                        mm(ps[:, n, 0:384], sel, fb1[:, u, 384 * n:384 * n + 384], True, False, skip_group_check=True)
                    pe.wait_ge(sem("yg"), g + 1)
                    for q in range(QP):
                        pe.wait_ge(sem(f"ld_fc1_{u}_{q}"), g2 * 16 + 16)
                    for c in range(3):
                        for n in range(2):
                            for q in range(QP):
                                ins = mm(ps[32 * q:32 * q + 32, n, 0:384], yg[:, u, c, q, :],
                                         fc1v[:, u, q, c, 384 * n:384 * n + 384], False, c == 2,
                                         skip_group_check=True)
                    ins.then_inc(sem("fc1_used"), 1)
                    pe.wait_ge(sem("xe"), g + 1)
                    for tt in range(TT):
                        ins = pe.transpose(ps[:, 3 + tt // 3, TR * (tt % 3):TR * (tt % 3) + TR],
                                           xe[:, tt].rearrange("p s b -> p (s b)"), idn[0:TR, 0:TR])
                    ins.then_inc(sem("cm_tp"), 1)
                    pe.wait_ge(sem("hid"), g * 2 + 2)
                    pe.wait_ge(sem("cmT"), g * 2 + 2)
                    for m in range(FT):
                        ins = pe.transpose(ps[:, 3 + m // 3, 128 * (m % 3):128 * (m % 3) + 128], hid[:, m:FF:FT], idn)
                        if m % 3 == 2:
                            ins.then_inc(sem("hidT_tp"), 1)
                    mm(ps[:, 2, 0:D], sel, fb2[:, u], True, False, skip_group_check=True)
                    pe.wait_ge(sem("hidT"), g * 4 + 4)
                    for q in range(QP):
                        pe.wait_ge(sem(f"ld_fc2_{u}_{q}"), g2 * 32 + 32)
                    for m in range(FT):
                        for par in range(2):
                            for q in range(QP):
                                ins = mm(ps[32 * q:32 * q + 32, 2, 0:D], hidT[:, m, par, 32 * q:32 * q + 32],
                                         fc2v[:, u, 2 * q + par, m, :], False, m == FT - 1 and par == 1,
                                         skip_group_check=True)
                    ins.then_inc(sem("fc2_used"), 1)
                    pe.wait_ge(sem("yslot"), g + 1)
                    for tt in range(TT):
                        ins = mm(ps[0:TR, 5 + tt // 2, D * (tt % 2):D * (tt % 2) + D], cmT[:, TR * tt:TR * tt + TR],
                                 yslot[:], False, False, skip_group_check=True)
                    ins.then_inc(sem("combined"), 1)

        class Steps:

            def __init__(self, eng, name):
                self.eng, self.sem, self.n = eng, sem(name), 0

            def __call__(self, ins):
                self.n += 1
                ins.then_inc(self.sem, 1)
                self.eng.wait_ge(self.sem, self.n)

        @block.vector
        def _(dve):
            step = Steps(dve, "dve_step")

            def stats(src):
                for tt in range(TT):
                    ins = dve.bn_stats(st[:, tt, :], src[:, tt, :])
                step(ins)
                for tt in range(TT):
                    ins = dve.bn_aggr(mv[:, tt, :], st[:, tt, :])
                return ins

            def normalise(name, src, dst):
                stats(src).then_inc(sem("var"), 1)
                dve.wait_ge(sem("rstd"), ROOT[name] + 1)
                for tt in range(TT):
                    dve.tensor_scalar(dst[:, tt, :], src[:, tt, :], mv[:, tt, 0:1], rs[:, tt:tt + 1],
                                      ALU.subtract, ALU.mult).then_inc(sem("rows"), 1)
                dve.wait_ge(sem("rows"), TT * NORM[name] + TT)

            def mean_square(src):
                step(stats(src))
                step(dve.tensor_tensor(m6[:, 0, :], mv[:, :, 0], mv[:, :, 0], ALU.mult))
                dve.tensor_tensor(m6[:, 1, :], m6[:, 0, :], mv[:, :, 1], ALU.add).then_inc(sem("var"), 1)

            def attention():
                def before(j):
                    dve.wait_ge(sem("s_mm"), j + 1)
                    v = ps[:, j % 2, 0:HEADS * S].rearrange("p (h n) -> p h n", h=HEADS)
                    o = sc[:, j % 2, :].rearrange("p (h n) -> p h n", h=HEADS)
                    if j >= 2:
                        dve.wait_ge(sem("pT_mm"), j - 1)
                    dve.tensor_tensor(o, v, dmask[:], ALU.mult).then_inc(sem("s_read"), 1)
                    dve.wait_ge(sem("s_read"), j + 1)
                    step(dve.tensor_reduce(mx[:, j % 2, :], o, X, ALU.max))
                    dve.tensor_tensor(o, o, bcast(mx[:, j % 2, :], 2, S), ALU.subtract).then_inc(sem("s_sub"), 1)

                def after(j):
                    dve.wait_ge(sem("exp"), j + 1)
                    o = sc[:, j % 2, :].rearrange("p (h n) -> p h n", h=HEADS)
                    step(dve.tensor_reduce(den[:, j % 2, :], o, X, ALU.add))
                    step(dve.reciprocal(den[:, j % 2, :], den[:, j % 2, :]))
                    dve.wait_ge(sem("o_mm"), j + 1)
                    if j >= 2:
                        dve.wait_ge(sem(f"gather{j % 2}"), 32 * (j // 2))
                    dve.tensor_tensor(ob[:, j % 2, :].rearrange("p (h d) -> p h d", h=HEADS),
                                      ps[:, 4 + j % 2, 0:D].rearrange("p (h d) -> p h d", h=HEADS),
                                      bcast(den[:, j % 2, :], 2, HD), ALU.mult).then_inc(sem("o_ready"), 1)

                before(0)
                for j in range(B // 2):
                    if j + 1 < B // 2:
                        before(j + 1)
                    after(j)
                for u in range(2):
                    dve.wait_ge(sem(f"gather{u}"), 16 * PAIRS)

            def first_max(src, mask):
                step(dve.tensor_reduce(m6[:, 0, :], src[:], X, ALU.max))
                step(dve.tensor_tensor(mask[:], src[:], bcast(m6[:, 0, :], 2, NE), ALU.is_equal))
                step(dve.tensor_tensor(key[:], mask[:], bcast(const("rev", TR), 1, TT), ALU.mult))
                step(dve.tensor_reduce(m6[:, 0, :], key[:], X, ALU.max))
                step(dve.tensor_tensor(mask[:], key[:], bcast(m6[:, 0, :], 2, NE), ALU.is_equal))

            for k in range(0, KT, 2):
                dve.wait_ge(sem(f"ld_x{k // 2}"), 16)
                if k >= 4:
                    dve.wait_ge(sem("patches_tp"), 2 * (k - 4) + 2)
                dve.tensor_copy(rows_of(k), xin[:, 2 * k:2 * k + 2].rearrange("p r v c -> p v r c"))\
                    .then_inc(sem("patches_rows0"), 1)
                for kk in (k, k + 1):
                    dve.wait_ge(sem("patches_tp"), 2 * kk + 1)
                    dve.tensor_copy(patT[:, kk, 0:288], ps[0:KH, (2 * kk) % 4, 0:288])\
                        .then_inc(sem("patches_copied0"), 1)
            dve.wait_ge(sem("ld_tok"), 16 * 9)
            step(dve.tensor_tensor(posr[:], posr[:], addr[:], ALU.add))
            dve.wait_ge(sem("emb_mm"), 2)
            dve.wait_ge(sem("pads_zero"), 1)
            for n in range(2):
                dve.tensor_copy(emb_out(0, n), emb_in(0, n)).then_inc(sem("emb_cols"), 1)
            for j in range(TT // 2):
                dve.wait_ge(sem("emb_tp"), j + 1)
                ins = dve.tensor_tensor(h[:, 2 * j:2 * j + 2, :],
                                        ps[0:TR, j, 0:2 * D].rearrange("p (i d) -> p i d", i=2),
                                        bcast(posr[:], 1, 2), ALU.add)
            step(ins)
            dve.wait_ge(sem("ld_small"), 16 * N_SMALL)
            step(dve.bn_stats(sst[:, 0:6], slots[:]))
            step(dve.bn_aggr(sst[:, 6:8], sst[:, 0:6]))
            step(dve.tensor_tensor(sst[:, 8:9], sst[:, 6:7], sst[:, 6:7], ALU.mult))
            dve.tensor_tensor(sst[:, 9:10], sst[:, 8:9], sst[:, 7:8], ALU.add).then_inc(sem("var"), 1)
            step(dve.tensor_tensor(dmask[:], bcast(const("eye"), 1, HEADS), bcast(temp[:], 2, S), ALU.mult))
            step(dve.tensor_scalar(dmask[:], dmask[:], -1.0, 1.0, ALU.mult, ALU.add))
            dve.wait_ge(sem("rstd"), ROOT["slots"] + 1)
            dve.tensor_scalar(slots[:], slots[:], sst[:, 10:11], slsc[:, 0:1], ALU.mult, ALU.mult)\
                .then_inc(sem("slots_rows"), 1)
            dve.wait_ge(sem("slots_tp"), 1)
            dve.tensor_copy(slT[:], ps[0:KH, 7, 0:2 * SLOTS].rearrange("p (c n) -> p c n", c=2))\
                .then_inc(sem("slT"), 1)

            normalise("in0", h, a)
            normalise("ln1", a, t)
            for j in range(TT // 2):
                dve.wait_ge(sem("qkv0_mm"), j + 1)
                if j == 0:
                    dve.wait_ge(sem("ld_att0"), 16 * N_ATT0)
                dve.tensor_tensor(qkv[:, 2 * j:2 * j + 2, :],
                                  ps[0:TR, 3 + j, 0:448].rearrange("p (i d) -> p i d", i=2),
                                  bcast(bqkv0[:], 1, 2), ALU.add).then_inc(sem("qkv0"), 1)
            dve.wait_ge(sem("qkv0"), TT // 2)

            def heads(ap, n):
                return ap.rearrange("p t (h e) -> p t h e", h=n)

            def rope(src, dst, tmp, n):
                def table(name, lo, hi):
                    return bcast(bcast(const(name, TR)[:, lo:hi], 1, n), 1, TT)

                half = HD // 2
                dve.tensor_tensor(heads(dst, n), heads(src, n), table("cos", 0, HD), ALU.mult)
                dve.tensor_tensor(heads(tmp, n)[:, :, :, 0:half], heads(src, n)[:, :, :, half:HD],
                                  table("sin", 0, half), ALU.mult)
                step(dve.tensor_tensor(heads(tmp, n)[:, :, :, half:HD], heads(src, n)[:, :, :, 0:half],
                                       table("sin", half, HD), ALU.mult))
                return dve.tensor_tensor(dst, dst, tmp, ALU.add)

            step(rope(qkv[:, :, 0:D], t[:], rtmp, HEADS))
            step(rope(qkv[:, :, D:D + HD], krot[:], ktmp[:], 1))
            q4 = heads(t[:], HEADS)
            step(dve.tensor_tensor(q4, q4, bcast(krot[:], 2, HEADS), ALU.mult))
            step(dve.tensor_reduce(s0[:, 0], q4, X, ALU.add))
            step(dve.tensor_tensor(s0[:, 1], s0[:, 0], s0[:, 0], ALU.max))
            dve.tensor_tensor(s0[:, 0], s0[:, 0], s0[:, 1], ALU.subtract).then_inc(sem("s0_sub"), 1)
            dve.wait_ge(sem("s0_exp"), 1)
            step(dve.tensor_scalar(s0[:, 1], s0[:, 0], float(HEADS), None, ALU.mult))
            step(dve.reciprocal(s0[:, 1], s0[:, 1]))
            step(dve.scalar_tensor_tensor(out=s0[:, 0], in0=s0[:, 0], scalar=float(HEADS), in1=s0[:, 1],
                                          op0=ALU.mult, op1=ALU.mult))
            step(dve.tensor_tensor(q4, bcast(s0[:, 0], 3, HD), bcast(qkv[:, :, D + HD:D + 2 * HD], 2, HEADS), ALU.mult))
            step(dve.tensor_tensor(a[:], a[:], t[:], ALU.add))

            normalise("ln2", a, t)
            dve.wait_ge(sem("gate_mm"), 1)
            step(dve.tensor_tensor(lg[:], ps[0:TR, 6, 0:TT * NE].rearrange("p (t e) -> p t e", t=TT),
                                   bcast(bg0[:], 1, TT), ALU.add))
            first_max(lg, oh)
            dve.tensor_copy(gate[:], oh[:]).then_inc(sem("onehot"), 1)
            dve.wait_ge(sem("ohT_tp"), 1)
            dve.wait_ge(sem("h_pads"), 1)
            dve.tensor_copy(ohT[0:NE, 0:4 * TR], ps[0:NE, 7, 0:4 * TR]).then_inc(sem("ohT"), 1)
            dve.tensor_copy(ohT[0:NE, 4 * TR:NPAD], ps[0:NE, 3, 0:2 * TR]).then_inc(sem("ohT"), 1)
            dve.wait_ge(sem("b2_mm"), 1)
            for j in range(TT // 2):
                ins = dve.tensor_tensor(a[:, 2 * j:2 * j + 2, :], a[:, 2 * j:2 * j + 2, :],
                                        ps[0:TR, j, 0:2 * D].rearrange("p (i d) -> p i d", i=2), ALU.add)
            ins.then_inc(sem("moe_y"), 1)

            def experts(name, gates):
                with dve.Fori(0, NE // 2) as e2:
                    for u in range(2):
                        e = e2 * 2 + u
                        dve.wait_ge(sem(f"{name}_y"), e * TT + 1)
                        dve.tensor_copy(gcol[:, u, :], gates[:, :, bass.ds(e, 1)].rearrange("p t o -> p (t o)"))\
                            .then_inc(sem(f"{name}_gcol"), 1)
                        dve.wait_ge(sem(f"{name}_gcol"), e + 1)
                        for tt in range(TT):
                            dve.wait_ge(sem(f"{name}_y_mm"), e * TT + (tt + 1))
                            dve.scalar_tensor_tensor(out=a[:, tt, :], in0=ps[0:TR, 4 + tt % 2, 0:D],
                                                     scalar=gcol[:, u, tt:tt + 1], in1=a[:, tt, :],
                                                     op0=ALU.mult, op1=ALU.add).then_inc(sem(f"{name}_y"), 1)
                dve.wait_ge(sem(f"{name}_y"), NE * TT + 1)

            experts("moe", oh)
            step(dve.tensor_tensor(h[:], h[:], a[:], ALU.add))

            normalise("ffn", h, a)
            dve.wait_ge(sem("logits_mm"), 1)
            step(dve.tensor_tensor(lg[:], ps[0:TR, 6, 0:TT * NE].rearrange("p (t e) -> p t e", t=TT),
                                   bcast(b2s[:], 1, TT), ALU.add))
            step(dve.tensor_reduce(m6[:, 0, :], lg[:], X, ALU.max))
            dve.tensor_tensor(lg[:], lg[:], bcast(m6[:, 0, :], 2, NE), ALU.subtract).then_inc(sem("router_sub"), 1)
            dve.wait_ge(sem("router_exp"), 1)
            step(dve.tensor_reduce(m6[:, 0, :], lg[:], X, ALU.add))
            step(dve.reciprocal(m6[:, 1, :], m6[:, 0, :]))
            step(dve.tensor_tensor(lg[:], lg[:], bcast(m6[:, 1, :], 2, NE), ALU.mult))
            first_max(lg, oh)
            step(dve.scalar_tensor_tensor(out=gate[:], in0=oh[:], scalar=-4.0, in1=lg[:], op0=ALU.mult, op1=ALU.add))
            step(dve.tensor_reduce(m6[:, 0, :], gate[:], X, ALU.max))
            step(dve.tensor_tensor(gate[:], gate[:], bcast(m6[:, 0, :], 2, NE), ALU.is_equal))
            step(dve.tensor_tensor(key[:], gate[:], bcast(const("rev", TR), 1, TT), ALU.mult))
            step(dve.tensor_reduce(m6[:, 0, :], key[:], X, ALU.max))
            step(dve.tensor_tensor(gate[:], key[:], bcast(m6[:, 0, :], 2, NE), ALU.is_equal))
            step(dve.tensor_tensor(oh[:], oh[:], gate[:], ALU.add))
            step(dve.tensor_tensor(oh[:], oh[:], lg[:], ALU.mult))
            step(dve.tensor_reduce(m6[:, 0, :], oh[:], X, ALU.add))
            step(dve.tensor_scalar(m6[:, 0, :], m6[:, 0, :], 1e-8, None, ALU.add))
            step(dve.reciprocal(m6[:, 1, :], m6[:, 0, :]))
            dve.tensor_tensor(gate[:], oh[:], bcast(m6[:, 1, :], 2, NE), ALU.mult).then_inc(sem("ffn_y"), 1)
            experts("ffn", gate)
            normalise("u", a, t)
            step(dve.tensor_tensor(t[:], t[:], bcast(gamma[:], 1, TT), ALU.mult))
            step(dve.tensor_tensor(t[:], t[:], bcast(beta[:], 1, TT), ALU.add))
            step(dve.tensor_tensor(h[:], h[:], t[:], ALU.add))

            normalise("ln3", h, t)
            for j in range(TT // 2):
                dve.wait_ge(sem("v1_mm"), j + 1)
                dve.tensor_copy(a[:, 2 * j:2 * j + 2, :], ps[0:TR, 4 + j, 0:2 * D].rearrange("p (i d) -> p i d", i=2))\
                    .then_inc(sem("v_ready"), 2)
            step(dve.tensor_tensor(h[:], h[:], bcast(bpr1[:], 1, TT), ALU.add))
            attention()
            for j in range(TT // 2):
                dve.wait_ge(sem("proj_mm"), j + 1)
                ins = dve.tensor_tensor(h[:, 2 * j:2 * j + 2, :], h[:, 2 * j:2 * j + 2, :],
                                        ps[0:TR, 5 + j, 0:2 * D].rearrange("p (i d) -> p i d", i=2), ALU.add)
            step(ins)

            normalise("tok0", h, a)
            mean_square(a)
            dve.wait_ge(sem("rstd"), ROOT["ms_a"] + 1)
            for tt in range(TT):
                ins = dve.scalar_tensor_tensor(out=a[:, tt, :], in0=a[:, tt, :], scalar=rs[:, tt:tt + 1], in1=nw[:],
                                               op0=ALU.mult, op1=ALU.mult)
            step(ins)
            mean_square(a)
            dve.wait_ge(sem("rstd"), ROOT["ms_x"] + 1)
            for tt in range(TT):
                dve.tensor_scalar(t[:, tt, :], a[:, tt, :], rs[:, tt:tt + 1], None, ALU.mult)\
                    .then_inc(sem("rows"), 1)
            dve.wait_ge(sem("disp_mm"), 1)
            dve.wait_ge(sem("soft_zero"), 1)

            def by_image(ap):
                return ap.rearrange("p (b s) -> p b s", s=S)

            for n in range(2):
                ins = dve.tensor_reduce(mxd[:, 0, 8 * n:8 * n + 8], by_image(ps[0:SLOTS, 4 + n, 0:NH]), X, ALU.max)
            step(ins)
            for n in range(2):
                ins = dve.tensor_tensor(by_image(disp[:, NH * n:NH * n + NH]), by_image(ps[0:SLOTS, 4 + n, 0:NH]),
                                        bcast(mxd[:, 0, 8 * n:8 * n + 8], 2, S), ALU.subtract)
            ins.then_inc(sem("disp_sub"), 1)
            dve.wait_ge(sem("comb_mm"), 1)
            cps = ps[0:TR, 3, 0:TT * SLOTS].rearrange("p (t s) -> p t s", t=TT)
            step(dve.tensor_reduce(mxc[:, 0, :], cps, X, ALU.max))
            dve.tensor_tensor(comb[:], cps, bcast(mxc[:, 0, :], 2, SLOTS), ALU.subtract).then_inc(sem("comb_sub"), 1)
            dve.wait_ge(sem("disp_exp"), 1)
            dd = by_image(disp[:, 0:NTOK])
            step(dve.tensor_reduce(mxd[:, 0, :], dd, X, ALU.add))
            step(dve.reciprocal(mxd[:, 1, :], mxd[:, 0, :]))
            dve.tensor_tensor(dd, dd, bcast(mxd[:, 1, :], 2, S), ALU.mult).then_inc(sem("disp"), 1)
            dve.wait_ge(sem("comb_exp"), 1)
            step(dve.tensor_reduce(mxc[:, 0, :], comb[:], X, ALU.add))
            step(dve.reciprocal(mxc[:, 1, :], mxc[:, 0, :]))
            dve.tensor_tensor(comb[:], comb[:], bcast(mxc[:, 1, :], 2, SLOTS), ALU.mult).then_inc(sem("comb"), 1)
            dve.wait_ge(sem("disp_tp"), 1)
            dve.tensor_tensor(dmt[:], bcast(ps[0:TR, 6, 0:TT * SLOTS].rearrange("p (t s) -> p t s", t=TT), 2, IPT),
                              bcast(bcast(const("vmask", TR), 1, TT), 3, SLOTS), ALU.mult).then_inc(sem("dm"), 1)
            for c in range(3):
                dve.wait_ge(sem("y_mm"), c + 1)
                dve.tensor_copy(ycmp[0:64, c], ps[0:64, c, :].rearrange("p (b j) -> p j b", b=B))\
                    .then_inc(sem("y_copied"), 1)
            with dve.Fori(0, NG) as g:
                dve.wait_ge(sem("cm_tp"), g + 2)
                dve.tensor_copy(cmT[:, 0:3 * TR], ps[:, 3, 0:3 * TR]).then_inc(sem("cmT"), 1)
                dve.wait_ge(sem("hidT_tp"), g * 2 + 1)
                for par in range(2):
                    dve.tensor_copy(hid_out(0, par), hid_in(0, par)).then_inc(sem("hidT"), 1)
                dve.wait_ge(sem("fc2_used"), g + 1)
                dve.tensor_copy(yslot[:], ps[:, 2, 0:D]).then_inc(sem("yslot"), 1)
            dve.wait_ge(sem("combined"), NG)
            for j in range(TT // 2):
                ins = dve.tensor_copy(h[:, 2 * j:2 * j + 2, :],
                                      ps[0:TR, 5 + j, 0:2 * D].rearrange("p (i d) -> p i d", i=2))
            ins.then_inc(sem("out_ready"), 1)

        @block.scalar
        def _(act):
            def columns(name, affine=None):
                for j in range(TT // 2):
                    act.wait_ge(sem("tp"), 3 * TURN[name] + j + 1)
                    lo, hi = 2 * TR * j, 2 * TR * j + 2 * TR
                    if affine is None:
                        act.activation(xT[:, :, lo:hi], ps[0:KH, j, :].rearrange("p (c n) -> p c n", c=2)[:, :, 0:2 * TR],
                                       ACT.Copy).then_inc(sem("cols"), 1)
                        continue
                    for c in range(2):
                        ins = act.activation(xT[:, c, lo:hi], ps[0:KH, j, 256 * c:256 * c + 2 * TR], ACT.Identity,
                                             scale=lnv[:, affine, c:c + 1], bias=lnv[:, affine + 1, c:c + 1])
                    ins.then_inc(sem("cols"), 1)

            def attention():
                def values(j):
                    if j >= 2:
                        act.wait_ge(sem("o_mm"), j - 1)
                    for x in range(IPT):
                        for i in range(2):
                            b = 2 * j + i
                            ins = act.activation(
                                vblk[:, j % 2, i, :, HD * x:HD * x + HD],
                                vrep[:, b, :].rearrange("p (g n) -> p g n", g=4)[:, :, HD * x:HD * x + HD],
                                ACT.Identity, scale=const("vmask", TR)[:, x:x + 1])
                    ins.then_inc(sem("vblk"), 1)

                def exps(j):
                    act.wait_ge(sem("s_sub"), j + 1)
                    act.activation(sc[:, j % 2, :], sc[:, j % 2, :], ACT.Exp, scale=HD ** -0.5)\
                        .then_inc(sem("exp"), 1)

                act.wait_ge(sem("vrep"), 16 * 9)
                values(0)
                exps(0)
                for j in range(B // 2):
                    if j + 1 < B // 2:
                        values(j + 1)
                        exps(j + 1)
                    act.wait_ge(sem("pT_mm"), j + 1)
                    if j >= 2:
                        act.wait_ge(sem("o_mm"), j - 1)
                    act.activation(pT[:, j % 2, :], ps[0:TR, 2 + j % 2, :], ACT.Copy).then_inc(sem("pT"), 1)

            for k in range(1, KT, 2):
                act.wait_ge(sem(f"ld_x{k // 2}"), 16)
                if k >= 4:
                    act.wait_ge(sem("patches_tp"), 2 * (k - 4) + 2)
                act.activation(rows_of(k), xin[:, 2 * k:2 * k + 2].rearrange("p r v c -> p v r c"), ACT.Copy)\
                    .then_inc(sem("patches_rows1"), 1)
                for kk in (k - 1, k):
                    act.wait_ge(sem("patches_tp"), 2 * kk + 2)
                    act.activation(patT[:, kk, 288:576], ps[0:KH, (2 * kk + 1) % 4, 0:288], ACT.Copy)\
                        .then_inc(sem("patches_copied1"), 1)
            act.wait_ge(sem("emb_mm"), 4)
            act.wait_ge(sem("pads_zero"), 1)
            for n in range(2):
                act.activation(emb_out(1, n), emb_in(1, n), ACT.Copy).then_inc(sem("emb_cols"), 1)

            act.wait_ge(sem("ld_small"), 16 * N_SMALL)
            columns("ln1", 0)
            act.wait_ge(sem("s0_sub"), 1)
            act.activation(s0[:, 0], s0[:, 0], ACT.Exp, scale=HD ** -0.5).then_inc(sem("s0_exp"), 1)
            columns("ln2", 2)
            act.wait_ge(sem("h_pads"), 1)
            with act.Fori(0, NE // 2) as e2:
                for u in range(2):
                    e = e2 * 2 + u
                    act.wait_ge(sem(f"ld_w1_{u}"), e2 * 32 + 32)
                    for q in range(2 * FT):
                        act.wait_ge(sem("moe_h_mm"), e * 12 + (q + 1))
                        act.activation(hT[:, q // 2, NH * (q % 2):NH * (q % 2) + NH], ps[:, q % 4, 0:NH], ACT.Gelu,
                                       bias=b1r[:, u, q // 2:q // 2 + 1]).then_inc(sem("moe_h"), 1)
            columns("ffn")
            act.wait_ge(sem("router_mm"), 1)
            for n in range(2):
                act.activation(rT[:, NH * n:NH * n + NH], ps[0:KH, 6 + n, 0:NH], ACT.Gelu, bias=b1s[:, 0:1])\
                    .then_inc(sem("router_h"), 1)
            act.wait_ge(sem("router_sub"), 1)
            act.activation(lg[:], lg[:], ACT.Exp).then_inc(sem("router_exp"), 1)
            with act.Fori(0, NE // 2) as e2:
                for u in range(2):
                    e = e2 * 2 + u
                    act.wait_ge(sem(f"ld_down_{u}"), e2 * 32 + 32)
                    for q in range(2 * ZT):
                        act.wait_ge(sem("ffn_z_mm"), e * 4 + (q + 1))
                        act.activation(zT[:, q // 2, NH * (q % 2):NH * (q % 2) + NH], ps[:, q, 0:NH], ACT.Gelu,
                                       bias=downb[:, u, q // 2:q // 2 + 1]).then_inc(sem("ffn_z"), 1)
            columns("ln3")
            for q in range(8):
                act.wait_ge(sem("qk1_mm"), q + 1)
                dst = (qT, kT)[q // 4]
                act.activation(dst[:, q // 2 % 2, NH * (q % 2):NH * (q % 2) + NH], ps[0:KH, q % 4, 0:NH], ACT.Copy)\
                    .then_inc(sem("qk1"), 1)
            attention()
            columns("proj")
            columns("tok")
            act.wait_ge(sem("disp_sub"), 1)
            act.activation(disp[:, 0:NTOK], disp[:, 0:NTOK], ACT.Exp).then_inc(sem("disp_exp"), 1)
            act.wait_ge(sem("comb_sub"), 1)
            act.activation(comb[:], comb[:], ACT.Exp).then_inc(sem("comb_exp"), 1)
            for c in range(3):
                act.wait_ge(sem("y_mm"), c + 1)
                act.activation(ycmp[64:128, c], ps[64:128, c, :].rearrange("p (b j) -> p j b", b=B), ACT.Copy)\
                    .then_inc(sem("y_copied"), 1)
            with act.Fori(0, NG) as g:
                act.wait_ge(sem("fc1_used"), g + 2)
                for n in range(2):
                    act.activation(hid[:, 384 * n:384 * n + 384], ps[:, n, 0:384], ACT.Gelu).then_inc(sem("hid"), 1)
                act.wait_ge(sem("cm_tp"), g + 2)
                act.activation(cmT[:, 3 * TR:NPAD], ps[:, 4, 0:3 * TR], ACT.Copy).then_inc(sem("cmT"), 1)
                act.wait_ge(sem("hidT_tp"), g * 2 + 2)
                for par in range(2):
                    act.activation(hid_out(1, par), hid_in(1, par), ACT.Copy).then_inc(sem("hidT"), 1)

        @block.gpsimd
        def _(pool):
            step = Steps(pool, "pool_step")

            def root(out_, in_, eps, name, rows=TR, n=TT, floor=False):
                pool.wait_ge(sem("var"), ROOT[name] + 1)
                half = const("mhalf", rows)[:, 0:n]
                step(pool.tensor_scalar(ve[0:rows, 0:n], in_, *eps))
                ins = pool.tensor_tensor(out_, ve[0:rows, 0:n], half, ALU.pow)
                if floor:
                    step(ins)
                    ins = pool.tensor_scalar(out_, out_, 1e5, None, ALU.min)
                ins.then_inc(sem("rstd"), 1)

            def keys():
                for j in range(B // 2):
                    if j >= 2:
                        pool.wait_ge(sem("s_mm"), j - 1)
                    for i in range(2):
                        b = 2 * j + i
                        for c in range(2):
                            ins = pool.tensor_tensor(kblk[:, j % 2, c, i, :].rearrange("p (x n) -> p x n", x=HH),
                                                     bcast(kT[:, c, S * b:S * b + S], 1, HH),
                                                     bcast(const("kmask", KH), 2, S), ALU.mult)
                    ins.then_inc(sem("kblk"), 1)

            plus = (LN_EPS, None, ALU.add)
            pool.memset(xT[:], 0.0)
            pool.memset(b2pad[:], 0.0)
            pool.memset(fb1[:], 0.0)
            pool.memset(fb2[:], 0.0).then_inc(sem("pads_zero"), 1)
            pool.wait_ge(sem("ld_cst"), 16)
            root(sst[:, 10:11], sst[:, 9:10], (float(D), None, ALU.mult), "slots", SLOTS, 1, True)
            for name in ("in0", "ln1"):
                root(rs[:, 0:TT], mv[:, :, 1], plus, name)
            pool.wait_ge(sem("emb_cols"), 4)
            pool.memset(ohT[:], 0.0)
            pool.memset(hT[:, :, NTOK:NPAD], 0.0).then_inc(sem("h_pads"), 1)
            for name in ("ln2", "ffn", "u", "ln3"):
                root(rs[:, 0:TT], mv[:, :, 1], plus, name)
            pool.memset(qT[:, :, NTOK:NPAD], 0.0).then_inc(sem("q_pads"), 1)
            pool.wait_ge(sem("qk1"), 8)
            keys()
            root(rs[:, 0:TT], mv[:, :, 1], plus, "tok0")
            pool.memset(cmT[:], 0.0)
            pool.memset(hidT[:], 0.0).then_inc(sem("soft_zero"), 1)
            root(rs[:, 0:TT], m6[:, 1, :], plus, "ms_a")
            root(rs[:, 0:TT], m6[:, 1, :], (float(D), None, ALU.mult), "ms_x", floor=True)
            pool.wait_ge(sem("comb"), 1)
            pool.wait_ge(sem("y_copied"), 6)
            with pool.Fori(0, NG // 2) as g2:
                for u in range(2):
                    g = g2 * 2 + u
                    pool.wait_ge(sem("fc1_used"), g2 * 2 + 1)
                    for c in range(3):
                        ins = pool.tensor_tensor(
                            yg[:, u, c].rearrange("p q (two b) -> p q two b", two=2),
                            bcast(ycmp[:, c, bass.ds(g * QP, QP), :], 2, 2),
                            bcast(bcast(const("pmask"), 1, QP), 3, B), ALU.mult)
                    ins.then_inc(sem("yg"), 1)
                    pool.wait_ge(sem("cm_tp"), g + 1)
                    for tt in range(TT):
                        ins = pool.tensor_tensor(xe[:, tt],
                                                 bcast(comb[:, tt, bass.ds(g * GS, GS)], 2, B),
                                                 bcast(const("bmask", TR)[:, B * tt:B * tt + B], 1, GS), ALU.mult)
                    ins.then_inc(sem("xe"), 1)


INPUTS = ["x", "L0_tok_W_proj", "L0_tok_b_proj", "L0_tok_cls_token", "L0_tok_pos_embedding", "L0_attn_ln1_g",
          "L0_attn_ln1_b", "L0_attn_Wq", "L0_attn_bq", "L0_attn_Wk", "L0_attn_bk", "L0_attn_Wv", "L0_attn_bv",
          "L0_attn_ln2_g", "L0_attn_ln2_b", "L0_attn_Wg", "L0_attn_bg", "L0_attn_W1", "L0_attn_b1", "L0_attn_W2",
          "L0_attn_b2", "L0_ffn_w1", "L0_ffn_b1", "L0_ffn_w2", "L0_ffn_b2", "L0_ffn_down_w", "L0_ffn_down_b",
          "L0_ffn_up_w", "L0_ffn_gamma", "L0_ffn_beta", "L1_attn_w_qkv", "L1_attn_w_proj", "L1_attn_b_proj",
          "L1_attn_temperature", "L1_ffn_slots", "L1_ffn_scale", "L1_ffn_fc1_weight", "L1_ffn_fc1_bias",
          "L1_ffn_fc2_weight", "L1_ffn_fc2_bias", "L1_ffn_norm_weight"]


def kernel(**inputs):
    import concourse.bacc as bacc
    from concourse.bass_utils import run_bass_kernel_spmd

    nc = bacc.Bacc("TRN2", target_bir_lowering=False, num_devices=1)
    arrays, w = {}, {}
    for name in INPUTS:
        v = np.ascontiguousarray(inputs[name])
        arrays[f"in_{name}"] = v
        w[name] = nc.dram_tensor(f"in_{name}", v.shape, mybir.dt.from_np(v.dtype), kind="ExternalInput").ap()
    table = constant_table()
    arrays["consts"] = table
    consts = nc.dram_tensor("consts", table.shape, F32, kind="ExternalInput").ap()
    out = nc.dram_tensor("out", (B, S, D), F32, kind="ExternalOutput").ap()
    vit_tower(nc, w, consts, out)
    r = run_bass_kernel_spmd(nc, [arrays], core_ids=[0])
    return r.results[0]["out"]
```

```python
from contextlib import ExitStack

import numpy as np

import concourse.bass as bass
from concourse import mybir

F32 = mybir.dt.float32
I32 = mybir.dt.int32
ALU = mybir.AluOpType
ACT = mybir.ActivationFunctionType
X = mybir.AxisListType.X

B, IMG, PATCH, CH = 16, 96, 16, 3
D = 192
KH = D // 2
S = (IMG // PATCH) ** 2 + 1
NTOK = B * S
IPT = 3
TR = IPT * S
TT = -(-B // IPT)
NPAD = TR * TT
LAST = NTOK - (TT - 1) * TR
NH = NTOK // 2
HEADS, HD = 12, 16
HH = HEADS // 2
HW = HH * S
NE = 8
FF = 768
FT = FF // 128
DZ = 256
ZT = DZ // 128
SLOTS = 64
GS = 8
NG = SLOTS // GS
QP = GS // 2
WP = IMG // PATCH
ROW = PATCH * CH
PDIM = PATCH * ROW
KT = PDIM // KH
LN_EPS = 1e-5
RT = 128
NRT = (NTOK + NE * (RT - 1)) // RT
LEVELS = -(-NTOK // RT)

CONSTS = {}
_at = 0
for _name, _n in (("ident", 128), ("sel", 128), ("kmask", HH), ("vmask", IPT), ("eye", S), ("cos", HD),
                  ("sin", HD), ("bmask", TT * B), ("rev", NE), ("pmask", 2), ("mhalf", 8), ("valid", 1), ("level", LEVELS),
                  ("lower", NE * NE), ("tile", NRT), ("before", TR), ("ones", TR)):
    CONSTS[_name] = (_at, _at + _n)
    _at += _n
NCONST = _at
NKEEP = CONSTS["before"][0]


def constant_table():
    c = np.zeros((128, NCONST), np.float32)

    def put(name, a):
        lo, hi = CONSTS[name]
        c[: a.shape[0], lo:hi] = a

    row = np.arange(128)
    put("ident", np.eye(128, dtype=np.float32))
    put("sel", (row[:GS, None] == row[None, :] // B).astype(np.float32))
    put("kmask", (row[:KH, None] // HD == np.arange(HH)[None, :]).astype(np.float32))
    put("vmask", (row[:TR, None] // S == np.arange(IPT)[None, :]).astype(np.float32))
    put("eye", (row[:, None] % 64 == np.arange(S)[None, :]).astype(np.float32))
    inv = (np.float32(1.0) / np.float32(10000.0) ** (np.arange(0, HD, 2, dtype=np.float32) / HD)).astype(np.float32)
    ang = ((row[:TR] % S).astype(np.float32)[:, None] * inv[None, :]).astype(np.float32)
    cos, sin = np.cos(ang), np.sin(ang)
    put("cos", np.concatenate([cos, cos], 1))
    put("sin", np.concatenate([-sin, sin], 1))
    image = IPT * np.arange(TT)[None, :] + row[:TR, None] // S
    put("bmask", (image[:, :, None] == np.arange(B)).astype(np.float32).reshape(TR, TT * B))
    put("rev", np.broadcast_to(np.arange(NE, 0, -1, dtype=np.float32), (128, NE)))
    put("pmask", (row[:, None] // 64 == np.arange(2)[None, :]).astype(np.float32))
    put("mhalf", np.full((128, 8), -0.5, np.float32))
    put("before", (row[:TR, None] < row[None, :TR]).astype(np.float32))
    put("ones", np.ones((TR, TR), np.float32))
    put("valid", (row[:TR, None] < LAST).astype(np.float32))
    put("level", np.broadcast_to(RT * np.arange(LEVELS, dtype=np.float32), (128, LEVELS)))
    lower = np.arange(NE)[:, None] > np.arange(NE)[None, :]
    put("lower", np.broadcast_to(lower.reshape(1, NE * NE), (128, NE * NE)).astype(np.float32))
    put("tile", np.broadcast_to(np.arange(NRT, dtype=np.float32), (128, NRT)))
    return c


def bcast(ap, axis, n):
    ap = ap.unsqueeze(axis)
    shape = list(ap.shape)
    shape[axis] = n
    return ap.broadcast_to(shape)


def vit_tower(nc, w, consts, out):
    with ExitStack() as ctx:
        def sb(name, shape, dtype=F32):
            return ctx.enter_context(nc.sbuf_tensor(name, shape, dtype))

        sems = {}

        def sem(name):
            if name not in sems:
                sems[name] = ctx.enter_context(nc.semaphore(name))
            return sems[name]

        ps = ctx.enter_context(nc.psum_tensor("ps", [128, 8, 512], F32))

        fc1 = sb("fc1", [128, 2, QP * 3 * FF])
        fc2 = sb("fc2", [128, 2, GS * FT * D])
        fc1v = fc1[:, :, :].rearrange("p u (q c f) -> p u q c f", q=QP, c=3)
        fc2v = fc2[:, :, :].rearrange("p u (s m d) -> p u s m d", s=GS, m=FT)
        wa, wb = fc1[:, 1, :], fc2[:, 1, :]

        at = [0, 0]

        def carve(which, parts, n):
            lo = at[which]
            at[which] = lo + n
            assert at[which] <= QP * 3 * FF
            return (wa, wb)[which][0:parts, lo:lo + n]

        w1r = carve(0, KH + 1, 2 * 2 * FF).rearrange("p (u k f) -> p u k f", u=2, k=2)
        w2r = carve(0, 128, 2 * FT * D).rearrange("p (u m d) -> p u m d", u=2, m=FT)
        wproj = carve(0, KH, KT * D).rearrange("p (k d) -> p k d", k=KT)
        downr = carve(0, KH, 2 * 2 * DZ).rearrange("p (u k f) -> p u k f", u=2, k=2)
        upr = carve(0, 128, 2 * ZT * D).rearrange("p (u j d) -> p u j d", u=2, j=ZT)
        xin = carve(1, B * WP, PATCH * IMG * CH).rearrange("p (r v c) -> p r v c", r=PATCH, v=WP)
        patT = carve(1, KH, KT * B * 36).rearrange("p (k n) -> p k n", k=KT)
        at[1] = 0
        vrep = carve(1, TR, B * D).rearrange("p (b d) -> p b d", b=B)
        kblk = carve(1, KH, 2 * 2 * 2 * HW).rearrange("p (u c i n) -> p u c i n", u=2, c=2, i=2)
        vblk = carve(1, TR, 2 * 2 * 4 * 51).rearrange("p (u n c) -> p u n c", u=2, c=51)
        qT = carve(1, KH, 2 * NPAD).rearrange("p (c n) -> p c n", c=2)
        kT = carve(1, KH, 2 * NPAD).rearrange("p (c n) -> p c n", c=2)
        ob = carve(1, 128, 2 * D).rearrange("p (u d) -> p u d", u=2)
        at[1] = 0
        hT = carve(1, 128, (ZT + 1) * NPAD).rearrange("p (m n) -> p m n", m=ZT + 1)
        ohT = carve(1, 128, NPAD)
        xs = carve(1, RT, 2 * D).rearrange("p (u d) -> p u d", u=2)
        xk = carve(1, KH + 1, 2 * 2 * RT).rearrange("p (u k n) -> p u k n", u=2, k=2)
        hs = carve(1, RT, 2 * FF).rearrange("p (u f) -> p u f", u=2)
        hk = carve(1, 128, 2 * FT * RT).rearrange("p (u m n) -> p u m n", u=2, m=FT)
        ys = carve(1, RT, 2 * D).rearrange("p (u d) -> p u d", u=2)
        zeros = carve(1, RT, NRT // 2 * D)
        krot, ktmp, kq = (carve(1, TR, TT * HD).rearrange("p (t d) -> p t d", t=TT) for _ in range(3))
        order = carve(1, TR, 2 * TR)
        before, ones = order[:, 0:TR], order[:, TR:2 * TR]
        count = carve(1, TR, NE * LEVELS).rearrange("p (e l) -> p e l", e=NE)
        ntile = carve(1, TR, 3 * NE).rearrange("p (n e) -> p n e", n=3)
        below = carve(1, TR, NE * NE).rearrange("p (a b) -> p a b", a=NE)
        owner = carve(1, 1, NRT * NE).rearrange("p (t e) -> p t e", t=NRT)
        owned = carve(1, 1, NRT)
        prow = carve(1, TR, TT * NE).rearrange("p (t e) -> p t e", t=TT)
        psum_row = carve(1, TR, TT)
        zT = (hT[:, 0:ZT, :], hs.rearrange("p u f -> p (u f)")[:, 0:ZT * NPAD].rearrange("p (m n) -> p m n", m=ZT))
        rT = hT[0:KH, ZT, :]

        cst = sb("cst", [128, NKEEP])

        def const(name, parts=128):
            lo, hi = CONSTS[name]
            return cst[0:parts, lo:hi]

        ident = const("ident")
        h = sb("h", [TR, TT, D])
        a = sb("a", [TR, TT, D])
        t = sb("t", [TR, TT, D])
        xT = sb("xT", [KH, 2, NPAD])
        slT = sb("slT", [KH, 2, 2 * SLOTS])
        slots = sb("slots", [SLOTS, D])
        slsc = sb("slsc", [SLOTS, 1])
        lnv = sb("lnv", [KH, 4, 2])
        nw = sb("nw", [TR, D])
        st = sb("st", [TR, TT, 6])
        mv = sb("mv", [TR, TT, 2])
        rs = sb("rs", [TR, 8])
        ve = sb("ve", [TR, 8])
        rs2 = sb("rs2", [TR, 8])
        rs3 = sb("rs3", [TR, 8])
        m6 = sb("m6", [TR, 4, TT])
        sst = sb("sst", [SLOTS, 12])
        place = sb("place", [TR, TT], I32)
        tile_expert = sb("tile_expert", [1, NRT], I32)
        xsorted = nc.dram_tensor("xsorted", (NRT * RT, D), F32).ap()
        ysorted = nc.dram_tensor("ysorted", (NRT * RT, D), F32).ap()
        fb1 = sb("fb1", [128, 2, FF])
        fb2 = sb("fb2", [128, 2, D])

        shared = sb("shared", [128, 8288])
        used = [0]

        def share(parts, *dims):
            n = int(np.prod(dims))
            lo = used[0]
            used[0] += n
            assert used[0] <= 8288, used[0]
            v = shared[0:parts, lo:lo + n]
            names = "abcd"[:len(dims)]
            if len(dims) > 1:
                v = v.rearrange(f"p ({' '.join(names)}) -> p {' '.join(names)}", **dict(zip(names, dims)))
            return v

        posr = share(TR, D)
        addr = share(TR, D)
        wqkv0 = share(KH, 2, D + 2 * HD)
        bqkv0 = share(TR, D + 2 * HD)
        qkv = share(TR, TT, D + 2 * HD)
        s0 = share(TR, 2, TT, HEADS)
        wg0 = share(KH, 2, NE)
        bg0 = share(TR, NE)
        b2pad = share(128, D)
        w1s = share(KH, 2, KH)
        b1s = share(KH, 1)
        w2s = share(KH, NE)
        b2s = share(TR, NE)
        downb = share(128, 2, ZT)
        gamma = share(TR, D)
        beta = share(TR, D)
        wqkv1 = share(KH, 2, 3 * D)
        wpr1 = share(KH, 2, D)
        bpr1 = share(TR, D)
        temp = share(128, HEADS)
        dmask = share(128, HEADS, S)
        sc = share(128, 3, HEADS * S)
        pT = share(TR, 2, 512)
        mx = share(128, 2, HEADS)
        den = share(128, 2, HEADS)
        lg = share(TR, TT, NE)
        key = share(TR, TT, NE)
        oh = share(TR, TT + 1, NE)
        gate = share(TR, TT, NE)
        gcol = share(TR, 2, TT)
        used[0] = 0
        ycmp = share(128, 3, SLOTS // 2, B)
        dmt = share(TR, TT, IPT, SLOTS)
        comb = share(TR, TT, SLOTS)
        yg = share(128, 2, 3, QP, 32)
        hid = share(128, FF)
        hidT = share(128, FT, 2, 128)
        yslot = share(128, D)
        xe = share(TR, TT, GS, B)
        cmT = share(128, NPAD)
        mxd = share(SLOTS, 2, B)
        mxc = share(TR, 2, TT)
        disp = cmT[0:SLOTS, :]

        def load(eng, dst, src, name):
            eng.dma_start(dst, src).then_inc(sem(name), 16)

        def rowb(v, n):
            return v.unsqueeze(0).broadcast_to([n, v.shape[0]])

        w1d = w["L0_attn_W1"].rearrange("e (k p) f -> e p k f", k=2)
        w2d = w["L0_attn_W2"].rearrange("e (m p) d -> e p m d", m=FT)
        downd = w["L0_ffn_down_w"].rearrange("e (k p) f -> e p k f", k=2)
        upd = w["L0_ffn_up_w"].rearrange("e (p j) d -> e p j d", j=ZT)
        downbd = w["L0_ffn_down_b"].rearrange("e (p j) -> e p j", j=ZT)
        fc1d = w["L1_ffn_fc1_weight"].rearrange("(g q two) (p c) f -> g q (two p) (c f)", q=QP, two=2, c=3)
        fc2d = w["L1_ffn_fc2_weight"].rearrange("(g s) (p m) d -> g s p (m d)", s=GS, m=FT)
        fb1d = w["L1_ffn_fc1_bias"].rearrange("(g s) f -> g s f", s=GS)
        fb2d = w["L1_ffn_fc2_bias"].rearrange("(g s) f -> g s f", s=GS)

        N_TOK, N_ATT0, N_SMALL = 10, 6, 23

        def w1_load(sp, u, e):
            load(sp, w1r[0:KH, u], w1d[bass.ds(e, 1)].rearrange("o p k f -> p (o k) f"), f"ld_w1_{u}")
            load(sp, w1r[KH:KH + 1, u, 0], w["L0_attn_b1"][bass.ds(e, 1)], f"ld_w1_{u}")

        def w2_load(sp, u, e):
            load(sp, w2r[:, u], w2d[bass.ds(e, 1)].rearrange("o p m d -> p (o m) d"), f"ld_w2_{u}")

        def expert_of(sp, tile):
            return sp.value_load(tile_expert[0:1, bass.ds(tile, 1)], min_val=0, max_val=NE - 1)

        def down_load(sp, u, e):
            load(sp, downr[:, u], downd[e], f"ld_down_{u}")
            load(sp, downb[:, u], downbd[e], f"ld_down_{u}")

        def up_load(sp, u, e):
            load(sp, upr[:, u], upd[e], f"ld_up_{u}")

        def fc1_load(sp, u, q, g):
            load(sp, fc1[:, u, q * 3 * FF:(q + 1) * 3 * FF], fc1d[g, q], f"ld_fc1_{u}_{q}")

        def fc2_load(sp, u, q, g):
            for s in (2 * q, 2 * q + 1):
                load(sp, fc2[:, u, s * FT * D:(s + 1) * FT * D], fc2d[g, s], f"ld_fc2_{u}_{q}")

        def bias_load(sp, u, g):
            load(sp, fb1[0:GS, u], fb1d[g], f"ld_fb_{u}")
            load(sp, fb2[0:GS, u], fb2d[g], f"ld_fb_{u}")

        def replicate_v(sp):
            sp.wait_ge(sem("v_ready"), TT)
            for r in range(IPT):
                n = TT if r == 0 else TT - 1
                for g in range(IPT):
                    sp.dma_start(vrep[S * g:S * g + S, r:r + IPT * (n - 1) + 1:IPT, :],
                                 a[S * r:S * r + S, 0:n, :]).then_inc(sem("vrep"), 16)

        def gather_heads(sp):
            for j in range(B // 2):
                sp.wait_ge(sem("o_ready"), j + 1)
                for i in range(2):
                    b = 2 * j + i
                    sp.dma_start(t[S * (b % IPT):S * (b % IPT) + S, b // IPT, :],
                                 ob[64 * i:64 * i + S, j % 2, :]).then_inc(sem(f"gather{j % 2}"), 16)

        def rows_of(k):
            buf = (a, t)[k // 2 % 2][0:KH].rearrange("p x y -> p (x y)")
            return buf[:, (k % 2) * 576:(k % 2) * 576 + 576].rearrange("p (v r c) -> p v r c", v=WP, r=2)

        def emb_out(m, n):
            return xT[:, m, 0:NTOK].rearrange("p (b s) -> p b s", s=S)[:, :, 1:S]\
                .rearrange("p b (y x) -> p b y x", y=WP)[:, :, :, 3 * n:3 * n + 3]

        def emb_in(m, n):
            return ps[0:KH, 4 + 2 * m + n, 0:288].rearrange("p (x b y) -> p b y x", x=3, b=B)

        def hid_out(k, par):
            return hidT[:, 3 * k:3 * k + 3, par, :].rearrange("p m (q two b) -> p m q two b", q=QP, two=2)[:, :, :, par, :]

        def hid_in(k, par):
            return ps[:, 3 + k, 0:384].rearrange("p (m q two b) -> p m q two b", m=3, q=QP, two=2)[:, :, :, par, :]

        NORM = {n: i for i, n in enumerate(("ln1", "ln2", "ffn", "ln3", "tok"))}
        ROOT = {n: i for i, n in enumerate(("ln1", "in0", "slots", "ln2", "ffn", "u", "ln3", "tok0", "tok"))}
        VARIANCE = {n: i for i, n in enumerate(("in0", "slots", "ln2", "ffn", "u", "ln3", "tok0"))}
        VARIANCE["ln1"] = VARIANCE["in0"]
        TURN = {n: i for i, n in enumerate(("ln1", "ln2", "ffn", "ln3", "proj", "tok"))}
        PAIRS = B // 2

        block = ctx.enter_context(nc.Block())

        @block.sync
        def _(sp):
            load(sp, cst[:, :], consts[:, 0:NKEEP], "ld_cst")
            xd = w["x"].rearrange("b (v r) x c -> (b v) r (x c)", v=WP)
            for k in range(4):
                load(sp, xin[:, 4 * k:4 * k + 4].rearrange("p r v c -> p r (v c)"), xd[:, 4 * k:4 * k + 4], f"ld_x{k}")
                if k == 0:
                    load(sp, wproj[:], w["L0_tok_W_proj"].rearrange("(k p) d -> p k d", p=KH), "ld_wproj")
            for r in range(IPT):
                load(sp, posr[S * r:S * r + S], w["L0_tok_pos_embedding"], "ld_tok")
                load(sp, addr[S * r + 1:S * r + S], rowb(w["L0_tok_b_proj"], S - 1), "ld_tok")
                load(sp, addr[S * r:S * r + 1], w["L0_tok_cls_token"].rearrange("a b d -> (a b) d"), "ld_tok")
            for n, (lo, hi) in zip("qkv", ((0, D), (D, D + HD), (D + HD, D + 2 * HD))):
                load(sp, wqkv0[:, :, lo:hi], w[f"L0_attn_W{n}"].rearrange("(k p) n -> p k n", k=2), "ld_att0")
                load(sp, bqkv0[:, lo:hi], rowb(w[f"L0_attn_b{n}"], TR), "ld_att0")
            for i, n in enumerate(("ln1_g", "ln1_b", "ln2_g", "ln2_b")):
                for k in range(2):
                    load(sp, lnv[:, i, k:k + 1], w[f"L0_attn_{n}"][KH * k:KH * k + KH].unsqueeze(1), "ld_small")
            for dst, src in (
                (wg0[:], w["L0_attn_Wg"].rearrange("(k p) n -> p k n", k=2)),
                (bg0[:], rowb(w["L0_attn_bg"], TR)),
                (w1s[:], w["L0_ffn_w1"].rearrange("(k p) n -> p k n", k=2)),
                (b1s[:], w["L0_ffn_b1"].unsqueeze(1)),
                (w2s[:], w["L0_ffn_w2"]),
                (b2s[:], rowb(w["L0_ffn_b2"], TR)),
                (gamma[:], rowb(w["L0_ffn_gamma"], TR)),
                (beta[:], rowb(w["L0_ffn_beta"], TR)),
                (wqkv1[:], w["L1_attn_w_qkv"].rearrange("(k p) n -> p k n", k=2)),
                (wpr1[:], w["L1_attn_w_proj"].rearrange("(k p) n -> p k n", k=2)),
                (bpr1[:], rowb(w["L1_attn_b_proj"], TR)),
                (temp[:], rowb(w["L1_attn_temperature"].rearrange("h a b -> (h a b)"), 128)),
                (nw[:], rowb(w["L1_ffn_norm_weight"], TR)),
                (slots[:], w["L1_ffn_slots"]),
                (slsc[:], w["L1_ffn_scale"].unsqueeze(1)),
            ):
                load(sp, dst, src, "ld_small")
            sp.wait_ge(sem("pads_zero"), 1)
            load(sp, b2pad[0:NE], w["L0_attn_b2"], "ld_b2")
            sp.wait_ge(sem("zeros"), 1)
            load(sp, order, consts[0:TR, NKEEP:], "ld_order")
            for u in range(2):
                load(sp, xsorted[u * NRT // 2 * RT:(u + 1) * NRT // 2 * RT].rearrange("(k p) d -> p k d", p=RT),
                     zeros.rearrange("p (k d) -> p k d", d=D), f"st_sorted_{u}")
            for u in range(2):
                down_load(sp, u, u)
                up_load(sp, u, u)
            for u in range(2):
                bias_load(sp, u, u)
            for q in range(QP):
                fc1_load(sp, 0, q, 0)
            for q in range(QP):
                fc2_load(sp, 0, q, 0)

            sp.wait_ge(sem("tile_expert"), 1)
            for u in range(2):
                e = expert_of(sp, u)
                w1_load(sp, u, e)
                w2_load(sp, u, e)
            sp.wait_ge(sem("scattered"), 16 * TT)
            for u in range(2):
                load(sp, xs[:, u], xsorted[u * RT:u * RT + RT], f"ld_xs_{u}")
            with sp.Fori(0, NRT // 2 - 1) as p:
                ex = [expert_of(sp, p * 2 + (u + 2)) for u in range(2)]
                for u in range(2):
                    sp.wait_ge(sem("x_tp"), p * 2 + (u + 1))
                    load(sp, xs[:, u], xsorted[bass.ds((p * 2 + (u + 2)) * RT, RT)], f"ld_xs_{u}")
                for u in range(2):
                    sp.wait_ge(sem("up_mm"), p * 4 + (2 * u + 2))
                    w1_load(sp, u, ex[u])
                for u in range(2):
                    sp.wait_ge(sem("y_out"), p * 2 + (u + 3))
                    w2_load(sp, u, ex[u])
                    load(sp, ysorted[bass.ds((p * 2 + u) * RT, RT)], ys[:, u], f"st_sorted_{u}")
            for u in range(2):
                sp.wait_ge(sem("y_out"), NRT + u + 1)
                load(sp, ysorted[(NRT - 2 + u) * RT:(NRT - 1 + u) * RT], ys[:, u], f"st_sorted_{u}")

            with sp.Fori(0, NE // 2 - 1) as e2:
                for u in range(2):
                    e = e2 * 2 + u
                    sp.wait_ge(sem("ffn_z"), e * 4 + 4)
                    down_load(sp, u, e + 2)
                    sp.wait_ge(sem("ffn_y_mm"), e * TT + TT)
                    up_load(sp, u, e + 2)

            sp.wait_ge(sem("ffn_y_mm"), TT * NE)
            for q in range(QP):
                fc1_load(sp, 1, q, 1)
            replicate_v(sp)
            gather_heads(sp)
            for u in range(2):
                sp.wait_ge(sem(f"gather{u}"), 16 * PAIRS)
            for q in range(QP):
                fc2_load(sp, 1, q, 1)

            with sp.Fori(0, NG // 2 - 1) as g2:
                for u in range(2):
                    g = g2 * 2 + u
                    sp.wait_ge(sem("fc1_used"), g + 2)
                    bias_wait = sem("fc2_used")
                    for q in range(QP):
                        fc1_load(sp, u, q, g + 2)
                    sp.wait_ge(bias_wait, g + 1)
                    bias_load(sp, u, g + 2)
                    for q in range(QP):
                        fc2_load(sp, u, q, g + 2)

            sp.wait_ge(sem("out_ready"), 1)
            full = (TT - 1) * TR
            rows = out.rearrange("b s d -> (b s) d")
            load(sp, rows[0:full].rearrange("(t p) d -> p t d", p=TR), h[:, 0:TT - 1, :], "stored")
            load(sp, rows[full:NTOK], h[0:LAST, TT - 1, :], "stored")
            sp.wait_ge(sem("stored"), 32)

        def embed(pe, mm, k):
            for v in range(2):
                pe.wait_ge(sem(f"patches_copied{v}"), k + 1)
            for m in range(2):
                for n in range(2):
                    ins = mm(ps[0:KH, 4 + 2 * m + n, 0:288], wproj[:, k, KH * m:KH * m + KH],
                             patT[:, k, 288 * n:288 * n + 288], k == 0, k == KT - 1)
                    if k == KT - 1:
                        ins.then_inc(sem("emb_mm"), 1)

        @block.tensor
        def _(pe):
            idn = ident

            def mm(o, l, r, start=True, stop=True, **k):
                return pe.matmul(o, l, r, start=start, stop=stop, **k)

            def to_features(name, src):
                for j in range(TT // 2):
                    for i in range(2):
                        tt = 2 * j + i
                        pe.wait_ge(sem("rows"), TT * NORM[name] + tt + 1)
                        for c in range(2):
                            ins = pe.transpose(ps[0:KH, j, 256 * c + TR * i:256 * c + TR * i + TR],
                                               src[:, tt, KH * c:KH * c + KH], idn[0:TR, 0:TR])
                    ins.then_inc(sem("tp"), 1)

            def attention():
                def scores(j):
                    pe.wait_ge(sem("kblk"), j + 1)
                    if j >= 3:
                        pe.wait_ge(sem("s_read"), j - 2)
                    for c in range(2):
                        for i in range(2):
                            b = 2 * j + i
                            ins = mm(ps[64 * i:64 * i + 64, j % 3, HW * c:HW * c + HW],
                                     qT[:, c, S * b:S * b + 64], kblk[:, j % 2, c, i, :])
                    ins.then_inc(sem("s_mm"), 1)

                def transposes(j):
                    pe.wait_ge(sem("exp"), j + 1)
                    if j >= 2:
                        pe.wait_ge(sem("pT"), j - 1)
                    for g in range(4):
                        ins = pe.transpose(ps[0:TR, 3 + j % 2, 128 * g:128 * g + 128],
                                           sc[:, j % 3, TR * g:TR * g + TR], idn)
                    ins.then_inc(sem("pT_mm"), 1)

                def outputs(j):
                    pe.wait_ge(sem("pT"), j + 1)
                    pe.wait_ge(sem("vblk"), j + 1)
                    if j >= 2:
                        pe.wait_ge(sem("o_ready"), j - 1)
                    for g in range(4):
                        for i in range(2):
                            n = (64, S)[i]
                            ins = mm(ps[64 * i:64 * i + n, 5 + j % 2, 51 * g:51 * g + 51],
                                     pT[:, j % 2, 128 * g + 64 * i:128 * g + 64 * i + n],
                                     vblk[:, j % 2, 4 * i + g, :])
                    ins.then_inc(sem("o_mm"), 1)

                scores(0)
                scores(1)
                for j in range(PAIRS + 1):
                    if j + 2 < PAIRS:
                        scores(j + 2)
                    if j < PAIRS:
                        transposes(j)
                    if j >= 1:
                        outputs(j - 1)

            pe.wait_ge(sem("ld_cst"), 16)
            pe.wait_ge(sem("ld_wproj"), 16)
            for k in range(KT):
                for v in range(2):
                    n = 2 * k + v
                    pe.wait_ge(sem(f"patches_rows{k % 2}"), k // 2 + 1)
                    if n >= 4:
                        pe.wait_ge(sem(f"patches_copied{v}"), k - 1)
                    for i in range(3):
                        wp = 3 * v + i
                        ins = pe.transpose(ps[0:KH, n % 4, KH * i:KH * i + KH],
                                           (a, t)[k // 2 % 2][0:KH].rearrange("p x y -> p (x y)")[
                                               :, (k % 2) * 576 + KH * wp:(k % 2) * 576 + KH * wp + KH],
                                           idn[0:KH, 0:KH])
                    ins.then_inc(sem("patches_tp"), 1)
                if k >= 1:
                    embed(pe, mm, k - 1)
            embed(pe, mm, KT - 1)
            pe.wait_ge(sem("emb_cols"), 4)
            for j in range(TT // 2):
                for i in range(2):
                    for c in range(2):
                        ins = pe.transpose(ps[0:TR, j, D * i + KH * c:D * i + KH * c + KH],
                                           xT[:, c, TR * (2 * j + i):TR * (2 * j + i) + TR], idn[0:KH, 0:KH])
                ins.then_inc(sem("emb_tp"), 1)

            to_features("ln1", t)
            pe.wait_ge(sem("cols"), 3 * TURN["ln1"] + 3)
            pe.wait_ge(sem("ld_att0"), 16 * N_ATT0)
            W3 = D + 2 * HD
            for tt in range(TT):
                for k in range(2):
                    ins = mm(ps[0:TR, 3 + tt // 2, W3 * (tt % 2):W3 * (tt % 2) + W3],
                             xT[:, k, TR * tt:TR * tt + TR], wqkv0[:, k, :], k == 0, k == 1)
                if tt % 2:
                    ins.then_inc(sem("qkv0_mm"), 1)

            pe.wait_ge(sem("slots_rows"), 1)
            for c in range(2):
                ins = pe.transpose(ps[0:KH, 7, SLOTS * c:SLOTS * c + SLOTS], slots[:, KH * c:KH * c + KH],
                                   idn[0:SLOTS, 0:SLOTS])
            ins.then_inc(sem("slots_tp"), 1)

            to_features("ln2", t)
            pe.wait_ge(sem("cols"), 3 * TURN["ln2"] + 3)
            for tt in range(TT):
                for k in range(2):
                    ins = mm(ps[0:TR, 6, NE * tt:NE * tt + NE], xT[:, k, TR * tt:TR * tt + TR], wg0[:, k, :],
                             k == 0, k == 1)
            ins.then_inc(sem("gate_mm"), 1)
            pe.wait_ge(sem("ld_order"), 16)
            pe.wait_ge(sem("onehot"), 1)
            mm(ps[0:TR, 5, 0:(TT + 1) * NE], before, oh[:].rearrange("p t e -> p (t e)"), True, False,
               skip_group_check=True)
            for tt in range(TT):
                ins = mm(ps[0:TR, 5, (tt + 1) * NE:(TT + 1) * NE], ones, bcast(oh[:, tt, :], 1, TT - tt),
                         False, tt == TT - 1, skip_group_check=True)
            ins.then_inc(sem("count_mm"), 1)
            for tt in range(TT):
                ins = pe.transpose(ps[0:NE, 7 if tt < 4 else 3, TR * (tt % 4):TR * (tt % 4) + TR], oh[:, tt, :],
                                   idn[0:TR, 0:TR])
            ins.then_inc(sem("ohT_tp"), 1)
            pe.wait_ge(sem("ohT"), 2)
            pe.wait_ge(sem("ld_b2"), 16)
            for tt in range(TT):
                ins = mm(ps[0:TR, tt // 2, D * (tt % 2):D * (tt % 2) + D], ohT[:, TR * tt:TR * tt + TR], b2pad[:])
            ins.then_inc(sem("b2_mm"), 1)

            def x_transposes(u):
                for k in range(2):
                    ins = pe.transpose(ps[0:KH, 2 * u + 1, RT * k:RT * k + RT], xs[:, u, KH * k:KH * k + KH], idn)
                ins.then_inc(sem("x_tp"), 1)

            def tile_pair(p, last):
                for u in range(2):
                    pe.wait_ge(sem(f"ld_w1_{u}"), p * 32 + 32)
                    pe.wait_ge(sem("xk"), p * 2 + (u + 1))
                    pe.wait_ge(sem("y_out"), p * 2 + (u + 1))
                    for n in range(2):
                        for k in range(2):
                            rows = KH + 1 - k
                            ins = mm(ps[:, 2 * u + n, 0:384], xk[0:rows, u, k, :],
                                     w1r[0:rows, u, k, 384 * n:384 * n + 384], k == 0, k == 1)
                        ins.then_inc(sem("up_mm"), 1)
                for u in range(2):
                    for n in range(2):
                        pe.wait_ge(sem("gelu"), p * 4 + (2 * u + n + 1))
                        for m in range(3):
                            ins = pe.transpose(ps[:, 4 + 2 * u + n, 128 * m:128 * m + 128],
                                               hs[:, u, 384 * n + 128 * m:384 * n + 128 * m + 128], idn)
                        ins.then_inc(sem("h_tp"), 1)
                    if not last:
                        pe.wait_ge(sem(f"ld_xs_{u}"), p * 16 + 32)
                        x_transposes(u)
                for u in range(2):
                    pe.wait_ge(sem(f"ld_w2_{u}"), p * 16 + 16)
                    pe.wait_ge(sem("hk0"), p * 2 + (u + 1))
                    pe.wait_ge(sem("hk1"), p * 2 + (u + 1))
                    for m in range(FT):
                        ins = mm(ps[:, 2 * u, 0:D], hk[:, u, m, :], w2r[:, u, m, :], m == 0, m == FT - 1)
                    ins.then_inc(sem("y_mm1"), 1)

            pe.wait_ge(sem("y_out"), 2)
            for u in range(2):
                pe.wait_ge(sem(f"ld_xs_{u}"), 16)
                x_transposes(u)
            with pe.Fori(0, NRT // 2 - 1) as p:
                tile_pair(p, False)
            tile_pair(NRT // 2 - 1, True)

            to_features("ffn", a)
            pe.wait_ge(sem("cols"), 3 * TURN["ffn"] + 3)
            for n in range(2):
                for k in range(2):
                    ins = mm(ps[0:KH, 6 + n, 0:NH], w1s[:, k, :], xT[:, k, NH * n:NH * n + NH], k == 0, k == 1)
            ins.then_inc(sem("router_mm"), 1)
            pe.wait_ge(sem("router_h"), 2)
            for tt in range(TT):
                ins = mm(ps[0:TR, 6, NE * tt:NE * tt + NE], rT[:, TR * tt:TR * tt + TR], w2s[:])
            ins.then_inc(sem("logits_mm"), 1)

            def hidden(u, e2, after):
                pe.wait_ge(sem(f"ld_down_{u}"), e2 * 32 + 32)
                if after is not None:
                    pe.wait_ge(sem("ffn_z"), after)
                for j in range(ZT):
                    for n in range(2):
                        for k in range(2):
                            ins = mm(ps[:, 2 * j + n, 0:NH], downr[:, u, k, j:DZ:ZT], xT[:, k, NH * n:NH * n + NH],
                                     k == 0, k == 1)
                        ins.then_inc(sem("ffn_z_mm"), 1)

            def expert_pair(e2, last):
                for u in range(2):
                    e = e2 * 2 + u
                    if not (last and u):
                        hidden(1 - u, e2 + u, e * 4 + 4)
                    pe.wait_ge(sem("ffn_z"), e * 4 + 4)
                    pe.wait_ge(sem(f"ld_up_{u}"), e2 * 16 + 16)
                    for tt in range(TT):
                        if tt >= 2:
                            pe.wait_ge(sem("ffn_y"), e * TT + tt)
                        else:
                            pe.wait_ge(sem("ffn_y"), e * TT + 1)
                        for j in range(ZT):
                            ins = mm(ps[0:TR, 4 + tt % 2, 0:D], zT[u][:, j, TR * tt:TR * tt + TR], upr[:, u, j, :],
                                     j == 0, j == ZT - 1)
                        ins.then_inc(sem("ffn_y_mm"), 1)

            hidden(0, 0, None)
            with pe.Fori(0, NE // 2 - 1) as e2:
                expert_pair(e2, False)
            expert_pair(NE // 2 - 1, True)

            to_features("ln3", t)
            pe.wait_ge(sem("cols"), 3 * TURN["ln3"] + 3)
            for tt in range(TT):
                for k in range(2):
                    ins = mm(ps[0:TR, 4 + tt // 2, D * (tt % 2):D * (tt % 2) + D], xT[:, k, TR * tt:TR * tt + TR],
                             wqkv1[:, k, 2 * D:3 * D], k == 0, k == 1)
                if tt % 2:
                    ins.then_inc(sem("v1_mm"), 1)
            for m in range(4):
                for n in range(2):
                    q = 2 * m + n
                    if q >= 4:
                        pe.wait_ge(sem("qk1"), q - 3)
                    for k in range(2):
                        ins = mm(ps[0:KH, q % 4, 0:NH], wqkv1[:, k, KH * m:KH * m + KH],
                                 xT[:, k, NH * n:NH * n + NH], k == 0, k == 1)
                    ins.then_inc(sem("qk1_mm"), 1)
            pe.wait_ge(sem("qk1"), 8)
            pe.wait_ge(sem("v_ready"), TT)
            attention()
            for u in range(2):
                pe.wait_ge(sem(f"gather{u}"), 16 * PAIRS)
            for j in range(TT // 2):
                for i in range(2):
                    for c in range(2):
                        ins = pe.transpose(ps[0:KH, j, 256 * c + TR * i:256 * c + TR * i + TR],
                                           t[:, 2 * j + i, KH * c:KH * c + KH], idn[0:TR, 0:TR])
                ins.then_inc(sem("tp"), 1)
            pe.wait_ge(sem("cols"), 3 * TURN["proj"] + 3)
            for tt in range(TT):
                for k in range(2):
                    ins = mm(ps[0:TR, 5 + tt // 2, D * (tt % 2):D * (tt % 2) + D], xT[:, k, TR * tt:TR * tt + TR],
                             wpr1[:, k, :], k == 0, k == 1)
                if tt % 2:
                    ins.then_inc(sem("proj_mm"), 1)

            to_features("tok", t)
            pe.wait_ge(sem("cols"), 3 * TURN["tok"] + 3)
            pe.wait_ge(sem("slT"), 1)
            for n in range(2):
                for k in range(2):
                    ins = mm(ps[:, 4 + n, 0:NH], slT[:, k, :], xT[:, k, NH * n:NH * n + NH], k == 0, k == 1)
                ins.then_inc(sem("disp_mm"), 1)
            pe.wait_ge(sem("logits"), 2)
            for tt in range(TT):
                ins = pe.transpose(ps[0:TR, 3, SLOTS * tt:SLOTS * tt + SLOTS], hid[0:SLOTS, TR * tt:TR * tt + TR],
                                   idn[0:SLOTS, 0:SLOTS])
            ins.then_inc(sem("comb_mm"), 1)
            pe.wait_ge(sem("disp"), 1)
            for tt in range(TT):
                ins = pe.transpose(ps[0:TR, 6, SLOTS * tt:SLOTS * tt + SLOTS], disp[:, TR * tt:TR * tt + TR],
                                   idn[0:SLOTS, 0:SLOTS])
            ins.then_inc(sem("disp_tp"), 1)
            pe.wait_ge(sem("dm"), 1)
            for c in range(3):
                for tt in range(TT):
                    n = IPT if tt < TT - 1 else 1
                    for par in range(2):
                        ins = mm(ps[64 * par:64 * par + 64, c, 96 * tt:96 * tt + 32 * n],
                                 a[:, tt, c:D:3], dmt[:, tt, 0:n, par:SLOTS:2])
                ins.then_inc(sem("y_mm"), 1)
            pe.wait_ge(sem("y_copied"), 6)
            for j in range(3):
                ins = mm(ps[0:TR, 5 + j, 0:2 * D], idn[0:TR, 0:TR],
                         h[:, 2 * j:2 * j + 2, :].rearrange("p a b -> p (a b)"), True, False, skip_group_check=True)
                if j < 2:
                    ins.then_inc(sem(("cm_tp", "fc1_used")[j]), 1)
            sel = const("sel")
            with pe.Fori(0, NG // 2) as g2:
                for u in range(2):
                    g = g2 * 2 + u
                    pe.wait_ge(sem(f"ld_fb_{u}"), g2 * 32 + 32)
                    for n in range(2):
                        mm(ps[:, n, 0:384], sel, fb1[:, u, 384 * n:384 * n + 384], True, False, skip_group_check=True)
                    pe.wait_ge(sem("yg"), g + 1)
                    for q in range(QP):
                        pe.wait_ge(sem(f"ld_fc1_{u}_{q}"), g2 * 16 + 16)
                    for c in range(3):
                        for n in range(2):
                            for q in range(QP):
                                ins = mm(ps[32 * q:32 * q + 32, n, 0:384], yg[:, u, c, q, :],
                                         fc1v[:, u, q, c, 384 * n:384 * n + 384], False, c == 2,
                                         skip_group_check=True)
                    ins.then_inc(sem("fc1_used"), 1)
                    pe.wait_ge(sem("xe"), g + 1)
                    for tt in range(TT):
                        ins = pe.transpose(ps[:, 3 + tt // 3, TR * (tt % 3):TR * (tt % 3) + TR],
                                           xe[:, tt].rearrange("p s b -> p (s b)"), idn[0:TR, 0:TR])
                    ins.then_inc(sem("cm_tp"), 1)
                    pe.wait_ge(sem("hid"), g * 2 + 2)
                    pe.wait_ge(sem("cmT"), g * 2 + 2)
                    for m in range(FT):
                        ins = pe.transpose(ps[:, 3 + m // 3, 128 * (m % 3):128 * (m % 3) + 128], hid[:, m:FF:FT], idn)
                        if m % 3 == 2:
                            ins.then_inc(sem("hidT_tp"), 1)
                    mm(ps[:, 2, 0:D], sel, fb2[:, u], True, False, skip_group_check=True)
                    pe.wait_ge(sem("hidT"), g * 4 + 4)
                    for q in range(QP):
                        pe.wait_ge(sem(f"ld_fc2_{u}_{q}"), g2 * 32 + 32)
                    for m in range(FT):
                        for par in range(2):
                            for q in range(QP):
                                ins = mm(ps[32 * q:32 * q + 32, 2, 0:D], hidT[:, m, par, 32 * q:32 * q + 32],
                                         fc2v[:, u, 2 * q + par, m, :], False, m == FT - 1 and par == 1,
                                         skip_group_check=True)
                    ins.then_inc(sem("fc2_used"), 1)
                    pe.wait_ge(sem("yslot"), g + 1)
                    for tt in range(TT):
                        ins = mm(ps[0:TR, 5 + tt // 2, D * (tt % 2):D * (tt % 2) + D], cmT[:, TR * tt:TR * tt + TR],
                                 yslot[:], False, False, skip_group_check=True)
                    ins.then_inc(sem("combined"), 1)

        class Steps:

            def __init__(self, eng, name):
                self.eng, self.sem, self.n = eng, sem(name), 0

            def __call__(self, ins):
                self.n += 1
                ins.then_inc(self.sem, 1)
                self.eng.wait_ge(self.sem, self.n)

        @block.vector
        def _(dve):
            step = Steps(dve, "dve_step")

            def stats(src, done=False):
                if not done:
                    for tt in range(TT):
                        ins = dve.bn_stats(st[:, tt, :], src[:, tt, :])
                    step(ins)
                for tt in range(TT):
                    ins = dve.bn_aggr(mv[:, tt, :], st[:, tt, :])
                return ins

            def normalise(name, src, dst, done=False):
                stats(src, done).then_inc(sem("var"), 1)
                dve.wait_ge(sem("rstd"), ROOT[name] + 1)
                for tt in range(TT):
                    dve.tensor_scalar(dst[:, tt, :], src[:, tt, :], mv[:, tt, 0:1], rs[:, tt:tt + 1],
                                      ALU.subtract, ALU.mult).then_inc(sem("rows"), 1)
                dve.wait_ge(sem("rows"), TT * NORM[name] + TT)

            def attention():
                def before(j):
                    dve.wait_ge(sem("s_mm"), j + 1)
                    v = ps[:, j % 3, 0:HEADS * S].rearrange("p (h n) -> p h n", h=HEADS)
                    o = sc[:, j % 3, :].rearrange("p (h n) -> p h n", h=HEADS)
                    if j >= 3:
                        dve.wait_ge(sem("pT_mm"), j - 2)
                    dve.tensor_tensor(o, v, dmask[:], ALU.mult).then_inc(sem("s_read"), 1)
                    dve.wait_ge(sem("s_read"), j + 1)
                    step(dve.tensor_reduce(mx[:, j % 2, :], o, X, ALU.max))
                    dve.tensor_tensor(o, o, bcast(mx[:, j % 2, :], 2, S), ALU.subtract).then_inc(sem("s_sub"), 1)

                def after(j):
                    dve.wait_ge(sem("o_mm"), j + 1)
                    v = ps[0:101, 5 + j % 2, 0:204].rearrange("p (h d) -> p h d", h=HEADS)
                    step(dve.reciprocal(den[0:101, j % 2, :], v[:, :, HD:HD + 1].rearrange("p h o -> p (h o)")))
                    if j >= 2:
                        dve.wait_ge(sem(f"gather{j % 2}"), 32 * (j // 2))
                    dve.tensor_tensor(ob[0:101, j % 2, :].rearrange("p (h d) -> p h d", h=HEADS), v[:, :, 0:HD],
                                      bcast(den[0:101, j % 2, :], 2, HD), ALU.mult).then_inc(sem("o_ready"), 1)

                before(0)
                before(1)
                for j in range(PAIRS + 1):
                    if j + 2 < PAIRS:
                        before(j + 2)
                    if j >= 1:
                        after(j - 1)
                for u in range(2):
                    dve.wait_ge(sem(f"gather{u}"), 16 * PAIRS)

            oh1 = oh[:, 0:TT, :]

            def first_max(src, mask):
                step(dve.tensor_reduce(m6[:, 0, :], src[:], X, ALU.max))
                step(dve.tensor_tensor(mask, src[:], bcast(m6[:, 0, :], 2, NE), ALU.is_equal))
                step(dve.tensor_tensor(key[:], mask, bcast(const("rev", TR), 1, TT), ALU.mult))
                step(dve.tensor_reduce(m6[:, 0, :], key[:], X, ALU.max))
                step(dve.tensor_tensor(mask, key[:], bcast(m6[:, 0, :], 2, NE), ALU.is_equal))

            for k in range(0, KT, 2):
                dve.wait_ge(sem(f"ld_x{k // 2}"), 16)
                if k >= 4:
                    dve.wait_ge(sem("patches_tp"), 2 * (k - 4) + 2)
                dve.tensor_copy(rows_of(k), xin[:, 2 * k:2 * k + 2].rearrange("p r v c -> p v r c"))\
                    .then_inc(sem("patches_rows0"), 1)
                for kk in (k, k + 1):
                    dve.wait_ge(sem("patches_tp"), 2 * kk + 1)
                    dve.tensor_copy(patT[:, kk, 0:288], ps[0:KH, (2 * kk) % 4, 0:288])\
                        .then_inc(sem("patches_copied0"), 1)
            dve.wait_ge(sem("ld_tok"), 16 * 9)
            step(dve.tensor_tensor(posr[:], posr[:], addr[:], ALU.add))
            dve.wait_ge(sem("emb_mm"), 2)
            dve.wait_ge(sem("pads_zero"), 1)
            for n in range(2):
                dve.tensor_copy(emb_out(0, n), emb_in(0, n)).then_inc(sem("emb_cols"), 1)
            for j in range(TT // 2):
                dve.wait_ge(sem("emb_tp"), j + 1)
                ins = dve.tensor_tensor(h[:, 2 * j:2 * j + 2, :],
                                        ps[0:TR, j, 0:2 * D].rearrange("p (i d) -> p i d", i=2),
                                        bcast(posr[:], 1, 2), ALU.add)
            step(ins)
            stats(h).then_inc(sem("var"), 1)
            dve.wait_ge(sem("var"), VARIANCE["in0"] + 1)
            dve.wait_ge(sem("rstd"), ROOT["ln1"] + 1)
            for tt in range(TT):
                dve.tensor_scalar(t[:, tt, :], h[:, tt, :], mv[:, tt, 0:1], rs2[:, tt:tt + 1],
                                  ALU.subtract, ALU.mult).then_inc(sem("rows"), 1)
            dve.wait_ge(sem("rstd"), ROOT["in0"] + 1)
            for tt in range(TT):
                dve.tensor_scalar(a[:, tt, :], h[:, tt, :], mv[:, tt, 0:1], rs[:, tt:tt + 1],
                                  ALU.subtract, ALU.mult)
            dve.wait_ge(sem("ld_small"), 16 * N_SMALL)
            step(dve.bn_stats(sst[:, 0:6], slots[:]))
            step(dve.bn_aggr(sst[:, 6:8], sst[:, 0:6]))
            step(dve.tensor_tensor(sst[:, 8:9], sst[:, 6:7], sst[:, 6:7], ALU.mult))
            dve.tensor_tensor(sst[:, 9:10], sst[:, 8:9], sst[:, 7:8], ALU.add).then_inc(sem("var"), 1)
            step(dve.tensor_tensor(dmask[:], bcast(const("eye"), 1, HEADS), bcast(temp[:], 2, S), ALU.mult))
            step(dve.tensor_scalar(dmask[:], dmask[:], -1.0, 1.0, ALU.mult, ALU.add))
            for j in range(TT // 2):
                dve.wait_ge(sem("qkv0_mm"), j + 1)
                if j == 0:
                    dve.wait_ge(sem("ld_att0"), 16 * N_ATT0)
                dve.tensor_tensor(qkv[:, 2 * j:2 * j + 2, :],
                                  ps[0:TR, 3 + j, 0:448].rearrange("p (i d) -> p i d", i=2),
                                  bcast(bqkv0[:], 1, 2), ALU.add).then_inc(sem("qkv0"), 1)
            dve.wait_ge(sem("qkv0"), TT // 2)

            def heads(ap, n):
                return ap.rearrange("p t (h e) -> p t h e", h=n)

            half = HD // 2

            def table(name, lo, hi):
                return bcast(const(name, TR)[:, lo:hi], 1, TT)

            k0 = qkv[:, :, D:D + HD]
            dve.tensor_tensor(krot, k0, table("cos", 0, HD), ALU.mult)
            dve.tensor_tensor(ktmp[:, :, 0:half], k0[:, :, half:HD], table("sin", 0, half), ALU.mult)
            step(dve.tensor_tensor(ktmp[:, :, half:HD], k0[:, :, 0:half], table("sin", half, HD), ALU.mult))
            step(dve.tensor_tensor(krot, krot, ktmp, ALU.add))
            dve.tensor_tensor(kq, krot, table("cos", 0, HD), ALU.mult)
            step(dve.tensor_tensor(ktmp, krot, table("sin", 0, HD), ALU.mult))
            dve.tensor_tensor(kq[:, :, 0:half], kq[:, :, 0:half], ktmp[:, :, half:HD], ALU.add)
            step(dve.tensor_tensor(kq[:, :, half:HD], kq[:, :, half:HD], ktmp[:, :, 0:half], ALU.add))
            q4 = heads(t[:], HEADS)
            step(dve.tensor_tensor(q4, heads(qkv[:, :, 0:D], HEADS), bcast(kq, 2, HEADS), ALU.mult))
            step(dve.tensor_reduce(s0[:, 0], q4, X, ALU.add))
            step(dve.tensor_tensor(s0[:, 1], s0[:, 0], s0[:, 0], ALU.max))
            dve.tensor_tensor(s0[:, 0], s0[:, 0], s0[:, 1], ALU.subtract).then_inc(sem("s0_sub"), 1)
            dve.wait_ge(sem("s0_exp"), 1)
            step(dve.tensor_scalar(s0[:, 1], s0[:, 0], float(HEADS), None, ALU.mult))
            step(dve.reciprocal(s0[:, 1], s0[:, 1]))
            step(dve.scalar_tensor_tensor(out=s0[:, 0], in0=s0[:, 0], scalar=float(HEADS), in1=s0[:, 1],
                                          op0=ALU.mult, op1=ALU.mult))
            step(dve.tensor_tensor(q4, bcast(s0[:, 0], 3, HD), bcast(qkv[:, :, D + HD:D + 2 * HD], 2, HEADS), ALU.mult))
            step(dve.tensor_tensor(a[:], a[:], t[:], ALU.add))

            normalise("ln2", a, t)
            dve.wait_ge(sem("rstd"), ROOT["slots"] + 1)
            dve.tensor_scalar(slots[:], slots[:], sst[:, 10:11], slsc[:, 0:1], ALU.mult, ALU.mult)\
                .then_inc(sem("slots_rows"), 1)
            dve.wait_ge(sem("slots_tp"), 1)
            for i in range(2):
                ins = dve.tensor_copy(slT[:, :, SLOTS * i:SLOTS * i + SLOTS],
                                      ps[0:KH, 7, 0:2 * SLOTS].rearrange("p (c n) -> p c n", c=2))
            ins.then_inc(sem("slT"), 1)

            dve.wait_ge(sem("gate_mm"), 1)
            step(dve.tensor_tensor(lg[:], ps[0:TR, 6, 0:TT * NE].rearrange("p (t e) -> p t e", t=TT),
                                   bcast(bg0[:], 1, TT), ALU.add))
            first_max(lg, oh1)
            dve.tensor_scalar(oh[:, TT - 1, :], oh[:, TT - 1, :], const("valid", TR), None, ALU.mult)\
                .then_inc(sem("onehot"), 1)
            dve.wait_ge(sem("count_mm"), 1)
            total = ps[0:TR, 5, TT * NE:(TT + 1) * NE]
            step(dve.tensor_tensor(count, bcast(total, 2, LEVELS), bcast(const("level", TR), 1, NE), ALU.is_gt))
            step(dve.tensor_reduce(ntile[:, 0, :], count, X, ALU.add))
            step(dve.tensor_tensor(below, bcast(ntile[:, 0, :], 1, NE),
                                   const("lower", TR).rearrange("p (a b) -> p a b", a=NE), ALU.mult))
            step(dve.tensor_reduce(ntile[:, 1, :], below, X, ALU.add))
            dve.tensor_tensor(ntile[:, 2, :], ntile[:, 0, :], ntile[:, 1, :], ALU.add)
            step(dve.scalar_tensor_tensor(out=prow, in0=bcast(ntile[:, 1, :], 1, TT), scalar=float(RT),
                                          in1=ps[0:TR, 5, 0:TT * NE].rearrange("p (t e) -> p t e", t=TT),
                                          op0=ALU.mult, op1=ALU.add))
            dve.tensor_tensor(owner, bcast(const("tile", 1), 2, NE), bcast(ntile[0:1, 2, :], 1, NRT), ALU.is_ge)
            step(dve.tensor_tensor(prow, prow, oh1, ALU.mult))
            dve.tensor_reduce(owned, owner, X, ALU.add)
            step(dve.tensor_reduce(psum_row, prow, X, ALU.add))
            dve.tensor_copy(place[:], psum_row).then_inc(sem("place"), 1)
            dve.tensor_scalar(tile_expert[:], owned, float(NE - 1), None, ALU.min)\
                .then_inc(sem("tile_expert"), 1)
            dve.wait_ge(sem("ohT_tp"), 1)
            dve.wait_ge(sem("h_pads"), 1)
            dve.tensor_copy(ohT[0:NE, 0:4 * TR], ps[0:NE, 7, 0:4 * TR]).then_inc(sem("ohT"), 1)
            dve.tensor_copy(ohT[0:NE, 4 * TR:NPAD], ps[0:NE, 3, 0:2 * TR]).then_inc(sem("ohT"), 1)
            dve.wait_ge(sem("b2_mm"), 1)
            for j in range(TT // 2):
                ins = dve.tensor_tensor(a[:, 2 * j:2 * j + 2, :], a[:, 2 * j:2 * j + 2, :],
                                        ps[0:TR, j, 0:2 * D].rearrange("p (i d) -> p i d", i=2), ALU.add)
            ins.then_inc(sem("y_out"), 2)
            with dve.Fori(0, NRT // 2) as p:
                for u in range(2):
                    dve.wait_ge(sem("h_tp"), p * 4 + (2 * u + 2))
                    dve.tensor_copy(hk[:, u, 3:6, :].rearrange("p m n -> p (m n)"), ps[:, 5 + 2 * u, 0:384])\
                        .then_inc(sem("hk1"), 1)
                for u in range(2):
                    dve.wait_ge(sem("y_mm1"), p * 2 + (u + 1))
                    dve.wait_ge(sem(f"st_sorted_{u}"), p * 16 + 16)
                    dve.tensor_copy(ys[:, u], ps[:, 2 * u, 0:D]).then_inc(sem("y_out"), 1)

            def experts(name, gates):
                with dve.Fori(0, NE // 2) as e2:
                    for u in range(2):
                        e = e2 * 2 + u
                        dve.wait_ge(sem(f"{name}_y"), e * TT + 1)
                        dve.tensor_copy(gcol[:, u, :], gates[:, :, bass.ds(e, 1)].rearrange("p t o -> p (t o)"))\
                            .then_inc(sem(f"{name}_gcol"), 1)
                        dve.wait_ge(sem(f"{name}_gcol"), e + 1)
                        for tt in range(TT):
                            dve.wait_ge(sem(f"{name}_y_mm"), e * TT + (tt + 1))
                            dve.scalar_tensor_tensor(out=a[:, tt, :], in0=ps[0:TR, 4 + tt % 2, 0:D],
                                                     scalar=gcol[:, u, tt:tt + 1], in1=a[:, tt, :],
                                                     op0=ALU.mult, op1=ALU.add).then_inc(sem(f"{name}_y"), 1)
                dve.wait_ge(sem(f"{name}_y"), NE * TT + 1)

            step(dve.tensor_tensor(h[:], h[:], a[:], ALU.add))
            for tt in range(TT):
                dve.wait_ge(sem(f"gathered{tt}"), 16)
                dve.tensor_tensor(h[:, tt, :], h[:, tt, :], t[:, tt, :], ALU.add).then_inc(sem("gather_sum"), 1)
                if tt:
                    dve.wait_ge(sem("gather_sum"), tt)
                    dve.bn_stats(st[:, tt - 1, :], h[:, tt - 1, :])
            dve.wait_ge(sem("gather_sum"), TT)
            step(dve.bn_stats(st[:, TT - 1, :], h[:, TT - 1, :]))

            normalise("ffn", h, a, True)
            dve.wait_ge(sem("logits_mm"), 1)
            step(dve.tensor_tensor(lg[:], ps[0:TR, 6, 0:TT * NE].rearrange("p (t e) -> p t e", t=TT),
                                   bcast(b2s[:], 1, TT), ALU.add))
            step(dve.tensor_reduce(m6[:, 0, :], lg[:], X, ALU.max))
            dve.tensor_tensor(lg[:], lg[:], bcast(m6[:, 0, :], 2, NE), ALU.subtract).then_inc(sem("router_sub"), 1)
            dve.wait_ge(sem("router_exp"), 1)
            step(dve.tensor_reduce(m6[:, 0, :], lg[:], X, ALU.add))
            step(dve.reciprocal(m6[:, 1, :], m6[:, 0, :]))
            step(dve.tensor_tensor(lg[:], lg[:], bcast(m6[:, 1, :], 2, NE), ALU.mult))
            first_max(lg, oh1)
            step(dve.scalar_tensor_tensor(out=gate[:], in0=oh1, scalar=-4.0, in1=lg[:], op0=ALU.mult, op1=ALU.add))
            step(dve.tensor_reduce(m6[:, 0, :], gate[:], X, ALU.max))
            step(dve.tensor_tensor(gate[:], gate[:], bcast(m6[:, 0, :], 2, NE), ALU.is_equal))
            step(dve.tensor_tensor(key[:], gate[:], bcast(const("rev", TR), 1, TT), ALU.mult))
            step(dve.tensor_reduce(m6[:, 0, :], key[:], X, ALU.max))
            step(dve.tensor_tensor(gate[:], key[:], bcast(m6[:, 0, :], 2, NE), ALU.is_equal))
            step(dve.tensor_tensor(oh1, oh1, gate[:], ALU.add))
            step(dve.tensor_tensor(oh1, oh1, lg[:], ALU.mult))
            step(dve.tensor_reduce(m6[:, 0, :], oh1, X, ALU.add))
            step(dve.tensor_scalar(m6[:, 0, :], m6[:, 0, :], 1e-8, None, ALU.add))
            step(dve.reciprocal(m6[:, 1, :], m6[:, 0, :]))
            dve.tensor_tensor(gate[:], oh1, bcast(m6[:, 1, :], 2, NE), ALU.mult).then_inc(sem("ffn_y"), 1)
            step(dve.tensor_tensor(h[:], h[:], bcast(beta[:], 1, TT), ALU.add))
            experts("ffn", gate)
            stats(a).then_inc(sem("var"), 1)
            dve.wait_ge(sem("var"), VARIANCE["u"] + 1)
            for tt in range(TT):
                ins = dve.scalar_tensor_tensor(out=t[:, tt, :], in0=a[:, tt, :], scalar=mv[:, tt, 0:1], in1=gamma[:],
                                               op0=ALU.subtract, op1=ALU.mult)
            step(ins)
            dve.wait_ge(sem("rstd"), ROOT["u"] + 1)
            for tt in range(TT):
                ins = dve.scalar_tensor_tensor(out=h[:, tt, :], in0=t[:, tt, :], scalar=rs[:, tt:tt + 1], in1=h[:, tt, :],
                                               op0=ALU.mult, op1=ALU.add)
            step(ins)

            normalise("ln3", h, t)
            for j in range(TT // 2):
                dve.wait_ge(sem("v1_mm"), j + 1)
                dve.tensor_copy(a[:, 2 * j:2 * j + 2, :], ps[0:TR, 4 + j, 0:2 * D].rearrange("p (i d) -> p i d", i=2))\
                    .then_inc(sem("v_ready"), 2)
            step(dve.tensor_tensor(h[:], h[:], bcast(bpr1[:], 1, TT), ALU.add))
            attention()
            for j in range(TT // 2):
                dve.wait_ge(sem("proj_mm"), j + 1)
                ins = dve.tensor_tensor(h[:, 2 * j:2 * j + 2, :], h[:, 2 * j:2 * j + 2, :],
                                        ps[0:TR, 5 + j, 0:2 * D].rearrange("p (i d) -> p i d", i=2), ALU.add)
            step(ins)

            stats(h).then_inc(sem("var"), 1)
            dve.wait_ge(sem("var"), VARIANCE["tok0"] + 1)
            for tt in range(TT):
                dve.scalar_tensor_tensor(out=a[:, tt, :], in0=h[:, tt, :], scalar=mv[:, tt, 0:1], in1=nw[:],
                                         op0=ALU.subtract, op1=ALU.mult).then_inc(sem("centred"), 1)
            dve.wait_ge(sem("centred"), TT)
            dve.wait_ge(sem("rstd"), ROOT["tok"] + 1)
            step(dve.scalar_tensor_tensor(out=rs3[:, 0:TT], in0=rs2[:, 0:TT], scalar=1e5, in1=m6[:, 3, :],
                                          op0=ALU.mult, op1=ALU.min))
            for tt in range(TT):
                dve.tensor_scalar(t[:, tt, :], a[:, tt, :], rs3[:, tt:tt + 1], None, ALU.mult)\
                    .then_inc(sem("rows"), 1)
            dve.wait_ge(sem("rows"), TT * NORM["tok"] + TT)
            dve.wait_ge(sem("squares"), TT)
            for tt in range(TT):
                ins = dve.tensor_scalar(a[:, tt, :], a[:, tt, :], rs2[:, tt:tt + 1], None, ALU.mult)
            step(ins)
            dve.wait_ge(sem("soft_zero"), 1)

            def by_image(ap):
                return ap.rearrange("p (b s) -> p b s", s=S)

            for n in range(2):
                dve.wait_ge(sem("logits"), n + 1)
                ins = dve.tensor_reduce(mxd[:, 0, 8 * n:8 * n + 8], by_image(hid[0:SLOTS, NH * n:NH * n + NH]), X, ALU.max)
            step(ins)
            for n in range(2):
                ins = dve.tensor_tensor(by_image(disp[:, NH * n:NH * n + NH]), by_image(hid[0:SLOTS, NH * n:NH * n + NH]),
                                        bcast(mxd[:, 0, 8 * n:8 * n + 8], 2, S), ALU.subtract)
            ins.then_inc(sem("disp_sub"), 1)
            dve.wait_ge(sem("comb_mm"), 1)
            cps = ps[0:TR, 3, 0:TT * SLOTS].rearrange("p (t s) -> p t s", t=TT)
            step(dve.tensor_reduce(mxc[:, 0, :], cps, X, ALU.max))
            dve.tensor_tensor(comb[:], cps, bcast(mxc[:, 0, :], 2, SLOTS), ALU.subtract).then_inc(sem("comb_sub"), 1)
            dve.wait_ge(sem("disp_exp"), 1)
            dd = by_image(disp[:, 0:NTOK])
            step(dve.tensor_reduce(mxd[:, 0, :], dd, X, ALU.add))
            step(dve.reciprocal(mxd[:, 1, :], mxd[:, 0, :]))
            dve.tensor_tensor(dd, dd, bcast(mxd[:, 1, :], 2, S), ALU.mult).then_inc(sem("disp"), 1)
            dve.wait_ge(sem("comb_exp"), 1)
            step(dve.tensor_reduce(mxc[:, 0, :], comb[:], X, ALU.add))
            step(dve.reciprocal(mxc[:, 1, :], mxc[:, 0, :]))
            dve.tensor_tensor(comb[:], comb[:], bcast(mxc[:, 1, :], 2, SLOTS), ALU.mult).then_inc(sem("comb"), 1)
            dve.wait_ge(sem("disp_tp"), 1)
            dve.tensor_tensor(dmt[:], bcast(ps[0:TR, 6, 0:TT * SLOTS].rearrange("p (t s) -> p t s", t=TT), 2, IPT),
                              bcast(bcast(const("vmask", TR), 1, TT), 3, SLOTS), ALU.mult).then_inc(sem("dm"), 1)
            for c in range(3):
                dve.wait_ge(sem("y_mm"), c + 1)
                dve.tensor_copy(ycmp[0:64, c], ps[0:64, c, :].rearrange("p (b j) -> p j b", b=B))\
                    .then_inc(sem("y_copied"), 1)
            with dve.Fori(0, NG) as g:
                dve.wait_ge(sem("cm_tp"), g + 2)
                dve.tensor_copy(cmT[:, 0:3 * TR], ps[:, 3, 0:3 * TR]).then_inc(sem("cmT"), 1)
                dve.wait_ge(sem("hidT_tp"), g * 2 + 1)
                for par in range(2):
                    dve.tensor_copy(hid_out(0, par), hid_in(0, par)).then_inc(sem("hidT"), 1)
                dve.wait_ge(sem("fc2_used"), g + 1)
                dve.tensor_copy(yslot[:], ps[:, 2, 0:D]).then_inc(sem("yslot"), 1)
            dve.wait_ge(sem("combined"), NG)
            for j in range(TT // 2):
                ins = dve.tensor_copy(h[:, 2 * j:2 * j + 2, :],
                                      ps[0:TR, 5 + j, 0:2 * D].rearrange("p (i d) -> p i d", i=2))
            ins.then_inc(sem("out_ready"), 1)

        @block.scalar
        def _(act):
            def columns(name, affine=None):
                for j in range(TT // 2):
                    act.wait_ge(sem("tp"), 3 * TURN[name] + j + 1)
                    lo, hi = 2 * TR * j, 2 * TR * j + 2 * TR
                    if affine is None:
                        act.activation(xT[:, :, lo:hi], ps[0:KH, j, :].rearrange("p (c n) -> p c n", c=2)[:, :, 0:2 * TR],
                                       ACT.Copy).then_inc(sem("cols"), 1)
                        continue
                    for c in range(2):
                        ins = act.activation(xT[:, c, lo:hi], ps[0:KH, j, 256 * c:256 * c + 2 * TR], ACT.Identity,
                                             scale=lnv[:, affine, c:c + 1], bias=lnv[:, affine + 1, c:c + 1])
                    ins.then_inc(sem("cols"), 1)

            def attention():
                def values(j):
                    if j >= 2:
                        act.wait_ge(sem("o_mm"), j - 1)
                    for x in range(IPT):
                        ins = act.activation(
                            vblk[:, j % 2, :, 17 * x:17 * x + HD],
                            vrep[:, 2 * j:2 * j + 2, :].rearrange("p i (g n) -> p (i g) n", g=4)[:, :, HD * x:HD * x + HD],
                            ACT.Identity, scale=const("vmask", TR)[:, x:x + 1])
                    ins.then_inc(sem("vblk"), 1)

                def exps(j):
                    act.wait_ge(sem("s_sub"), j + 1)
                    act.activation(sc[:, j % 3, :], sc[:, j % 3, :], ACT.Exp, scale=HD ** -0.5).then_inc(sem("exp"), 1)

                act.wait_ge(sem("v_ones"), 1)
                act.wait_ge(sem("vrep"), 16 * 9)
                values(0)
                exps(0)
                exps(1)
                for j in range(PAIRS):
                    if j + 2 < PAIRS:
                        exps(j + 2)
                    act.wait_ge(sem("pT_mm"), j + 1)
                    if j >= 2:
                        act.wait_ge(sem("o_mm"), j - 1)
                    act.activation(pT[:, j % 2, :], ps[0:TR, 3 + j % 2, :], ACT.Copy).then_inc(sem("pT"), 1)
                    if j + 1 < PAIRS:
                        values(j + 1)

            for k in range(1, KT, 2):
                act.wait_ge(sem(f"ld_x{k // 2}"), 16)
                if k >= 4:
                    act.wait_ge(sem("patches_tp"), 2 * (k - 4) + 2)
                act.activation(rows_of(k), xin[:, 2 * k:2 * k + 2].rearrange("p r v c -> p v r c"), ACT.Copy)\
                    .then_inc(sem("patches_rows1"), 1)
                for kk in (k - 1, k):
                    act.wait_ge(sem("patches_tp"), 2 * kk + 2)
                    act.activation(patT[:, kk, 288:576], ps[0:KH, (2 * kk + 1) % 4, 0:288], ACT.Copy)\
                        .then_inc(sem("patches_copied1"), 1)
            act.wait_ge(sem("emb_mm"), 4)
            act.wait_ge(sem("pads_zero"), 1)
            for n in range(2):
                act.activation(emb_out(1, n), emb_in(1, n), ACT.Copy).then_inc(sem("emb_cols"), 1)

            act.wait_ge(sem("ld_small"), 16 * N_SMALL)
            columns("ln1", 0)
            act.wait_ge(sem("s0_sub"), 1)
            act.activation(s0[:, 0], s0[:, 0], ACT.Exp, scale=HD ** -0.5).then_inc(sem("s0_exp"), 1)
            columns("ln2", 2)

            def x_features(u, count):
                act.wait_ge(sem("x_tp"), count)
                for k in range(2):
                    ins = act.activation(xk[0:KH, u, k, :], ps[0:KH, 2 * u + 1, RT * k:RT * k + RT], ACT.Identity,
                                         scale=lnv[:, 2, k:k + 1], bias=lnv[:, 3, k:k + 1])
                ins.then_inc(sem("xk"), 1)

            def tile_pair(p, last):
                for u in range(2):
                    for n in range(2):
                        act.wait_ge(sem("up_mm"), p * 4 + (2 * u + n + 1))
                        act.activation(hs[:, u, 384 * n:384 * n + 384], ps[:, 2 * u + n, 0:384], ACT.Gelu)\
                            .then_inc(sem("gelu"), 1)
                for u in range(2):
                    act.wait_ge(sem("h_tp"), p * 4 + (2 * u + 1))
                    act.activation(hk[:, u, 0:3, :].rearrange("p m n -> p (m n)"), ps[:, 4 + 2 * u, 0:384], ACT.Copy)\
                        .then_inc(sem("hk0"), 1)
                    if not last:
                        x_features(u, p * 2 + (u + 3))

            act.wait_ge(sem("xk_ones"), 1)
            for u in range(2):
                x_features(u, u + 1)
            with act.Fori(0, NRT // 2 - 1) as p:
                tile_pair(p, False)
            tile_pair(NRT // 2 - 1, True)
            act.wait_ge(sem("h_pads"), 1)
            columns("ffn")
            act.wait_ge(sem("router_mm"), 1)
            for n in range(2):
                act.activation(rT[:, NH * n:NH * n + NH], ps[0:KH, 6 + n, 0:NH], ACT.Gelu, bias=b1s[:, 0:1])\
                    .then_inc(sem("router_h"), 1)
            act.wait_ge(sem("router_sub"), 1)
            act.activation(lg[:], lg[:], ACT.Exp).then_inc(sem("router_exp"), 1)
            with act.Fori(0, NE // 2) as e2:
                for u in range(2):
                    e = e2 * 2 + u
                    act.wait_ge(sem(f"ld_down_{u}"), e2 * 32 + 32)
                    for q in range(2 * ZT):
                        act.wait_ge(sem("ffn_z_mm"), e * 4 + (q + 1))
                        act.activation(zT[u][:, q // 2, NH * (q % 2):NH * (q % 2) + NH], ps[:, q, 0:NH], ACT.Gelu,
                                       bias=downb[:, u, q // 2:q // 2 + 1]).then_inc(sem("ffn_z"), 1)
            columns("ln3")
            for q in range(8):
                act.wait_ge(sem("qk1_mm"), q + 1)
                dst = (qT, kT)[q // 4]
                act.activation(dst[:, q // 2 % 2, NH * (q % 2):NH * (q % 2) + NH], ps[0:KH, q % 4, 0:NH], ACT.Copy)\
                    .then_inc(sem("qk1"), 1)
            attention()
            columns("proj")
            for tt in range(TT):
                act.wait_ge(sem("centred"), tt + 1)
                act.activation(t[:, tt, :], a[:, tt, :], ACT.Square, accum_out=m6[:, 2, tt:tt + 1])\
                    .then_inc(sem("squares"), 1)
            columns("tok")
            act.wait_ge(sem("soft_zero"), 1)
            for n in range(2):
                act.wait_ge(sem("disp_mm"), n + 1)
                act.activation(hid[0:SLOTS, NH * n:NH * n + NH], ps[0:SLOTS, 4 + n, 0:NH], ACT.Copy)\
                    .then_inc(sem("logits"), 1)
            act.wait_ge(sem("disp_sub"), 1)
            act.activation(disp[:, 0:NTOK], disp[:, 0:NTOK], ACT.Exp).then_inc(sem("disp_exp"), 1)
            act.wait_ge(sem("comb_sub"), 1)
            act.activation(comb[:], comb[:], ACT.Exp).then_inc(sem("comb_exp"), 1)
            for c in range(3):
                act.wait_ge(sem("y_mm"), c + 1)
                act.activation(ycmp[64:128, c], ps[64:128, c, :].rearrange("p (b j) -> p j b", b=B), ACT.Copy)\
                    .then_inc(sem("y_copied"), 1)
            with act.Fori(0, NG) as g:
                act.wait_ge(sem("fc1_used"), g + 2)
                for n in range(2):
                    act.activation(hid[:, 384 * n:384 * n + 384], ps[:, n, 0:384], ACT.Gelu).then_inc(sem("hid"), 1)
                act.wait_ge(sem("cm_tp"), g + 2)
                act.activation(cmT[:, 3 * TR:NPAD], ps[:, 4, 0:3 * TR], ACT.Copy).then_inc(sem("cmT"), 1)
                act.wait_ge(sem("hidT_tp"), g * 2 + 2)
                for par in range(2):
                    act.activation(hid_out(1, par), hid_in(1, par), ACT.Copy).then_inc(sem("hidT"), 1)

        @block.gpsimd
        def _(pool):
            step = Steps(pool, "pool_step")

            def root(out_, in_, eps, name, rows=TR, n=TT, floor=False):
                pool.wait_ge(sem("var"), VARIANCE[name] + 1)
                if ROOT[name]:
                    pool.wait_ge(sem("rstd"), ROOT[name])
                half = const("mhalf", rows)[:, 0:n]
                step(pool.tensor_scalar(ve[0:rows, 0:n], in_, *eps))
                ins = pool.tensor_tensor(out_, ve[0:rows, 0:n], half, ALU.pow)
                if floor:
                    step(ins)
                    ins = pool.tensor_scalar(out_, out_, 1e5, None, ALU.min)
                ins.then_inc(sem("rstd"), 1)

            def keys():
                for j in range(B // 2):
                    if j >= 2:
                        pool.wait_ge(sem("s_mm"), j - 1)
                    for i in range(2):
                        b = 2 * j + i
                        for c in range(2):
                            ins = pool.tensor_tensor(kblk[:, j % 2, c, i, :].rearrange("p (x n) -> p x n", x=HH),
                                                     bcast(kT[:, c, S * b:S * b + S], 1, HH),
                                                     bcast(const("kmask", KH), 2, S), ALU.mult)
                    ins.then_inc(sem("kblk"), 1)

            plus = (LN_EPS, None, ALU.add)
            pool.memset(xT[:], 0.0)
            pool.memset(b2pad[:], 0.0)
            pool.memset(oh[:, TT, :], 0.0)
            pool.memset(fb1[:], 0.0)
            pool.memset(fb2[:], 0.0).then_inc(sem("pads_zero"), 1)
            pool.wait_ge(sem("ld_cst"), 16)
            twice = (1.0 + LN_EPS, LN_EPS * LN_EPS, ALU.mult, ALU.add)
            root(rs2[:, 0:TT], mv[:, :, 1], twice, "ln1")
            root(rs[:, 0:TT], mv[:, :, 1], plus, "in0")
            pool.wait_ge(sem("emb_cols"), 4)
            pool.memset(zeros, 0.0).then_inc(sem("zeros"), 1)
            pool.memset(xk[:], 1.0).then_inc(sem("xk_ones"), 1)
            pool.memset(ohT[:], 0.0)
            pool.memset(hT[:, :, NTOK:NPAD], 0.0).then_inc(sem("h_pads"), 1)
            root(sst[:, 10:11], sst[:, 9:10], (float(D), None, ALU.mult), "slots", SLOTS, 1, True)
            root(rs[:, 0:TT], mv[:, :, 1], plus, "ln2")
            for u in range(2):
                pool.wait_ge(sem(f"st_sorted_{u}"), 16)
            pool.wait_ge(sem("place"), 1)
            for tt in range(TT):
                n = TR if tt < TT - 1 else LAST
                pool.indirect_dma_start(xsorted, bass.IndirectOffsetOnAxis(ap=place[0:n, tt:tt + 1], axis=0),
                                        t[0:n, tt, :], None).then_inc(sem("scattered"), 16)
            for u in range(2):
                pool.wait_ge(sem(f"st_sorted_{u}"), 16 * (NRT // 2 + 1))
            for tt in range(TT):
                n = TR if tt < TT - 1 else LAST
                pool.indirect_dma_start(t[0:n, tt, :], None, ysorted,
                                        bass.IndirectOffsetOnAxis(ap=place[0:n, tt:tt + 1], axis=0))\
                    .then_inc(sem(f"gathered{tt}"), 16)
            for name in ("ffn", "u", "ln3"):
                root(rs[:, 0:TT], mv[:, :, 1], plus, name)
            pool.memset(qT[:, :, NTOK:NPAD], 0.0).then_inc(sem("q_pads"), 1)
            pool.tensor_copy(vblk[:].rearrange("p u n (x c) -> p (u n) x c", x=IPT)[:, :, :, HD],
                             bcast(const("vmask", TR), 1, 16)).then_inc(sem("v_ones"), 1)
            pool.wait_ge(sem("qk1"), 8)
            keys()
            root(rs2[:, 0:TT], mv[:, :, 1], twice, "tok0")
            pool.wait_ge(sem("squares"), TT)
            pool.tensor_tensor(m6[:, 3, :], m6[:, 2, :], const("mhalf", TR)[:, 0:TT], ALU.pow)\
                .then_inc(sem("rstd"), 1)
            pool.memset(hid[0:SLOTS, NTOK:NPAD], 0.0)
            pool.memset(cmT[:], 0.0)
            pool.memset(hidT[:], 0.0).then_inc(sem("soft_zero"), 1)
            pool.wait_ge(sem("comb"), 1)
            pool.wait_ge(sem("y_copied"), 6)
            with pool.Fori(0, NG // 2) as g2:
                for u in range(2):
                    g = g2 * 2 + u
                    pool.wait_ge(sem("fc1_used"), g2 * 2 + 1)
                    for c in range(3):
                        ins = pool.tensor_tensor(
                            yg[:, u, c].rearrange("p q (two b) -> p q two b", two=2),
                            bcast(ycmp[:, c, bass.ds(g * QP, QP), :], 2, 2),
                            bcast(bcast(const("pmask"), 1, QP), 3, B), ALU.mult)
                    ins.then_inc(sem("yg"), 1)
                    pool.wait_ge(sem("cm_tp"), g + 1)
                    for tt in range(TT):
                        ins = pool.tensor_tensor(xe[:, tt],
                                                 bcast(comb[:, tt, bass.ds(g * GS, GS)], 2, B),
                                                 bcast(const("bmask", TR)[:, B * tt:B * tt + B], 1, GS), ALU.mult)
                    ins.then_inc(sem("xe"), 1)


INPUTS = ["x", "L0_tok_W_proj", "L0_tok_b_proj", "L0_tok_cls_token", "L0_tok_pos_embedding", "L0_attn_ln1_g",
          "L0_attn_ln1_b", "L0_attn_Wq", "L0_attn_bq", "L0_attn_Wk", "L0_attn_bk", "L0_attn_Wv", "L0_attn_bv",
          "L0_attn_ln2_g", "L0_attn_ln2_b", "L0_attn_Wg", "L0_attn_bg", "L0_attn_W1", "L0_attn_b1", "L0_attn_W2",
          "L0_attn_b2", "L0_ffn_w1", "L0_ffn_b1", "L0_ffn_w2", "L0_ffn_b2", "L0_ffn_down_w", "L0_ffn_down_b",
          "L0_ffn_up_w", "L0_ffn_gamma", "L0_ffn_beta", "L1_attn_w_qkv", "L1_attn_w_proj", "L1_attn_b_proj",
          "L1_attn_temperature", "L1_ffn_slots", "L1_ffn_scale", "L1_ffn_fc1_weight", "L1_ffn_fc1_bias",
          "L1_ffn_fc2_weight", "L1_ffn_fc2_bias", "L1_ffn_norm_weight"]


def kernel(**inputs):
    import concourse.bacc as bacc
    from concourse.bass_utils import run_bass_kernel_spmd

    nc = bacc.Bacc("TRN2", target_bir_lowering=False, num_devices=1)
    arrays, w = {}, {}
    for name in INPUTS:
        v = np.ascontiguousarray(inputs[name])
        arrays[f"in_{name}"] = v
        w[name] = nc.dram_tensor(f"in_{name}", v.shape, mybir.dt.from_np(v.dtype), kind="ExternalInput").ap()
    table = constant_table()
    arrays["consts"] = table
    consts = nc.dram_tensor("consts", table.shape, F32, kind="ExternalInput").ap()
    out = nc.dram_tensor("out", (B, S, D), F32, kind="ExternalOutput").ap()
    vit_tower(nc, w, consts, out)
    r = run_bass_kernel_spmd(nc, [arrays], core_ids=[0])
    return r.results[0]["out"]
```

```python
from contextlib import ExitStack

import numpy as np

import concourse.bass as bass
from concourse import mybir

F32 = mybir.dt.float32
I32 = mybir.dt.int32
ALU = mybir.AluOpType
ACT = mybir.ActivationFunctionType
X = mybir.AxisListType.X

B, IMG, PATCH, CH = 16, 96, 16, 3
D = 192
KH = D // 2
S = (IMG // PATCH) ** 2 + 1
NTOK = B * S
IPT = 3
TR = IPT * S
TT = -(-B // IPT)
NPAD = TR * TT
LAST = NTOK - (TT - 1) * TR
NH = NTOK // 2
HEADS, HD = 12, 16
HH = HEADS // 2
HW = HH * S
NE = 8
FF = 768
FT = FF // 128
DZ = 256
ZT = DZ // 128
SLOTS = 64
GS = 8
NG = SLOTS // GS
QP = GS // 2
WP = IMG // PATCH
ROW = PATCH * CH
PDIM = PATCH * ROW
KT = PDIM // 128
XP = 4
LN_EPS = 1e-5
RT = 128
NRT = (NTOK + NE * (RT - 1)) // RT
LEVELS = -(-NTOK // RT)

CONSTS = {}
_at = 0
for _name, _n in (("ident", 128), ("sel", 128), ("kmask", HH), ("vmask", IPT), ("eye", S), ("cos", HD),
                  ("sin", HD), ("bmask", TT * B), ("rev", NE), ("pmask", 2), ("mhalf", 8), ("valid", 1), ("level", LEVELS),
                  ("lower", NE * NE), ("tile", NRT), ("before", TR), ("ones", TR)):
    CONSTS[_name] = (_at, _at + _n)
    _at += _n
NCONST = _at
NKEEP = CONSTS["before"][0]


def constant_table():
    c = np.zeros((128, NCONST), np.float32)

    def put(name, a):
        lo, hi = CONSTS[name]
        c[: a.shape[0], lo:hi] = a

    row = np.arange(128)
    put("ident", np.eye(128, dtype=np.float32))
    put("sel", (row[:GS, None] == row[None, :] // B).astype(np.float32))
    put("kmask", (row[:KH, None] // HD == np.arange(HH)[None, :]).astype(np.float32))
    put("vmask", (row[:TR, None] // S == np.arange(IPT)[None, :]).astype(np.float32))
    put("eye", (row[:, None] % 64 == np.arange(S)[None, :]).astype(np.float32))
    inv = (np.float32(1.0) / np.float32(10000.0) ** (np.arange(0, HD, 2, dtype=np.float32) / HD)).astype(np.float32)
    ang = ((row[:TR] % S).astype(np.float32)[:, None] * inv[None, :]).astype(np.float32)
    cos, sin = np.cos(ang), np.sin(ang)
    put("cos", np.concatenate([cos, cos], 1))
    put("sin", np.concatenate([-sin, sin], 1))
    image = IPT * np.arange(TT)[None, :] + row[:TR, None] // S
    put("bmask", (image[:, :, None] == np.arange(B)).astype(np.float32).reshape(TR, TT * B))
    put("rev", np.broadcast_to(np.arange(NE, 0, -1, dtype=np.float32), (128, NE)))
    put("pmask", (row[:, None] // 64 == np.arange(2)[None, :]).astype(np.float32))
    put("mhalf", np.full((128, 8), -0.5, np.float32))
    put("before", (row[:TR, None] < row[None, :TR]).astype(np.float32))
    put("ones", np.ones((TR, TR), np.float32))
    put("valid", (row[:TR, None] < LAST).astype(np.float32))
    put("level", np.broadcast_to(RT * np.arange(LEVELS, dtype=np.float32), (128, LEVELS)))
    lower = np.arange(NE)[:, None] > np.arange(NE)[None, :]
    put("lower", np.broadcast_to(lower.reshape(1, NE * NE), (128, NE * NE)).astype(np.float32))
    put("tile", np.broadcast_to(np.arange(NRT, dtype=np.float32), (128, NRT)))
    return c


def bcast(ap, axis, n):
    ap = ap.unsqueeze(axis)
    shape = list(ap.shape)
    shape[axis] = n
    return ap.broadcast_to(shape)


def vit_tower(nc, w, consts, out):
    with ExitStack() as ctx:
        def sb(name, shape, dtype=F32):
            return ctx.enter_context(nc.sbuf_tensor(name, shape, dtype))

        sems = {}

        def sem(name):
            if name not in sems:
                sems[name] = ctx.enter_context(nc.semaphore(name))
            return sems[name]

        ps = ctx.enter_context(nc.psum_tensor("ps", [128, 8, 512], F32))

        fc1 = sb("fc1", [128, 2, QP * 3 * FF])
        fc2 = sb("fc2", [128, 2, GS * FT * D])
        fc1v = fc1[:, :, :].rearrange("p u (q c f) -> p u q c f", q=QP, c=3)
        fc2v = fc2[:, :, :].rearrange("p u (s m d) -> p u s m d", s=GS, m=FT)
        wa, wb = fc1[:, 1, :], fc2[:, 1, :]

        at = [0, 0]

        def carve(which, parts, n):
            lo = at[which]
            at[which] = lo + n
            assert at[which] <= QP * 3 * FF
            return (wa, wb)[which][0:parts, lo:lo + n]

        w1r = carve(0, KH + 1, 2 * 2 * FF).rearrange("p (u k f) -> p u k f", u=2, k=2)
        w2r = carve(0, 128, 2 * FT * D).rearrange("p (u m d) -> p u m d", u=2, m=FT)
        wproj = carve(0, 128, KT * D).rearrange("p (k d) -> p k d", k=KT)
        downr = carve(0, KH, 2 * 2 * DZ).rearrange("p (u k f) -> p u k f", u=2, k=2)
        upr = carve(0, 128, 2 * ZT * D).rearrange("p (u j d) -> p u j d", u=2, j=ZT)
        xin = carve(1, B * WP, PATCH * IMG * CH).rearrange("p (r v c) -> p r v c", r=PATCH, v=WP)
        patT = carve(1, 128, KT * B * 36).rearrange("p (k n) -> p k n", k=KT)
        at[1] = 0
        vrep = carve(1, TR, B * D).rearrange("p (b d) -> p b d", b=B)
        kblk = carve(1, KH, 2 * 2 * 2 * HW).rearrange("p (u c i n) -> p u c i n", u=2, c=2, i=2)
        vblk = carve(1, TR, 2 * 2 * 4 * 51).rearrange("p (u n c) -> p u n c", u=2, c=51)
        qT = carve(1, KH, 2 * NPAD).rearrange("p (c n) -> p c n", c=2)
        kT = carve(1, KH, 2 * NPAD).rearrange("p (c n) -> p c n", c=2)
        ob = carve(1, 128, 2 * D).rearrange("p (u d) -> p u d", u=2)
        at[1] = 0
        hT = carve(1, 128, (ZT + 1) * NPAD).rearrange("p (m n) -> p m n", m=ZT + 1)
        ohT = carve(1, 128, NPAD)
        xs = carve(1, RT, 2 * D).rearrange("p (u d) -> p u d", u=2)
        xk = carve(1, KH + 1, 2 * 2 * RT).rearrange("p (u k n) -> p u k n", u=2, k=2)
        hs = carve(1, RT, 2 * FF).rearrange("p (u f) -> p u f", u=2)
        hk = carve(1, 128, 2 * FT * RT).rearrange("p (u m n) -> p u m n", u=2, m=FT)
        ys = carve(1, RT, 2 * D).rearrange("p (u d) -> p u d", u=2)
        zeros = carve(1, RT, NRT // 2 * D)
        krot, ktmp, kq = (carve(1, TR, TT * HD).rearrange("p (t d) -> p t d", t=TT) for _ in range(3))
        order = carve(1, TR, 2 * TR)
        before, ones = order[:, 0:TR], order[:, TR:2 * TR]
        count = carve(1, TR, NE * LEVELS).rearrange("p (e l) -> p e l", e=NE)
        ntile = carve(1, TR, 3 * NE).rearrange("p (n e) -> p n e", n=3)
        run = carve(1, TR, (TT + 1) * NE).rearrange("p (t e) -> p t e", t=TT + 1)
        below = carve(1, TR, NE * NE).rearrange("p (a b) -> p a b", a=NE)
        owner = carve(1, 1, NRT * NE).rearrange("p (t e) -> p t e", t=NRT)
        owned = carve(1, 1, NRT)
        prow = carve(1, TR, TT * NE).rearrange("p (t e) -> p t e", t=TT)
        row_sum = carve(1, TR, TT)
        zT = (hT[:, 0:ZT, :], hs.rearrange("p u f -> p (u f)")[:, 0:ZT * NPAD].rearrange("p (m n) -> p m n", m=ZT))
        rT = hT[0:KH, ZT, :]

        cst = sb("cst", [128, NKEEP])

        def const(name, parts=128):
            lo, hi = CONSTS[name]
            return cst[0:parts, lo:hi]

        ident = const("ident")
        h = sb("h", [TR, TT, D])
        a = sb("a", [TR, TT, D])
        t = sb("t", [TR, TT, D])
        xT = sb("xT", [KH, 2, NPAD])
        slT = sb("slT", [KH, 2, 2 * SLOTS])
        slots = sb("slots", [SLOTS, D])
        slsc = sb("slsc", [SLOTS, 1])
        lnv = sb("lnv", [KH, 4, 2])
        nw = sb("nw", [TR, D])
        st = sb("st", [TR, TT, 6])
        mv = sb("mv", [TR, TT, 2])
        rs = sb("rs", [TR, 8])
        ve = sb("ve", [TR, 8])
        rs2 = sb("rs2", [TR, 8])
        rs3 = sb("rs3", [TR, 8])
        m6 = sb("m6", [TR, 4, TT])
        sst = sb("sst", [SLOTS, 12])
        place = sb("place", [TR, TT], I32)
        tile_expert = sb("tile_expert", [1, NRT], I32)
        xsorted = nc.dram_tensor("xsorted", (NRT * RT, D), F32).ap()
        ysorted = nc.dram_tensor("ysorted", (NRT * RT, D), F32).ap()
        fb1 = sb("fb1", [128, 2, FF])
        fb2 = sb("fb2", [128, 2, D])

        shared = sb("shared", [128, 8288])
        used = [0]

        def share(parts, *dims):
            n = int(np.prod(dims))
            lo = used[0]
            used[0] += n
            assert used[0] <= 8288, used[0]
            v = shared[0:parts, lo:lo + n]
            names = "abcd"[:len(dims)]
            if len(dims) > 1:
                v = v.rearrange(f"p ({' '.join(names)}) -> p {' '.join(names)}", **dict(zip(names, dims)))
            return v

        posr = share(TR, D)
        addr = share(TR, D)
        wqkv0 = share(KH, 2, D + 2 * HD)
        bqkv0 = share(TR, D + 2 * HD)
        qkv = share(TR, TT, D + 2 * HD)
        s0 = share(TR, 2, TT, HEADS)
        wg0 = share(KH, 2, NE)
        bg0 = share(TR, NE)
        b2pad = share(128, D)
        w1s = share(KH, 2, KH)
        b1s = share(KH, 1)
        w2s = share(KH, NE)
        b2s = share(TR, NE)
        downb = share(128, 2, ZT)
        gamma = share(TR, D)
        beta = share(TR, D)
        wqkv1 = share(KH, 2, 3 * D)
        wpr1 = share(KH, 2, D)
        bpr1 = share(TR, D)
        temp = share(128, HEADS)
        dmask = share(128, HEADS, S)
        sc = share(128, 3, HEADS * S)
        pT = share(TR, 2, 512)
        mx = share(128, 2, HEADS)
        den = share(128, 2, HEADS)
        lg = share(TR, TT, NE)
        key = share(TR, TT, NE)
        oh = share(TR, TT, NE)
        gate = share(TR, TT, NE)
        gcol = share(TR, 2, TT)
        used[0] = 0
        ycmp = share(128, 3, SLOTS // 2, B)
        dmt = share(TR, TT, IPT, SLOTS)
        comb = share(TR, TT, SLOTS)
        yg = share(128, 2, 3, QP, 32)
        hid = share(128, FF)
        hidT = share(128, FT, 2, 128)
        yslot = share(128, D)
        xe = share(TR, TT, GS, B)
        cmT = share(128, NPAD)
        mxd = share(SLOTS, 2, B)
        mxc = share(TR, 2, TT)
        disp = cmT[0:SLOTS, :]

        def load(eng, dst, src, name):
            eng.dma_start(dst, src).then_inc(sem(name), 16)

        def rowb(v, n):
            return v.unsqueeze(0).broadcast_to([n, v.shape[0]])

        w1d = w["L0_attn_W1"].rearrange("e (k p) f -> e p k f", k=2)
        w2d = w["L0_attn_W2"].rearrange("e (m p) d -> e p m d", m=FT)
        downd = w["L0_ffn_down_w"].rearrange("e (k p) f -> e p k f", k=2)
        upd = w["L0_ffn_up_w"].rearrange("e (p j) d -> e p j d", j=ZT)
        downbd = w["L0_ffn_down_b"].rearrange("e (p j) -> e p j", j=ZT)
        fc1d = w["L1_ffn_fc1_weight"].rearrange("(g q two) (p c) f -> g q (two p) (c f)", q=QP, two=2, c=3)
        fc2d = w["L1_ffn_fc2_weight"].rearrange("(g s) (p m) d -> g s p (m d)", s=GS, m=FT)
        fb1d = w["L1_ffn_fc1_bias"].rearrange("(g s) f -> g s f", s=GS)
        fb2d = w["L1_ffn_fc2_bias"].rearrange("(g s) f -> g s f", s=GS)

        N_ATT0, N_SMALL = 6, 23

        def w1_load(sp, u, e):
            load(sp, w1r[0:KH, u], w1d[bass.ds(e, 1)].rearrange("o p k f -> p (o k) f"), f"ld_w1_{u}")
            load(sp, w1r[KH:KH + 1, u, 0], w["L0_attn_b1"][bass.ds(e, 1)], f"ld_w1_{u}")

        def w2_load(sp, u, e):
            load(sp, w2r[:, u], w2d[bass.ds(e, 1)].rearrange("o p m d -> p (o m) d"), f"ld_w2_{u}")

        def expert_of(sp, tile):
            return sp.value_load(tile_expert[0:1, bass.ds(tile, 1)], min_val=0, max_val=NE - 1)

        def down_load(sp, u, e):
            load(sp, downr[:, u], downd[e], f"ld_down_{u}")
            load(sp, downb[:, u], downbd[e], f"ld_down_{u}")

        def up_load(sp, u, e):
            load(sp, upr[:, u], upd[e], f"ld_up_{u}")

        def fc1_load(sp, u, q, g):
            load(sp, fc1[:, u, q * 3 * FF:(q + 1) * 3 * FF], fc1d[g, q], f"ld_fc1_{u}_{q}")

        def fc2_load(sp, u, q, g):
            for s in (2 * q, 2 * q + 1):
                load(sp, fc2[:, u, s * FT * D:(s + 1) * FT * D], fc2d[g, s], f"ld_fc2_{u}_{q}")

        def bias1_load(sp, u, g):
            load(sp, fb1[0:GS, u], fb1d[g], f"ld_fb1_{u}")

        def bias2_load(sp, u, g):
            load(sp, fb2[0:GS, u], fb2d[g], f"ld_fb2_{u}")

        def replicate_v(sp):
            sp.wait_ge(sem("v_ready"), TT)
            for r in range(IPT):
                n = TT if r == 0 else TT - 1
                for g in range(IPT):
                    sp.dma_start(vrep[S * g:S * g + S, r:r + IPT * (n - 1) + 1:IPT, :],
                                 a[S * r:S * r + S, 0:n, :]).then_inc(sem("vrep"), 16)

        def gather_heads(sp):
            for j in range(B // 2):
                sp.wait_ge(sem("o_ready"), j + 1)
                for i in range(2):
                    b = 2 * j + i
                    sp.dma_start(t[S * (b % IPT):S * (b % IPT) + S, b // IPT, :],
                                 ob[64 * i:64 * i + S, j % 2, :]).then_inc(sem(f"gather{j % 2}"), 16)

        patches = fc1[0:B * WP, 0, 0:WP * PDIM].rearrange("p (v f) -> p v f", v=WP)

        def patch_rows(part, v):
            lo = part * PATCH // XP * ROW
            return patches[:, 3 * v:3 * v + 3, lo:lo + PATCH // XP * ROW].rearrange("p v (r c) -> p v r c", c=ROW)

        def image_rows(part, v):
            n = PATCH // XP
            return xin[:, n * part:n * part + n, 3 * v:3 * v + 3, :].rearrange("p r v c -> p v r c")

        def emb_out(m, n):
            return xT[:, m, 0:NTOK].rearrange("p (b s) -> p b s", s=S)[:, :, 1:S]\
                .rearrange("p b (y x) -> p b y x", y=WP)[:, :, :, 3 * n:3 * n + 3]

        def emb_in(m, n):
            return ps[0:KH, 4 + 2 * m + n, 0:288].rearrange("p (x b y) -> p b y x", x=3, b=B)

        def hid_out(k, par):
            return hidT[:, 3 * k:3 * k + 3, par, :].rearrange("p m (q two b) -> p m q two b", q=QP, two=2)[:, :, :, par, :]

        def hid_in(k, par):
            return ps[:, 3 + k, 0:384].rearrange("p (m q two b) -> p m q two b", m=3, q=QP, two=2)[:, :, :, par, :]

        NORM = {n: i for i, n in enumerate(("ln1", "ln2", "ffn", "ln3", "tok"))}
        ROOT = {n: i for i, n in enumerate(("ln1", "in0", "slots", "ln2", "ffn", "u", "ln3", "tok0", "tok"))}
        VARIANCE = {n: i for i, n in enumerate(("in0", "slots", "ln2", "ffn", "u", "ln3", "tok0"))}
        VARIANCE["ln1"] = VARIANCE["in0"]
        TURN = {n: i for i, n in enumerate(("ln1", "ln2", "ffn", "ln3", "proj", "tok"))}
        PAIRS = B // 2
        PROJ_BANK = (7, 3, 4)
        HALVES = (range(TT // 2), range(TT // 2, TT))

        block = ctx.enter_context(nc.Block())

        @block.sync
        def _(sp):
            load(sp, cst[:, :], consts[:, 0:NKEEP], "ld_cst")
            xd = w["x"].rearrange("b (v r) x c -> (b v) r (x c)", v=WP)
            for k in range(4):
                load(sp, xin[:, 4 * k:4 * k + 4].rearrange("p r v c -> p r (v c)"), xd[:, 4 * k:4 * k + 4], f"ld_x{k}")
                if k == 0:
                    load(sp, wproj[:], w["L0_tok_W_proj"].rearrange("(k p) d -> p k d", p=128), "ld_wproj")
            for r in range(IPT):
                load(sp, posr[S * r:S * r + S], w["L0_tok_pos_embedding"], "ld_tok")
                load(sp, addr[S * r + 1:S * r + S], rowb(w["L0_tok_b_proj"], S - 1), "ld_tok")
                load(sp, addr[S * r:S * r + 1], w["L0_tok_cls_token"].rearrange("a b d -> (a b) d"), "ld_tok")
            for n, (lo, hi) in zip("qkv", ((0, D), (D, D + HD), (D + HD, D + 2 * HD))):
                load(sp, wqkv0[:, :, lo:hi], w[f"L0_attn_W{n}"].rearrange("(k p) n -> p k n", k=2), "ld_att0")
                load(sp, bqkv0[:, lo:hi], rowb(w[f"L0_attn_b{n}"], TR), "ld_att0")
            for i, n in enumerate(("ln1_g", "ln1_b", "ln2_g", "ln2_b")):
                for k in range(2):
                    load(sp, lnv[:, i, k:k + 1], w[f"L0_attn_{n}"][KH * k:KH * k + KH].unsqueeze(1), "ld_small")
            for dst, src in (
                (wg0[:], w["L0_attn_Wg"].rearrange("(k p) n -> p k n", k=2)),
                (bg0[:], rowb(w["L0_attn_bg"], TR)),
                (w1s[:], w["L0_ffn_w1"].rearrange("(k p) n -> p k n", k=2)),
                (b1s[:], w["L0_ffn_b1"].unsqueeze(1)),
                (w2s[:], w["L0_ffn_w2"]),
                (b2s[:], rowb(w["L0_ffn_b2"], TR)),
                (gamma[:], rowb(w["L0_ffn_gamma"], TR)),
                (beta[:], rowb(w["L0_ffn_beta"], TR)),
                (wqkv1[:], w["L1_attn_w_qkv"].rearrange("(k p) n -> p k n", k=2)),
                (wpr1[:], w["L1_attn_w_proj"].rearrange("(k p) n -> p k n", k=2)),
                (bpr1[:], rowb(w["L1_attn_b_proj"], TR)),
                (temp[:], rowb(w["L1_attn_temperature"].rearrange("h a b -> (h a b)"), 128)),
                (nw[:], rowb(w["L1_ffn_norm_weight"], TR)),
                (slots[:], w["L1_ffn_slots"]),
                (slsc[:], w["L1_ffn_scale"].unsqueeze(1)),
            ):
                load(sp, dst, src, "ld_small")
            sp.wait_ge(sem("pads_zero"), 1)
            load(sp, b2pad[0:NE], w["L0_attn_b2"], "ld_b2")
            sp.wait_ge(sem("zeros"), 1)
            load(sp, order, consts[0:TR, NKEEP:], "ld_order")
            for u in range(2):
                load(sp, xsorted[u * NRT // 2 * RT:(u + 1) * NRT // 2 * RT].rearrange("(k p) d -> p k d", p=RT),
                     zeros.rearrange("p (k d) -> p k d", d=D), f"st_sorted_{u}")
            for u in range(2):
                down_load(sp, u, u)
                up_load(sp, u, u)
            for u in range(2):
                bias1_load(sp, u, u)
                bias2_load(sp, u, u)
            for q in range(QP):
                fc1_load(sp, 0, q, 0)
            for q in range(QP):
                fc2_load(sp, 0, q, 0)

            sp.wait_ge(sem("tile_expert"), 1)
            ex = [expert_of(sp, u) for u in range(2)]
            for u in range(2):
                w1_load(sp, u, ex[u])
            sp.wait_ge(sem("scattered"), 16 * TT)
            for u in range(2):
                load(sp, xs[:, u], xsorted[u * RT:u * RT + RT], f"ld_xs_{u}")
            for u in range(2):
                w2_load(sp, u, ex[u])
            with sp.Fori(0, NRT // 2 - 1) as p:
                ex = [expert_of(sp, p * 2 + (u + 2)) for u in range(2)]
                for u in range(2):
                    sp.wait_ge(sem("x_tp"), p * 2 + (u + 1))
                    load(sp, xs[:, u], xsorted[bass.ds((p * 2 + (u + 2)) * RT, RT)], f"ld_xs_{u}")
                for u in range(2):
                    sp.wait_ge(sem("up_mm"), p * 4 + (2 * u + 2))
                    w1_load(sp, u, ex[u])
                for u in range(2):
                    sp.wait_ge(sem("y_out"), p * 2 + (u + 3))
                    w2_load(sp, u, ex[u])
                    load(sp, ysorted[bass.ds((p * 2 + u) * RT, RT)], ys[:, u], f"st_sorted_{u}")
            for u in range(2):
                sp.wait_ge(sem("y_out"), NRT + u + 1)
                load(sp, ysorted[(NRT - 2 + u) * RT:(NRT - 1 + u) * RT], ys[:, u], f"st_sorted_{u}")

            with sp.Fori(0, NE // 2 - 1) as e2:
                for u in range(2):
                    e = e2 * 2 + u
                    sp.wait_ge(sem("ffn_z"), e * 4 + 4)
                    down_load(sp, u, e + 2)
                    sp.wait_ge(sem("ffn_y_mm"), e * TT + TT)
                    up_load(sp, u, e + 2)

            sp.wait_ge(sem("ffn_y_mm"), TT * NE)
            for q in range(QP):
                fc1_load(sp, 1, q, 1)
            replicate_v(sp)
            gather_heads(sp)
            for u in range(2):
                sp.wait_ge(sem(f"gather{u}"), 16 * PAIRS)
            for q in range(QP):
                fc2_load(sp, 1, q, 1)

            with sp.Fori(0, NG // 2 - 1) as g2:
                for u in range(2):
                    g = g2 * 2 + u
                    sp.wait_ge(sem("fc1_used"), g + 2)
                    bias1_load(sp, u, g + 2)
                    for q in range(QP):
                        fc1_load(sp, u, q, g + 2)
                    sp.wait_ge(sem("fc2_used"), g + 1)
                    bias2_load(sp, u, g + 2)
                    for q in range(QP):
                        fc2_load(sp, u, q, g + 2)

            full = (TT - 1) * TR
            rows = out.rearrange("b s d -> (b s) d")
            for j in range(TT // 2):
                sp.wait_ge(sem("out_ready"), j + 1)
                n = 2 if j < TT // 2 - 1 else 1
                load(sp, rows[2 * j * TR:(2 * j + n) * TR].rearrange("(t p) d -> p t d", p=TR),
                     h[:, 2 * j:2 * j + n, :], "stored")
            load(sp, rows[full:NTOK], h[0:LAST, TT - 1, :], "stored")
            sp.wait_ge(sem("stored"), 16 * (TT // 2 + 1))

        def embed(pe, mm, k):
            for v in range(2):
                pe.wait_ge(sem(f"patches_copied{v}"), k + 1)
            for m in range(2):
                for n in range(2):
                    ins = mm(ps[0:KH, 4 + 2 * m + n, 0:288], wproj[:, k, KH * m:KH * m + KH],
                             patT[:, k, 288 * n:288 * n + 288], k == 0, k == KT - 1)
                    if k == KT - 1:
                        ins.then_inc(sem("emb_mm"), 1)

        @block.tensor
        def _(pe):
            idn = ident

            def mm(o, l, r, start=True, stop=True, **k):
                return pe.matmul(o, l, r, start=start, stop=stop, **k)

            def to_features(name, src):
                for j in range(TT // 2):
                    for i in range(2):
                        tt = 2 * j + i
                        pe.wait_ge(sem("rows"), TT * NORM[name] + tt + 1)
                        for c in range(2):
                            ins = pe.transpose(ps[0:KH, j, 256 * c + TR * i:256 * c + TR * i + TR],
                                               src[:, tt, KH * c:KH * c + KH], idn[0:TR, 0:TR])
                    ins.then_inc(sem("tp"), 1)

            def projection_columns(j):
                last = min(IPT * (2 * j + 2), B) // 2
                for u in range(2):
                    pe.wait_ge(sem(f"gather{u}"), 32 * (last // 2))
                for i in range(2):
                    for c in range(2):
                        ins = pe.transpose(ps[0:KH, j, 256 * c + TR * i:256 * c + TR * i + TR],
                                           t[:, 2 * j + i, KH * c:KH * c + KH], idn[0:TR, 0:TR])
                ins.then_inc(sem("tp"), 1)

            def projection(j):
                pe.wait_ge(sem("cols"), 3 * TURN["proj"] + j + 1)
                for i in range(2):
                    tt = 2 * j + i
                    for k in range(2):
                        ins = mm(ps[0:TR, PROJ_BANK[j], D * i:D * i + D], xT[:, k, TR * tt:TR * tt + TR],
                                 wpr1[:, k, :], k == 0, k == 1)
                ins.then_inc(sem("proj_mm"), 1)

            def keys_queries(n, parts=range(4)):
                for i in parts:
                    m = (i + 2) % 4
                    for k in range(2):
                        ins = mm(ps[0:KH, 3 * n + i, 0:NH], wqkv1[:, k, KH * m:KH * m + KH],
                                 xT[:, k, NH * n:NH * n + NH], k == 0, k == 1)
                    ins.then_inc(sem("qk1_mm"), 1)

            def attention():
                def scores(j):
                    pe.wait_ge(sem("kblk"), j + 1)
                    if j >= 3:
                        pe.wait_ge(sem("s_read"), j - 2)
                    for c in range(2):
                        for i in range(2):
                            b = 2 * j + i
                            ins = mm(ps[64 * i:64 * i + 64, j % 3, HW * c:HW * c + HW],
                                     qT[:, c, S * b:S * b + 64], kblk[:, j % 2, c, i, :])
                    ins.then_inc(sem("s_mm"), 1)

                def transposes(j):
                    pe.wait_ge(sem("exp"), j + 1)
                    if j >= 2:
                        pe.wait_ge(sem("pT"), j - 1)
                    for g in range(4):
                        ins = pe.transpose(ps[0:TR, 3 + j % 2, 128 * g:128 * g + 128],
                                           sc[:, j % 3, TR * g:TR * g + TR], idn)
                    ins.then_inc(sem("pT_mm"), 1)

                def outputs(j):
                    pe.wait_ge(sem("pT"), j + 1)
                    pe.wait_ge(sem("vblk"), j + 1)
                    if j >= 2:
                        pe.wait_ge(sem("o_ready"), j - 1)
                    for g in range(4):
                        for i in range(2):
                            n = (64, S)[i]
                            ins = mm(ps[64 * i:64 * i + n, 5 + j % 2, 51 * g:51 * g + 51],
                                     pT[:, j % 2, 128 * g + 64 * i:128 * g + 64 * i + n],
                                     vblk[:, j % 2, 4 * i + g, :])
                    ins.then_inc(sem("o_mm"), 1)

                pe.wait_ge(sem("qk1"), 4)
                scores(0)
                scores(1)
                keys_queries(1)
                pe.wait_ge(sem("qk1"), 8)
                for j in range(PAIRS + 1):
                    if j + 2 < PAIRS:
                        scores(j + 2)
                    if j < PAIRS:
                        transposes(j)
                    if j == PAIRS:
                        projection_columns(0)
                    if j >= 1:
                        outputs(j - 1)

            pe.wait_ge(sem("ld_cst"), 16)
            for k in range(KT):
                for v in range(2):
                    n = 2 * k + v
                    pe.wait_ge(sem(f"patches_rows{v}"), (128 * k + 127) // (PDIM // XP) + 1)
                    if n >= 4:
                        pe.wait_ge(sem(f"patches_copied{v}"), k - 1)
                    for i in range(3):
                        ins = pe.transpose(ps[:, n % 4, KH * i:KH * i + KH],
                                           patches[:, 3 * v + i, 128 * k:128 * k + 128], idn[0:KH, 0:KH])
                    ins.then_inc(sem("patches_tp"), 1)
                if k == 0:
                    pe.wait_ge(sem("ld_wproj"), 16)
                if k >= 1:
                    embed(pe, mm, k - 1)
            embed(pe, mm, KT - 1)
            pe.wait_ge(sem("emb_cols"), 4)
            for j in range(TT // 2):
                for i in range(2):
                    for c in range(2):
                        ins = pe.transpose(ps[0:TR, j, D * i + KH * c:D * i + KH * c + KH],
                                           xT[:, c, TR * (2 * j + i):TR * (2 * j + i) + TR], idn[0:KH, 0:KH])
                ins.then_inc(sem("emb_tp"), 1)

            to_features("ln1", t)
            pe.wait_ge(sem("ld_att0"), 16 * N_ATT0)
            W3 = D + 2 * HD
            for tt in range(TT):
                pe.wait_ge(sem("cols"), 3 * TURN["ln1"] + tt // 2 + 1)
                for k in range(2):
                    ins = mm(ps[0:TR, 3 + tt // 2, W3 * (tt % 2):W3 * (tt % 2) + W3],
                             xT[:, k, TR * tt:TR * tt + TR], wqkv0[:, k, :], k == 0, k == 1)
                if tt % 2:
                    ins.then_inc(sem("qkv0_mm"), 1)

            to_features("ln2", t)
            for tt in range(TT):
                pe.wait_ge(sem("cols"), 3 * TURN["ln2"] + tt // 2 + 1)
                for k in range(2):
                    ins = mm(ps[0:TR, 6, NE * tt:NE * tt + NE], xT[:, k, TR * tt:TR * tt + TR], wg0[:, k, :],
                             k == 0, k == 1)
            ins.then_inc(sem("gate_mm"), 1)
            pe.wait_ge(sem("ld_order"), 16)
            pe.wait_ge(sem("onehot"), 1)
            mm(ps[0:TR, 5, 0:TT * NE], ones, oh[:].rearrange("p t e -> p (t e)")).then_inc(sem("total_mm"), 1)
            ins = mm(ps[0:TR, 6, TT * NE:2 * TT * NE], before, oh[:].rearrange("p t e -> p (t e)"))
            ins.then_inc(sem("count_mm"), 1)
            for tt in range(TT):
                ins = pe.transpose(ps[0:NE, 7 if tt < 4 else 3, TR * (tt % 4):TR * (tt % 4) + TR], oh[:, tt, :],
                                   idn[0:TR, 0:TR])
            ins.then_inc(sem("ohT_tp"), 1)
            pe.wait_ge(sem("ohT"), 2)
            pe.wait_ge(sem("ld_b2"), 16)
            for tt in range(TT):
                ins = mm(ps[0:TR, tt // 2, D * (tt % 2):D * (tt % 2) + D], ohT[:, TR * tt:TR * tt + TR], b2pad[:])
            ins.then_inc(sem("b2_mm"), 1)
            pe.wait_ge(sem("slots_rows"), 1)
            for c in range(2):
                ins = pe.transpose(ps[0:KH, 7, SLOTS * c:SLOTS * c + SLOTS], slots[:, KH * c:KH * c + KH],
                                   idn[0:SLOTS, 0:SLOTS])
            ins.then_inc(sem("slots_tp"), 1)
            pe.wait_ge(sem("slT"), 1)

            def x_transposes(u):
                for k in range(2):
                    ins = pe.transpose(ps[0:KH, 2 * u + 1, RT * k:RT * k + RT], xs[:, u, KH * k:KH * k + KH], idn)
                ins.then_inc(sem("x_tp"), 1)

            def tile_pair(p, last):
                for u in range(2):
                    pe.wait_ge(sem(f"ld_w1_{u}"), p * 32 + 32)
                    pe.wait_ge(sem("xk"), p * 2 + (u + 1))
                    pe.wait_ge(sem("y_out"), p * 2 + (u + 1))
                    for n in range(2):
                        for k in range(2):
                            rows = KH + 1 - k
                            ins = mm(ps[:, 2 * u + n, 0:384], xk[0:rows, u, k, :],
                                     w1r[0:rows, u, k, 384 * n:384 * n + 384], k == 0, k == 1)
                        ins.then_inc(sem("up_mm"), 1)
                for u in range(2):
                    for n in range(2):
                        pe.wait_ge(sem("gelu"), p * 4 + (2 * u + n + 1))
                        for m in range(3):
                            ins = pe.transpose(ps[:, 4 + 2 * u + n, 128 * m:128 * m + 128],
                                               hs[:, u, 384 * n + 128 * m:384 * n + 128 * m + 128], idn)
                        ins.then_inc(sem("h_tp"), 1)
                    if not last:
                        pe.wait_ge(sem(f"ld_xs_{u}"), p * 16 + 32)
                        x_transposes(u)
                for u in range(2):
                    pe.wait_ge(sem(f"ld_w2_{u}"), p * 16 + 16)
                    pe.wait_ge(sem("hk0"), p * 2 + (u + 1))
                    pe.wait_ge(sem("hk1"), p * 2 + (u + 1))
                    for m in range(FT):
                        ins = mm(ps[:, 2 * u, 0:D], hk[:, u, m, :], w2r[:, u, m, :], m == 0, m == FT - 1)
                    ins.then_inc(sem("moe_y_mm"), 1)

            pe.wait_ge(sem("y_out"), 2)
            for u in range(2):
                pe.wait_ge(sem(f"ld_xs_{u}"), 16)
                x_transposes(u)
            with pe.Fori(0, NRT // 2 - 1) as p:
                tile_pair(p, False)
            tile_pair(NRT // 2 - 1, True)

            to_features("ffn", a)
            for n in range(2):
                pe.wait_ge(sem("cols"), 3 * TURN["ffn"] + n + 2)
                for k in range(2):
                    ins = mm(ps[0:KH, 6 + n, 0:NH], w1s[:, k, :], xT[:, k, NH * n:NH * n + NH], k == 0, k == 1)
            ins.then_inc(sem("router_mm"), 1)

            def hidden(u, e2, after):
                pe.wait_ge(sem(f"ld_down_{u}"), e2 * 32 + 32)
                if after is not None:
                    pe.wait_ge(sem("ffn_z"), after)
                for j in range(ZT):
                    for n in range(2):
                        for k in range(2):
                            ins = mm(ps[:, 2 * j + n, 0:NH], downr[:, u, k, j:DZ:ZT], xT[:, k, NH * n:NH * n + NH],
                                     k == 0, k == 1)
                        ins.then_inc(sem("ffn_z_mm"), 1)

            def expert_pair(e2, last):
                for u in range(2):
                    e = e2 * 2 + u
                    if not (last and u):
                        hidden(1 - u, e2 + u, e * 4 + 4)
                    pe.wait_ge(sem("ffn_z"), e * 4 + 4)
                    pe.wait_ge(sem(f"ld_up_{u}"), e2 * 16 + 16)
                    for tt in range(TT):
                        if tt >= 2:
                            pe.wait_ge(sem("ffn_y"), e * TT + tt)
                        else:
                            pe.wait_ge(sem("ffn_y"), e * TT + 1)
                        for j in range(ZT):
                            ins = mm(ps[0:TR, 4 + tt % 2, 0:D], zT[u][:, j, TR * tt:TR * tt + TR], upr[:, u, j, :],
                                     j == 0, j == ZT - 1)
                        ins.then_inc(sem("ffn_y_mm"), 1)

            hidden(0, 0, None)
            pe.wait_ge(sem("router_h"), 2)
            for tt in range(TT):
                ins = mm(ps[0:TR, 6, NE * tt:NE * tt + NE], rT[:, TR * tt:TR * tt + TR], w2s[:])
            ins.then_inc(sem("logits_mm"), 1)
            with pe.Fori(0, NE // 2 - 1) as e2:
                expert_pair(e2, False)
            expert_pair(NE // 2 - 1, True)

            to_features("ln3", t)
            pe.wait_ge(sem("cols"), 3 * TURN["ln3"] + 2)
            keys_queries(0, (0, 1))
            for tt in range(TT):
                pe.wait_ge(sem("cols"), 3 * TURN["ln3"] + tt // 2 + 1)
                for k in range(2):
                    ins = mm(ps[0:TR, 4 + tt // 2, D * (tt % 2):D * (tt % 2) + D], xT[:, k, TR * tt:TR * tt + TR],
                             wqkv1[:, k, 2 * D:3 * D], k == 0, k == 1)
                if tt % 2:
                    ins.then_inc(sem("v1_mm"), 1)
            keys_queries(0, (2, 3))
            pe.wait_ge(sem("v_ready"), TT)
            attention()
            projection_columns(1)
            projection(0)
            projection_columns(2)
            projection(1)
            projection(2)

            pe.wait_ge(sem("var"), 2 * VARIANCE["tok0"] + 2)
            for j in range(3):
                ins = mm(ps[0:TR, 5 + j, 0:2 * D], idn[0:TR, 0:TR],
                         h[:, 2 * j:2 * j + 2, :].rearrange("p a b -> p (a b)"), True, False, skip_group_check=True)
                if j < 2:
                    ins.then_inc(sem(("cm_tp", "fc1_used")[j]), 1)

            to_features("tok", t)
            pe.wait_ge(sem("slT"), 1)
            for n in range(2):
                pe.wait_ge(sem("cols"), 3 * TURN["tok"] + n + 2)
                for k in range(2):
                    ins = mm(ps[SLOTS * n:SLOTS * n + SLOTS, n, 0:NH], slT[:, k, 0:SLOTS], xT[:, k, NH * n:NH * n + NH], k == 0, k == 1)
                ins.then_inc(sem("disp_mm"), 1)
            pe.wait_ge(sem("logits"), 2)
            for tt in range(TT):
                ins = pe.transpose(ps[0:TR, 3, SLOTS * tt:SLOTS * tt + SLOTS], hid[0:SLOTS, TR * tt:TR * tt + TR],
                                   idn[0:SLOTS, 0:SLOTS])
            ins.then_inc(sem("comb_mm"), 1)
            sel = const("sel")

            def hidden_bias(u, loads):
                pe.wait_ge(sem(f"ld_fb1_{u}"), loads)
                for n in range(2):
                    mm(ps[:, n, 0:384], sel, fb1[:, u, 384 * n:384 * n + 384], True, False, skip_group_check=True)

            hidden_bias(0, 16)
            pe.wait_ge(sem("disp"), 1)
            for tt in range(TT):
                ins = pe.transpose(ps[0:TR, 4, SLOTS * tt:SLOTS * tt + SLOTS], disp[:, TR * tt:TR * tt + TR],
                                   idn[0:SLOTS, 0:SLOTS])
            ins.then_inc(sem("disp_tp"), 1)
            pe.wait_ge(sem("comb_sub"), 1)
            for c in range(3):
                for tt in range(TT):
                    n = IPT if tt < TT - 1 else 1
                    if c == 0:
                        pe.wait_ge(sem("dm"), tt // 2 + 1)
                    for par in range(2):
                        ins = mm(ps[64 * par:64 * par + 64, 2 + c, 96 * tt:96 * tt + 32 * n],
                                 a[:, tt, c:D:3], dmt[:, tt, 0:n, par:SLOTS:2])
                ins.then_inc(sem("y_mm"), 1)
            pe.wait_ge(sem("y_copied"), 6)

            def group_pair(g2, last):
                for u in range(2):
                    g = g2 * 2 + u
                    pe.wait_ge(sem("yg"), g + 1)
                    for q in range(QP):
                        pe.wait_ge(sem(f"ld_fc1_{u}_{q}"), g2 * 16 + 16)
                    for c in range(3):
                        for n in range(2):
                            for q in range(QP):
                                ins = mm(ps[32 * q:32 * q + 32, n, 0:384], yg[:, u, c, q, :],
                                         fc1v[:, u, q, c, 384 * n:384 * n + 384], False, c == 2,
                                         skip_group_check=True)
                    ins.then_inc(sem("fc1_used"), 1)
                    pe.wait_ge(sem("xe"), g + 1)
                    for tt in range(TT):
                        ins = pe.transpose(ps[:, 3 + tt // 3, TR * (tt % 3):TR * (tt % 3) + TR],
                                           xe[:, tt].rearrange("p s b -> p (s b)"), idn[0:TR, 0:TR])
                    ins.then_inc(sem("cm_tp"), 1)
                    pe.wait_ge(sem("hid"), g * 2 + 2)
                    pe.wait_ge(sem("cmT"), g * 2 + 2)
                    for m in range(FT):
                        ins = pe.transpose(ps[:, 3 + m // 3, 128 * (m % 3):128 * (m % 3) + 128], hid[:, m:FF:FT], idn)
                        if m % 3 == 2:
                            ins.then_inc(sem("hidT_tp"), 1)
                    pe.wait_ge(sem(f"ld_fb2_{u}"), g2 * 16 + 16)
                    mm(ps[:, 2, 0:D], sel, fb2[:, u], True, False, skip_group_check=True)
                    pe.wait_ge(sem("hidT"), g * 4 + 4)
                    for pairs in ((0, 1), (2, 3)) if last and u else (range(QP),):
                        for q in pairs:
                            pe.wait_ge(sem(f"ld_fc2_{u}_{q}"), g2 * 32 + 32)
                        for m in range(FT):
                            for par in range(2):
                                for q in pairs:
                                    ins = mm(ps[32 * q:32 * q + 32, 2, 0:D], hidT[:, m, par, 32 * q:32 * q + 32],
                                             fc2v[:, u, 2 * q + par, m, :], False, m == FT - 1 and par == 1,
                                             skip_group_check=True)
                    ins.then_inc(sem("fc2_used"), 1)
                    if not (last and u):
                        hidden_bias(1 - u, (g2 + u) * 16 + 16)
                    pe.wait_ge(sem("yslot"), g + 1)
                    for tt in range(TT):
                        ins = mm(ps[0:TR, 5 + tt // 2, D * (tt % 2):D * (tt % 2) + D], cmT[:, TR * tt:TR * tt + TR],
                                 yslot[:], False, False, skip_group_check=True)
                        if last and u and tt % 2:
                            ins.then_inc(sem("combined"), 1)

            with pe.Fori(0, NG // 2 - 1) as g2:
                group_pair(g2, False)
            group_pair(NG // 2 - 1, True)

        class Steps:

            def __init__(self, eng, name):
                self.eng, self.sem, self.n = eng, sem(name), 0

            def __call__(self, ins):
                self.n += 1
                ins.then_inc(self.sem, 1)
                self.eng.wait_ge(self.sem, self.n)

        @block.vector
        def _(dve):
            step = Steps(dve, "dve_step")

            def stats(src, done=0):
                for half in HALVES:
                    ins = None
                    for tt in half:
                        if tt >= done:
                            ins = dve.bn_stats(st[:, tt, :], src[:, tt, :])
                    if ins is not None:
                        step(ins)
                    for tt in half:
                        ins = dve.bn_aggr(mv[:, tt, :], st[:, tt, :])
                    ins.then_inc(sem("var"), 1)

            def normalise(name, src, dst, done=0, r=None):
                r = rs if r is None else r
                stats(src, done)
                for i, half in enumerate(HALVES):
                    dve.wait_ge(sem("var"), 2 * VARIANCE[name] + i + 1)
                    dve.wait_ge(sem("rstd"), 2 * ROOT[name] + i + 1)
                    for tt in half:
                        dve.tensor_scalar(dst[:, tt, :], src[:, tt, :], mv[:, tt, 0:1], r[:, tt:tt + 1],
                                          ALU.subtract, ALU.mult).then_inc(sem("rows"), 1)
                dve.wait_ge(sem("rows"), TT * NORM[name] + TT)

            def attention():
                def before(j):
                    dve.wait_ge(sem("s_mm"), j + 1)
                    v = ps[:, j % 3, 0:HEADS * S].rearrange("p (h n) -> p h n", h=HEADS)
                    o = sc[:, j % 3, :].rearrange("p (h n) -> p h n", h=HEADS)
                    if j >= 3:
                        dve.wait_ge(sem("pT_mm"), j - 2)
                    dve.tensor_tensor(o, v, dmask[:], ALU.mult).then_inc(sem("s_read"), 1)
                    dve.wait_ge(sem("s_read"), j + 1)
                    step(dve.tensor_reduce(mx[:, j % 2, :], o, X, ALU.max))
                    dve.tensor_tensor(o, o, bcast(mx[:, j % 2, :], 2, S), ALU.subtract).then_inc(sem("s_sub"), 1)

                def after(j):
                    dve.wait_ge(sem("o_mm"), j + 1)
                    v = ps[0:101, 5 + j % 2, 0:204].rearrange("p (h d) -> p h d", h=HEADS)
                    step(dve.reciprocal(den[0:101, j % 2, :], v[:, :, HD:HD + 1].rearrange("p h o -> p (h o)")))
                    if j >= 2:
                        dve.wait_ge(sem(f"gather{j % 2}"), 32 * (j // 2))
                    dve.tensor_tensor(ob[0:101, j % 2, :].rearrange("p (h d) -> p h d", h=HEADS), v[:, :, 0:HD],
                                      bcast(den[0:101, j % 2, :], 2, HD), ALU.mult).then_inc(sem("o_ready"), 1)

                before(0)
                before(1)
                for j in range(PAIRS + 1):
                    if j + 2 < PAIRS:
                        before(j + 2)
                    if j >= 1:
                        after(j - 1)
                for u in range(2):
                    dve.wait_ge(sem(f"gather{u}"), 16 * PAIRS)

            def first_max(src, mask):
                step(dve.tensor_reduce(m6[:, 0, :], src[:], X, ALU.max))
                step(dve.tensor_tensor(mask, src[:], bcast(m6[:, 0, :], 2, NE), ALU.is_equal))
                step(dve.tensor_tensor(key[:], mask, bcast(const("rev", TR), 1, TT), ALU.mult))
                step(dve.tensor_reduce(m6[:, 0, :], key[:], X, ALU.max))
                step(dve.tensor_tensor(mask, key[:], bcast(m6[:, 0, :], 2, NE), ALU.is_equal))

            for k in range(KT):
                if k < XP:
                    dve.wait_ge(sem(f"ld_x{k}"), 16)
                    dve.tensor_copy(patch_rows(k, 0), image_rows(k, 0)).then_inc(sem("patches_rows0"), 1)
                dve.wait_ge(sem("patches_tp"), 2 * k + 1)
                dve.tensor_copy(patT[:, k, 0:288], ps[:, (2 * k) % 4, 0:288]).then_inc(sem("patches_copied0"), 1)
            dve.wait_ge(sem("ld_tok"), 16 * 9)
            step(dve.tensor_tensor(posr[:], posr[:], addr[:], ALU.add))
            dve.wait_ge(sem("emb_mm"), 2)
            dve.wait_ge(sem("pads_zero"), 1)
            for n in range(2):
                dve.tensor_copy(emb_out(0, n), emb_in(0, n)).then_inc(sem("emb_cols"), 1)
            for j in range(TT // 2):
                dve.wait_ge(sem("emb_tp"), j + 1)
                ins = dve.tensor_tensor(h[:, 2 * j:2 * j + 2, :],
                                        ps[0:TR, j, 0:2 * D].rearrange("p (i d) -> p i d", i=2),
                                        bcast(posr[:], 1, 2), ALU.add)
            step(ins)
            normalise("ln1", h, t, r=rs2)
            dve.wait_ge(sem("rstd"), 2 * ROOT["in0"] + 2)
            for tt in range(TT):
                dve.tensor_scalar(a[:, tt, :], h[:, tt, :], mv[:, tt, 0:1], rs[:, tt:tt + 1],
                                  ALU.subtract, ALU.mult)
            dve.wait_ge(sem("ld_small"), 16 * N_SMALL)
            step(dve.bn_stats(sst[:, 0:6], slots[:]))
            step(dve.bn_aggr(sst[:, 6:8], sst[:, 0:6]))
            step(dve.tensor_tensor(sst[:, 8:9], sst[:, 6:7], sst[:, 6:7], ALU.mult))
            dve.tensor_tensor(sst[:, 9:10], sst[:, 8:9], sst[:, 7:8], ALU.add).then_inc(sem("var"), 2)
            step(dve.tensor_tensor(dmask[:], bcast(const("eye"), 1, HEADS), bcast(temp[:], 2, S), ALU.mult))
            step(dve.tensor_scalar(dmask[:], dmask[:], -1.0, 1.0, ALU.mult, ALU.add))
            for j in range(TT // 2):
                dve.wait_ge(sem("qkv0_mm"), j + 1)
                if j == 0:
                    dve.wait_ge(sem("ld_att0"), 16 * N_ATT0)
                dve.tensor_tensor(qkv[:, 2 * j:2 * j + 2, :],
                                  ps[0:TR, 3 + j, 0:448].rearrange("p (i d) -> p i d", i=2),
                                  bcast(bqkv0[:], 1, 2), ALU.add).then_inc(sem("qkv0"), 1)
            dve.wait_ge(sem("qkv0"), TT // 2)

            def heads(ap, n):
                return ap.rearrange("p t (h e) -> p t h e", h=n)

            half = HD // 2

            def table(name, lo, hi):
                return bcast(const(name, TR)[:, lo:hi], 1, TT)

            k0 = qkv[:, :, D:D + HD]
            dve.tensor_tensor(krot, k0, table("cos", 0, HD), ALU.mult)
            dve.tensor_tensor(ktmp[:, :, 0:half], k0[:, :, half:HD], table("sin", 0, half), ALU.mult)
            step(dve.tensor_tensor(ktmp[:, :, half:HD], k0[:, :, 0:half], table("sin", half, HD), ALU.mult))
            step(dve.tensor_tensor(krot, krot, ktmp, ALU.add))
            dve.tensor_tensor(kq, krot, table("cos", 0, HD), ALU.mult)
            step(dve.tensor_tensor(ktmp, krot, table("sin", 0, HD), ALU.mult))
            dve.tensor_tensor(kq[:, :, 0:half], kq[:, :, 0:half], ktmp[:, :, half:HD], ALU.add)
            step(dve.tensor_tensor(kq[:, :, half:HD], kq[:, :, half:HD], ktmp[:, :, 0:half], ALU.add))
            q4 = heads(t[:], HEADS)
            step(dve.tensor_tensor(q4, heads(qkv[:, :, 0:D], HEADS), bcast(kq, 2, HEADS), ALU.mult))
            step(dve.tensor_reduce(s0[:, 0], q4, X, ALU.add))
            step(dve.tensor_tensor(s0[:, 1], s0[:, 0], s0[:, 0], ALU.max))
            dve.tensor_tensor(s0[:, 0], s0[:, 0], s0[:, 1], ALU.subtract).then_inc(sem("s0_sub"), 1)
            dve.wait_ge(sem("s0_exp"), 1)
            step(dve.tensor_scalar(s0[:, 1], s0[:, 0], float(HEADS), None, ALU.mult))
            step(dve.reciprocal(s0[:, 1], s0[:, 1]))
            step(dve.scalar_tensor_tensor(out=s0[:, 0], in0=s0[:, 0], scalar=float(HEADS), in1=s0[:, 1],
                                          op0=ALU.mult, op1=ALU.mult))
            step(dve.tensor_tensor(q4, bcast(s0[:, 0], 3, HD), bcast(qkv[:, :, D + HD:D + 2 * HD], 2, HEADS), ALU.mult))
            step(dve.tensor_tensor(a[:], a[:], t[:], ALU.add))

            normalise("ln2", a, t)
            dve.wait_ge(sem("rstd"), 2 * ROOT["slots"] + 2)
            dve.tensor_scalar(slots[:], slots[:], sst[:, 10:11], slsc[:, 0:1], ALU.mult, ALU.mult)\
                .then_inc(sem("slots_rows"), 1)

            dve.wait_ge(sem("gate_mm"), 1)
            step(dve.tensor_tensor(lg[:], ps[0:TR, 6, 0:TT * NE].rearrange("p (t e) -> p t e", t=TT),
                                   bcast(bg0[:], 1, TT), ALU.add))
            first_max(lg, oh[:])
            dve.tensor_scalar(oh[:, TT - 1, :], oh[:, TT - 1, :], const("valid", TR), None, ALU.mult)\
                .then_inc(sem("onehot"), 1)
            dve.wait_ge(sem("total_mm"), 1)
            step(dve.tensor_copy(run[:, 1:TT + 1], ps[0:TR, 5, 0:TT * NE].rearrange("p (t e) -> p t e", t=TT)))
            for tt in range(2, TT + 1):
                step(dve.tensor_tensor(run[:, tt], run[:, tt], run[:, tt - 1], ALU.add))
            step(dve.tensor_tensor(count, bcast(run[:, TT], 2, LEVELS), bcast(const("level", TR), 1, NE), ALU.is_gt))
            step(dve.tensor_reduce(ntile[:, 0, :], count, X, ALU.add))
            step(dve.tensor_tensor(below, bcast(ntile[:, 0, :], 1, NE),
                                   const("lower", TR).rearrange("p (a b) -> p a b", a=NE), ALU.mult))
            step(dve.tensor_reduce(ntile[:, 1, :], below, X, ALU.add))
            dve.tensor_tensor(ntile[:, 2, :], ntile[:, 0, :], ntile[:, 1, :], ALU.add)
            dve.wait_ge(sem("count_mm"), 1)
            step(dve.tensor_tensor(run[:, 0:TT], run[:, 0:TT],
                                   ps[0:TR, 6, TT * NE:2 * TT * NE].rearrange("p (t e) -> p t e", t=TT), ALU.add))
            step(dve.scalar_tensor_tensor(out=prow, in0=bcast(ntile[:, 1, :], 1, TT), scalar=float(RT),
                                          in1=run[:, 0:TT], op0=ALU.mult, op1=ALU.add))
            dve.tensor_tensor(owner, bcast(const("tile", 1), 2, NE), bcast(ntile[0:1, 2, :], 1, NRT), ALU.is_ge)
            step(dve.tensor_tensor(prow, prow, oh[:], ALU.mult))
            dve.tensor_reduce(owned, owner, X, ALU.add)
            step(dve.tensor_reduce(row_sum, prow, X, ALU.add))
            dve.tensor_copy(place[:], row_sum).then_inc(sem("place"), 1)
            dve.tensor_scalar(tile_expert[:], owned, float(NE - 1), None, ALU.min)\
                .then_inc(sem("tile_expert"), 1)
            dve.wait_ge(sem("ohT_tp"), 1)
            dve.wait_ge(sem("h_pads"), 1)
            dve.tensor_copy(ohT[0:NE, 0:4 * TR], ps[0:NE, 7, 0:4 * TR]).then_inc(sem("ohT"), 1)
            dve.tensor_copy(ohT[0:NE, 4 * TR:NPAD], ps[0:NE, 3, 0:2 * TR]).then_inc(sem("ohT"), 1)
            dve.wait_ge(sem("b2_mm"), 1)
            for j in range(TT // 2):
                ins = dve.tensor_tensor(a[:, 2 * j:2 * j + 2, :], a[:, 2 * j:2 * j + 2, :],
                                        ps[0:TR, j, 0:2 * D].rearrange("p (i d) -> p i d", i=2), ALU.add)
            ins.then_inc(sem("y_out"), 2)
            dve.wait_ge(sem("slots_tp"), 1)
            for i in range(2):
                ins = dve.tensor_copy(slT[:, :, SLOTS * i:SLOTS * i + SLOTS],
                                      ps[0:KH, 7, 0:2 * SLOTS].rearrange("p (c n) -> p c n", c=2))
            ins.then_inc(sem("slT"), 1)
            with dve.Fori(0, NRT // 2) as p:
                for u in range(2):
                    dve.wait_ge(sem("h_tp"), p * 4 + (2 * u + 2))
                    dve.tensor_copy(hk[:, u, 3:6, :].rearrange("p m n -> p (m n)"), ps[:, 5 + 2 * u, 0:384])\
                        .then_inc(sem("hk1"), 1)
                for u in range(2):
                    dve.wait_ge(sem("moe_y_mm"), p * 2 + (u + 1))
                    dve.wait_ge(sem(f"st_sorted_{u}"), p * 16 + 16)
                    dve.tensor_copy(ys[:, u], ps[:, 2 * u, 0:D]).then_inc(sem("y_out"), 1)

            def expert_pair(e2, last):
                for u in range(2):
                    e = e2 * 2 + u
                    dve.wait_ge(sem("ffn_y"), e * TT + 1)
                    dve.tensor_copy(gcol[:, u, :], gate[:, :, bass.ds(e, 1)].rearrange("p t o -> p (t o)"))\
                        .then_inc(sem("ffn_gcol"), 1)
                    dve.wait_ge(sem("ffn_gcol"), e + 1)
                    for tt in range(TT):
                        dve.wait_ge(sem("ffn_y_mm"), e * TT + (tt + 1))
                        dve.scalar_tensor_tensor(out=a[:, tt, :], in0=ps[0:TR, 4 + tt % 2, 0:D],
                                                 scalar=gcol[:, u, tt:tt + 1], in1=a[:, tt, :],
                                                 op0=ALU.mult, op1=ALU.add).then_inc(sem("ffn_y"), 1)
                        if last and u and tt:
                            dve.wait_ge(sem("ffn_y"), e * TT + 1 + tt)
                            dve.bn_stats(st[:, tt - 1, :], a[:, tt - 1, :])

            step(dve.tensor_tensor(h[:], h[:], a[:], ALU.add))
            for tt in range(TT):
                dve.wait_ge(sem(f"moe_back{tt}"), 16)
                dve.tensor_tensor(h[:, tt, :], h[:, tt, :], t[:, tt, :], ALU.add).then_inc(sem("moe_sum"), 1)
                if tt:
                    dve.wait_ge(sem("moe_sum"), tt)
                    dve.bn_stats(st[:, tt - 1, :], h[:, tt - 1, :])
            dve.wait_ge(sem("moe_sum"), TT)

            normalise("ffn", h, a, TT - 1)
            step(dve.tensor_tensor(h[:], h[:], bcast(beta[:], 1, TT), ALU.add))
            dve.wait_ge(sem("logits_mm"), 1)
            step(dve.tensor_tensor(lg[:], ps[0:TR, 6, 0:TT * NE].rearrange("p (t e) -> p t e", t=TT),
                                   bcast(b2s[:], 1, TT), ALU.add))
            step(dve.tensor_reduce(m6[:, 0, :], lg[:], X, ALU.max))
            dve.tensor_tensor(lg[:], lg[:], bcast(m6[:, 0, :], 2, NE), ALU.subtract).then_inc(sem("router_sub"), 1)
            dve.wait_ge(sem("router_exp"), 1)
            step(dve.tensor_reduce(m6[:, 0, :], lg[:], X, ALU.add))
            step(dve.reciprocal(m6[:, 1, :], m6[:, 0, :]))
            step(dve.tensor_tensor(lg[:], lg[:], bcast(m6[:, 1, :], 2, NE), ALU.mult))
            first_max(lg, oh[:])
            step(dve.scalar_tensor_tensor(out=gate[:], in0=oh[:], scalar=-4.0, in1=lg[:], op0=ALU.mult, op1=ALU.add))
            step(dve.tensor_reduce(m6[:, 0, :], gate[:], X, ALU.max))
            step(dve.tensor_tensor(gate[:], gate[:], bcast(m6[:, 0, :], 2, NE), ALU.is_equal))
            step(dve.tensor_tensor(key[:], gate[:], bcast(const("rev", TR), 1, TT), ALU.mult))
            step(dve.tensor_reduce(m6[:, 0, :], key[:], X, ALU.max))
            step(dve.tensor_tensor(gate[:], key[:], bcast(m6[:, 0, :], 2, NE), ALU.is_equal))
            step(dve.tensor_tensor(oh[:], oh[:], gate[:], ALU.add))
            step(dve.tensor_tensor(oh[:], oh[:], lg[:], ALU.mult))
            step(dve.tensor_reduce(m6[:, 0, :], oh[:], X, ALU.add))
            step(dve.tensor_scalar(m6[:, 0, :], m6[:, 0, :], 1e-8, None, ALU.add))
            step(dve.reciprocal(m6[:, 1, :], m6[:, 0, :]))
            dve.tensor_tensor(gate[:], oh[:], bcast(m6[:, 1, :], 2, NE), ALU.mult).then_inc(sem("ffn_y"), 1)
            with dve.Fori(0, NE // 2 - 1) as e2:
                expert_pair(e2, False)
            expert_pair(NE // 2 - 1, True)
            dve.wait_ge(sem("ffn_y"), NE * TT + 1)
            stats(a, TT - 1)
            dve.wait_ge(sem("var"), 2 * VARIANCE["u"] + 2)
            for tt in range(TT):
                ins = dve.scalar_tensor_tensor(out=t[:, tt, :], in0=a[:, tt, :], scalar=mv[:, tt, 0:1], in1=gamma[:],
                                               op0=ALU.subtract, op1=ALU.mult)
            step(ins)
            dve.wait_ge(sem("rstd"), 2 * ROOT["u"] + 2)
            for tt in range(TT):
                ins = dve.scalar_tensor_tensor(out=h[:, tt, :], in0=t[:, tt, :], scalar=rs[:, tt:tt + 1], in1=h[:, tt, :],
                                               op0=ALU.mult, op1=ALU.add)
            step(ins)

            normalise("ln3", h, t)
            for j in range(TT // 2):
                dve.wait_ge(sem("v1_mm"), j + 1)
                dve.tensor_copy(a[:, 2 * j:2 * j + 2, :], ps[0:TR, 4 + j, 0:2 * D].rearrange("p (i d) -> p i d", i=2))\
                    .then_inc(sem("v_ready"), 2)
            step(dve.tensor_tensor(h[:], h[:], bcast(bpr1[:], 1, TT), ALU.add))
            attention()
            for j in range(TT // 2):
                dve.wait_ge(sem("proj_mm"), j + 1)
                step(dve.tensor_tensor(h[:, 2 * j:2 * j + 2, :], h[:, 2 * j:2 * j + 2, :],
                                       ps[0:TR, PROJ_BANK[j], 0:2 * D].rearrange("p (i d) -> p i d", i=2), ALU.add))
                for tt in (2 * j, 2 * j + 1):
                    ins = dve.bn_stats(st[:, tt, :], h[:, tt, :])
            step(ins)

            stats(h, TT)
            dve.wait_ge(sem("var"), 2 * VARIANCE["tok0"] + 2)
            for tt in range(TT):
                dve.scalar_tensor_tensor(out=a[:, tt, :], in0=h[:, tt, :], scalar=mv[:, tt, 0:1], in1=nw[:],
                                         op0=ALU.subtract, op1=ALU.mult).then_inc(sem("centred"), 1)
            dve.wait_ge(sem("centred"), TT)
            for i, half in enumerate(HALVES):
                dve.wait_ge(sem("rstd"), 2 * ROOT["tok"] + i + 1)
                lo, hi = half[0], half[-1] + 1
                step(dve.scalar_tensor_tensor(out=rs3[:, lo:hi], in0=rs2[:, lo:hi], scalar=1e5, in1=m6[:, 3, lo:hi],
                                              op0=ALU.mult, op1=ALU.min))
                for tt in half:
                    dve.tensor_scalar(t[:, tt, :], a[:, tt, :], rs3[:, tt:tt + 1], None, ALU.mult)\
                        .then_inc(sem("rows"), 1)
            dve.wait_ge(sem("rows"), TT * NORM["tok"] + TT)
            dve.wait_ge(sem("squares"), TT)
            for tt in range(TT):
                ins = dve.tensor_scalar(a[:, tt, :], a[:, tt, :], rs2[:, tt:tt + 1], None, ALU.mult)
            step(ins)
            dve.wait_ge(sem("soft_zero"), 1)

            def by_image(ap):
                return ap.rearrange("p (b s) -> p b s", s=S)

            for n in range(2):
                dve.wait_ge(sem("logits"), n + 1)
                ins = dve.tensor_reduce(mxd[:, 0, 8 * n:8 * n + 8], by_image(hid[0:SLOTS, NH * n:NH * n + NH]), X, ALU.max)
            step(ins)
            for n in range(2):
                ins = dve.tensor_tensor(by_image(disp[:, NH * n:NH * n + NH]), by_image(hid[0:SLOTS, NH * n:NH * n + NH]),
                                        bcast(mxd[:, 0, 8 * n:8 * n + 8], 2, S), ALU.subtract)
            ins.then_inc(sem("disp_sub"), 1)
            dve.wait_ge(sem("comb_mm"), 1)
            cps = ps[0:TR, 3, 0:TT * SLOTS].rearrange("p (t s) -> p t s", t=TT)
            step(dve.tensor_reduce(mxc[:, 0, :], cps, X, ALU.max))
            dve.wait_ge(sem("disp_exp"), 1)
            dd = by_image(disp[:, 0:NTOK])
            step(dve.tensor_reduce(mxd[:, 0, :], dd, X, ALU.add))
            step(dve.reciprocal(mxd[:, 1, :], mxd[:, 0, :]))
            dve.tensor_tensor(dd, dd, bcast(mxd[:, 1, :], 2, S), ALU.mult).then_inc(sem("disp"), 1)
            dve.tensor_tensor(comb[:], cps, bcast(mxc[:, 0, :], 2, SLOTS), ALU.subtract).then_inc(sem("comb_sub"), 1)
            dve.wait_ge(sem("disp_tp"), 1)
            for j in range(TT // 2):
                tiles = slice(2 * j, 2 * j + 2)
                dve.tensor_tensor(dmt[:, tiles],
                                  bcast(ps[0:TR, 4, 0:TT * SLOTS].rearrange("p (t s) -> p t s", t=TT)[:, tiles], 2, IPT),
                                  bcast(bcast(const("vmask", TR), 1, 2), 3, SLOTS), ALU.mult).then_inc(sem("dm"), 1)
            dve.wait_ge(sem("comb_exp"), 1)
            step(dve.tensor_reduce(mxc[:, 0, :], comb[:], X, ALU.add))
            step(dve.reciprocal(mxc[:, 1, :], mxc[:, 0, :]))
            dve.tensor_tensor(comb[:], comb[:], bcast(mxc[:, 1, :], 2, SLOTS), ALU.mult).then_inc(sem("comb"), 1)
            for c in range(3):
                dve.wait_ge(sem("y_mm"), c + 1)
                dve.tensor_copy(ycmp[0:64, c], ps[0:64, 2 + c, :].rearrange("p (b j) -> p j b", b=B))\
                    .then_inc(sem("y_copied"), 1)
            with dve.Fori(0, NG) as g:
                dve.wait_ge(sem("cm_tp"), g + 2)
                dve.tensor_copy(cmT[:, 0:3 * TR], ps[:, 3, 0:3 * TR]).then_inc(sem("cmT"), 1)
                dve.wait_ge(sem("hidT_tp"), g * 2 + 1)
                for par in range(2):
                    dve.tensor_copy(hid_out(0, par), hid_in(0, par)).then_inc(sem("hidT"), 1)
                dve.wait_ge(sem("fc2_used"), g + 1)
                dve.tensor_copy(yslot[:], ps[:, 2, 0:D]).then_inc(sem("yslot"), 1)
            for j in range(TT // 2):
                dve.wait_ge(sem("combined"), j + 1)
                dve.tensor_copy(h[:, 2 * j:2 * j + 2, :],
                                ps[0:TR, 5 + j, 0:2 * D].rearrange("p (i d) -> p i d", i=2))\
                    .then_inc(sem("out_ready"), 1)

        @block.scalar
        def _(act):
            def columns(name, affine=None):
                for j in range(TT // 2):
                    act.wait_ge(sem("tp"), 3 * TURN[name] + j + 1)
                    lo, hi = 2 * TR * j, 2 * TR * j + 2 * TR
                    if affine is None:
                        act.activation(xT[:, :, lo:hi], ps[0:KH, j, :].rearrange("p (c n) -> p c n", c=2)[:, :, 0:2 * TR],
                                       ACT.Copy).then_inc(sem("cols"), 1)
                        continue
                    for c in range(2):
                        ins = act.activation(xT[:, c, lo:hi], ps[0:KH, j, 256 * c:256 * c + 2 * TR], ACT.Identity,
                                             scale=lnv[:, affine, c:c + 1], bias=lnv[:, affine + 1, c:c + 1])
                    ins.then_inc(sem("cols"), 1)

            def keys_queries(n):
                for i in range(4):
                    act.wait_ge(sem("qk1_mm"), 4 * n + i + 1)
                    dst = (kT, qT)[i // 2]
                    act.activation(dst[:, i % 2, NH * n:NH * n + NH], ps[0:KH, 3 * n + i, 0:NH], ACT.Copy)\
                        .then_inc(sem("qk1"), 1)

            def attention():
                def values(j):
                    if j >= 2:
                        act.wait_ge(sem("o_mm"), j - 1)
                    for x in range(IPT):
                        ins = act.activation(
                            vblk[:, j % 2, :, 17 * x:17 * x + HD],
                            vrep[:, 2 * j:2 * j + 2, :].rearrange("p i (g n) -> p (i g) n", g=4)[:, :, HD * x:HD * x + HD],
                            ACT.Identity, scale=const("vmask", TR)[:, x:x + 1])
                    ins.then_inc(sem("vblk"), 1)

                def exps(j):
                    act.wait_ge(sem("s_sub"), j + 1)
                    act.activation(sc[:, j % 3, :], sc[:, j % 3, :], ACT.Exp, scale=HD ** -0.5).then_inc(sem("exp"), 1)

                exps(0)
                keys_queries(1)
                exps(1)
                act.wait_ge(sem("v_ones"), 1)
                act.wait_ge(sem("vrep"), 16 * 9)
                values(0)
                for j in range(PAIRS):
                    if j + 2 < PAIRS:
                        exps(j + 2)
                    act.wait_ge(sem("pT_mm"), j + 1)
                    if j >= 2:
                        act.wait_ge(sem("o_mm"), j - 1)
                    act.activation(pT[:, j % 2, :], ps[0:TR, 3 + j % 2, :], ACT.Copy).then_inc(sem("pT"), 1)
                    if j + 1 < PAIRS:
                        values(j + 1)

            for k in range(KT):
                if k < XP:
                    act.wait_ge(sem(f"ld_x{k}"), 16)
                    act.activation(patch_rows(k, 1), image_rows(k, 1), ACT.Copy).then_inc(sem("patches_rows1"), 1)
                act.wait_ge(sem("patches_tp"), 2 * k + 2)
                act.activation(patT[:, k, 288:576], ps[:, (2 * k + 1) % 4, 0:288], ACT.Copy)\
                    .then_inc(sem("patches_copied1"), 1)
            act.wait_ge(sem("emb_mm"), 4)
            act.wait_ge(sem("pads_zero"), 1)
            for n in range(2):
                act.activation(emb_out(1, n), emb_in(1, n), ACT.Copy).then_inc(sem("emb_cols"), 1)

            act.wait_ge(sem("ld_small"), 16 * N_SMALL)
            columns("ln1", 0)
            act.wait_ge(sem("s0_sub"), 1)
            act.activation(s0[:, 0], s0[:, 0], ACT.Exp, scale=HD ** -0.5).then_inc(sem("s0_exp"), 1)
            columns("ln2", 2)

            def x_features(u, count):
                act.wait_ge(sem("x_tp"), count)
                for k in range(2):
                    ins = act.activation(xk[0:KH, u, k, :], ps[0:KH, 2 * u + 1, RT * k:RT * k + RT], ACT.Identity,
                                         scale=lnv[:, 2, k:k + 1], bias=lnv[:, 3, k:k + 1])
                ins.then_inc(sem("xk"), 1)

            def tile_pair(p, last):
                for u in range(2):
                    for n in range(2):
                        act.wait_ge(sem("up_mm"), p * 4 + (2 * u + n + 1))
                        act.activation(hs[:, u, 384 * n:384 * n + 384], ps[:, 2 * u + n, 0:384], ACT.Gelu)\
                            .then_inc(sem("gelu"), 1)
                for u in range(2):
                    act.wait_ge(sem("h_tp"), p * 4 + (2 * u + 1))
                    act.activation(hk[:, u, 0:3, :].rearrange("p m n -> p (m n)"), ps[:, 4 + 2 * u, 0:384], ACT.Copy)\
                        .then_inc(sem("hk0"), 1)
                    if not last:
                        x_features(u, p * 2 + (u + 3))

            act.wait_ge(sem("xk_ones"), 1)
            for u in range(2):
                x_features(u, u + 1)
            with act.Fori(0, NRT // 2 - 1) as p:
                tile_pair(p, False)
            tile_pair(NRT // 2 - 1, True)
            act.wait_ge(sem("h_pads"), 1)
            columns("ffn")
            act.wait_ge(sem("router_mm"), 1)
            for n in range(2):
                act.activation(rT[:, NH * n:NH * n + NH], ps[0:KH, 6 + n, 0:NH], ACT.Gelu, bias=b1s[:, 0:1])\
                    .then_inc(sem("router_h"), 1)

            def hidden(u, e2, e):
                act.wait_ge(sem(f"ld_down_{u}"), e2 * 32 + 32)
                for q in range(2 * ZT):
                    act.wait_ge(sem("ffn_z_mm"), e * 4 + (q + 1))
                    act.activation(zT[u][:, q // 2, NH * (q % 2):NH * (q % 2) + NH], ps[:, q, 0:NH], ACT.Gelu,
                                   bias=downb[:, u, q // 2:q // 2 + 1]).then_inc(sem("ffn_z"), 1)

            hidden(0, 0, 0)
            act.wait_ge(sem("router_sub"), 1)
            act.activation(lg[:], lg[:], ACT.Exp).then_inc(sem("router_exp"), 1)
            with act.Fori(0, NE // 2 - 1) as e2:
                hidden(1, e2, e2 * 2 + 1)
                hidden(0, e2 + 1, e2 * 2 + 2)
            hidden(1, NE // 2 - 1, NE - 1)
            columns("ln3")
            keys_queries(0)
            attention()
            columns("proj")
            for tt in range(TT):
                act.wait_ge(sem("centred"), tt + 1)
                act.activation(t[:, tt, :], a[:, tt, :], ACT.Square, accum_out=m6[:, 2, tt:tt + 1])\
                    .then_inc(sem("squares"), 1)
            columns("tok")
            act.wait_ge(sem("soft_zero"), 1)
            for n in range(2):
                act.wait_ge(sem("disp_mm"), n + 1)
                act.activation(hid[0:SLOTS, NH * n:NH * n + NH], ps[SLOTS * n:SLOTS * n + SLOTS, n, 0:NH], ACT.Copy)\
                    .then_inc(sem("logits"), 1)
            act.wait_ge(sem("disp_sub"), 1)
            act.activation(disp[:, 0:NTOK], disp[:, 0:NTOK], ACT.Exp).then_inc(sem("disp_exp"), 1)
            act.wait_ge(sem("comb_sub"), 1)
            act.activation(comb[:], comb[:], ACT.Exp).then_inc(sem("comb_exp"), 1)
            for c in range(3):
                act.wait_ge(sem("y_mm"), c + 1)
                act.activation(ycmp[64:128, c], ps[64:128, 2 + c, :].rearrange("p (b j) -> p j b", b=B), ACT.Copy)\
                    .then_inc(sem("y_copied"), 1)
            with act.Fori(0, NG) as g:
                act.wait_ge(sem("fc1_used"), g + 2)
                for n in range(2):
                    act.activation(hid[:, 384 * n:384 * n + 384], ps[:, n, 0:384], ACT.Gelu).then_inc(sem("hid"), 1)
                act.wait_ge(sem("cm_tp"), g + 2)
                act.activation(cmT[:, 3 * TR:NPAD], ps[:, 4, 0:3 * TR], ACT.Copy).then_inc(sem("cmT"), 1)
                act.wait_ge(sem("hidT_tp"), g * 2 + 2)
                for par in range(2):
                    act.activation(hid_out(1, par), hid_in(1, par), ACT.Copy).then_inc(sem("hidT"), 1)

        @block.gpsimd
        def _(pool):
            step = Steps(pool, "pool_step")

            def root(out_, factors, name):
                for i, half in enumerate(HALVES):
                    lo, hi = half[0], half[-1] + 1
                    pool.wait_ge(sem("var"), 2 * VARIANCE[name] + i + 1)
                    if ROOT[name]:
                        pool.wait_ge(sem("rstd"), 2 * ROOT[name])
                    step(pool.tensor_scalar(ve[:, lo:hi], mv[:, lo:hi, 1], *factors))
                    pool.tensor_tensor(out_[:, lo:hi], ve[:, lo:hi], const("mhalf", TR)[:, lo:hi], ALU.pow)\
                        .then_inc(sem("rstd"), 1)

            def slots_root():
                pool.wait_ge(sem("var"), 2 * VARIANCE["slots"] + 2)
                step(pool.tensor_scalar(sst[:, 11:12], sst[:, 9:10], float(D), None, ALU.mult))
                step(pool.tensor_tensor(sst[:, 10:11], sst[:, 11:12], const("mhalf", SLOTS)[:, 0:1], ALU.pow))
                pool.tensor_scalar(sst[:, 10:11], sst[:, 10:11], 1e5, None, ALU.min).then_inc(sem("rstd"), 2)

            def keys():
                for j in range(B // 2):
                    pool.wait_ge(sem("qk1"), 2 if j < B // 4 else 6)
                    if j >= 2:
                        pool.wait_ge(sem("s_mm"), j - 1)
                    for i in range(2):
                        b = 2 * j + i
                        for c in range(2):
                            ins = pool.tensor_tensor(kblk[:, j % 2, c, i, :].rearrange("p (x n) -> p x n", x=HH),
                                                     bcast(kT[:, c, S * b:S * b + S], 1, HH),
                                                     bcast(const("kmask", KH), 2, S), ALU.mult)
                    ins.then_inc(sem("kblk"), 1)

            plus = (1.0, LN_EPS, ALU.mult, ALU.add)
            pool.memset(xT[:], 0.0)
            pool.memset(b2pad[:], 0.0)
            pool.memset(fb1[:], 0.0)
            pool.memset(fb2[:], 0.0).then_inc(sem("pads_zero"), 1)
            pool.wait_ge(sem("ld_cst"), 16)
            twice = (1.0 + LN_EPS, LN_EPS * LN_EPS, ALU.mult, ALU.add)
            root(rs2, twice, "ln1")
            root(rs, plus, "in0")
            pool.wait_ge(sem("emb_cols"), 4)
            pool.memset(run[:, 0], 0.0)
            pool.memset(zeros, 0.0).then_inc(sem("zeros"), 1)
            pool.memset(xk[:], 1.0).then_inc(sem("xk_ones"), 1)
            pool.memset(ohT[:], 0.0)
            pool.memset(hT[:, :, NTOK:NPAD], 0.0).then_inc(sem("h_pads"), 1)
            slots_root()
            root(rs, plus, "ln2")
            for u in range(2):
                pool.wait_ge(sem(f"st_sorted_{u}"), 16)
            pool.wait_ge(sem("place"), 1)
            for tt in range(TT):
                n = TR if tt < TT - 1 else LAST
                pool.indirect_dma_start(xsorted, bass.IndirectOffsetOnAxis(ap=place[0:n, tt:tt + 1], axis=0),
                                        t[0:n, tt, :], None).then_inc(sem("scattered"), 16)
            for u in range(2):
                pool.wait_ge(sem(f"st_sorted_{u}"), 16 * (NRT // 2 + 1))
            for tt in range(TT):
                n = TR if tt < TT - 1 else LAST
                pool.indirect_dma_start(t[0:n, tt, :], None, ysorted,
                                        bass.IndirectOffsetOnAxis(ap=place[0:n, tt:tt + 1], axis=0))\
                    .then_inc(sem(f"moe_back{tt}"), 16)
            for name in ("ffn", "u", "ln3"):
                root(rs, plus, name)
            pool.memset(qT[:, :, NTOK:NPAD], 0.0).then_inc(sem("q_pads"), 1)
            pool.tensor_copy(vblk[:].rearrange("p u n (x c) -> p (u n) x c", x=IPT)[:, :, :, HD],
                             bcast(const("vmask", TR), 1, 16)).then_inc(sem("v_ones"), 1)
            keys()
            root(rs2, twice, "tok0")
            for half in HALVES:
                lo, hi = half[0], half[-1] + 1
                pool.wait_ge(sem("squares"), hi)
                pool.tensor_tensor(m6[:, 3, lo:hi], m6[:, 2, lo:hi], const("mhalf", TR)[:, lo:hi], ALU.pow)\
                    .then_inc(sem("rstd"), 1)
            pool.memset(hid[0:SLOTS, NTOK:NPAD], 0.0)
            pool.memset(cmT[:], 0.0)
            pool.memset(hidT[:], 0.0).then_inc(sem("soft_zero"), 1)
            pool.wait_ge(sem("comb"), 1)
            pool.wait_ge(sem("y_copied"), 6)
            with pool.Fori(0, NG // 2) as g2:
                for u in range(2):
                    g = g2 * 2 + u
                    pool.wait_ge(sem("fc1_used"), g2 * 2 + 1)
                    for c in range(3):
                        ins = pool.tensor_tensor(
                            yg[:, u, c].rearrange("p q (two b) -> p q two b", two=2),
                            bcast(ycmp[:, c, bass.ds(g * QP, QP), :], 2, 2),
                            bcast(bcast(const("pmask"), 1, QP), 3, B), ALU.mult)
                    ins.then_inc(sem("yg"), 1)
                    pool.wait_ge(sem("cm_tp"), g + 1)
                    for tt in range(TT):
                        ins = pool.tensor_tensor(xe[:, tt],
                                                 bcast(comb[:, tt, bass.ds(g * GS, GS)], 2, B),
                                                 bcast(const("bmask", TR)[:, B * tt:B * tt + B], 1, GS), ALU.mult)
                    ins.then_inc(sem("xe"), 1)


INPUTS = ["x", "L0_tok_W_proj", "L0_tok_b_proj", "L0_tok_cls_token", "L0_tok_pos_embedding", "L0_attn_ln1_g",
          "L0_attn_ln1_b", "L0_attn_Wq", "L0_attn_bq", "L0_attn_Wk", "L0_attn_bk", "L0_attn_Wv", "L0_attn_bv",
          "L0_attn_ln2_g", "L0_attn_ln2_b", "L0_attn_Wg", "L0_attn_bg", "L0_attn_W1", "L0_attn_b1", "L0_attn_W2",
          "L0_attn_b2", "L0_ffn_w1", "L0_ffn_b1", "L0_ffn_w2", "L0_ffn_b2", "L0_ffn_down_w", "L0_ffn_down_b",
          "L0_ffn_up_w", "L0_ffn_gamma", "L0_ffn_beta", "L1_attn_w_qkv", "L1_attn_w_proj", "L1_attn_b_proj",
          "L1_attn_temperature", "L1_ffn_slots", "L1_ffn_scale", "L1_ffn_fc1_weight", "L1_ffn_fc1_bias",
          "L1_ffn_fc2_weight", "L1_ffn_fc2_bias", "L1_ffn_norm_weight"]


def kernel(**inputs):
    import concourse.bacc as bacc
    from concourse.bass_utils import run_bass_kernel_spmd

    nc = bacc.Bacc("TRN2", target_bir_lowering=False, num_devices=1)
    arrays, w = {}, {}
    for name in INPUTS:
        v = np.ascontiguousarray(inputs[name])
        arrays[f"in_{name}"] = v
        w[name] = nc.dram_tensor(f"in_{name}", v.shape, mybir.dt.from_np(v.dtype), kind="ExternalInput").ap()
    table = constant_table()
    arrays["consts"] = table
    consts = nc.dram_tensor("consts", table.shape, F32, kind="ExternalInput").ap()
    out = nc.dram_tensor("out", (B, S, D), F32, kind="ExternalOutput").ap()
    vit_tower(nc, w, consts, out)
    r = run_bass_kernel_spmd(nc, [arrays], core_ids=[0])
    return r.results[0]["out"]
```
